# Optimizing a Trainium2 kernel written in Bass

```python
import numpy as np
import jax
import jax.numpy as jnp

def _softmax(x, axis=-1):
    return jax.nn.softmax(x, axis=axis)

def _gelu(x):
    return jax.nn.gelu(x, approximate=True)

def _silu(x):
    return jax.nn.silu(x)

def _sigmoid(x):
    return jax.nn.sigmoid(x)

def _layernorm(x, axis=-1, eps=1e-05):
    m = jnp.mean(x, axis=axis, keepdims=True)
    v = jnp.var(x, axis=axis, keepdims=True)
    return (x - m) / jnp.sqrt(v + eps)

def _scatter_add(tgt, idx, src, axis=0):
    return tgt.at[idx].add(src)

def _segment_sum(src, seg, n):
    return jax.ops.segment_sum(src, seg, n)
kernel_name = 'mk_perceiver_d1_seqx_r4_db39cf'

def setup_inputs(seed: int=0):
    np.random.seed(seed)
    _w = jnp.asarray

    def _rec_inputs():
        import jax
        import jax.numpy as jnp
        _rk = jax.random.key(seed)
        x = -0.0005207 + 1.001 * jax.random.normal(jax.random.fold_in(_rk, 1), (1, 256, 1024), jnp.float32)
        _lenS = 256 - jax.random.randint(jax.random.fold_in(_rk, 7), (1,), 0, max(1, 256 // 4) + 1, jnp.int32)
        _lenS2 = 4096 - jax.random.randint(jax.random.fold_in(_rk, 8), (1,), 0, max(1, 4096 // 4) + 1, jnp.int32)
        _ctx_4096P = jax.random.normal(jax.random.fold_in(_rk, 11), (1, 16, 1024), jnp.float32)
        _ctx_4096c = jax.random.dirichlet(jax.random.fold_in(_rk, 511), 0.3 * jnp.ones((16,), jnp.float32), (1, 4096))
        _ctx_4096t = jnp.einsum('bsk,bkd->bsd', _ctx_4096c, _ctx_4096P)
        _ctx_4096t = _ctx_4096t * jax.lax.rsqrt(jnp.mean(jnp.square(_ctx_4096t)) + 1e-12) * 0.953939
        ctx_4096 = -0.00010331 + 0.999899 * (_ctx_4096t + 0.3 * jax.random.normal(jax.random.fold_in(_rk, 611), (1, 4096, 1024), jnp.float32))
        return (x, ctx_4096)
    x, ctx_4096 = _rec_inputs()

    def _L0_xattn_setup():
        import jax, jax.numpy as jnp
        import numpy as np
        import math
        HIDDEN = 1024
        N_HEADS = 32
        HEAD_DIM = 128
        N_KV_HEADS = 4
        N_GROUPS = N_HEADS // N_KV_HEADS
        key = jax.random.key(seed)
        ks = jax.random.split(key, 6)
        B, NL, S = (8, 64, 1024)
        latents = jax.random.normal(ks[0], (B, NL, HIDDEN), dtype=jnp.float32)
        context = jax.random.normal(ks[1], (B, S, HIDDEN), dtype=jnp.float32)
        scale = 1.0 / math.sqrt(HIDDEN)
        Wq = jax.random.normal(ks[2], (HIDDEN, N_HEADS * HEAD_DIM), dtype=jnp.float32) * scale
        Wk = jax.random.normal(ks[3], (HIDDEN, N_KV_HEADS * HEAD_DIM), dtype=jnp.float32) * scale
        Wv = jax.random.normal(ks[4], (HIDDEN, N_KV_HEADS * HEAD_DIM), dtype=jnp.float32) * scale
        Wo = jax.random.normal(ks[5], (N_HEADS * HEAD_DIM, HIDDEN), dtype=jnp.float32) * scale
        return {'latents': latents, 'context': context, 'Wq': Wq, 'Wk': Wk, 'Wv': Wv, 'Wo': Wo}
    _L0_xattn_all = _L0_xattn_setup()
    _L0_xattn_in = {k: v for k, v in _L0_xattn_all.items() if k in ('Wq', 'Wk', 'Wv', 'Wo')}
    del _L0_xattn_all

    def _L0_attn_setup():
        import jax, jax.numpy as jnp
        import numpy as np
        BATCH, SEQ, HIDDEN = (2, 1024, 1024)
        HEADS, HEAD_DIM, BLOCK = (32, 128, 64)
        LAYER_IDX, N_LAYERS = (1, 32)
        EPS = 1e-05

        def _decays():
            base = 1.0 / 2.0 ** (8.0 / HEADS)
            exponent = jnp.arange(HEADS, dtype=jnp.float32) + 1.0
            factor = 1.0 - LAYER_IDX / (N_LAYERS - 1 + 1e-05) + 1e-05
            slope = (base ** exponent * factor)[:, None, None]
            r = jnp.arange(BLOCK, dtype=jnp.float32) + 1.0
            q_decay = jnp.exp(-slope * r[:, None])
            k_decay = jnp.exp(-slope * (BLOCK - r)[:, None])
            diff = r[:, None] - r[None, :]
            diag = slope[None] * diff[None, None]
            diag = jnp.where(diag >= 0, -diag, -jnp.inf)
            diag_decay = jnp.exp(diag)
            block_decay = jnp.exp(-slope * BLOCK)
            return (q_decay, k_decay, diag_decay, block_decay)
        key = jax.random.key(seed)
        ks = jax.random.split(key, 5)
        s = 0.02
        return {'hidden_states': jax.random.normal(ks[0], (BATCH, SEQ, HIDDEN), jnp.float32), 'qkv_w': jax.random.normal(ks[1], (3 * HEADS * HEAD_DIM, HIDDEN), jnp.float32) * s, 'out_w': jax.random.normal(ks[2], (HIDDEN, HEADS * HEAD_DIM), jnp.float32) * s, 'gate_w': jax.random.normal(ks[3], (HEADS * HEAD_DIM, HIDDEN), jnp.float32) * s, 'norm_w': jnp.ones((HEADS * HEAD_DIM,), jnp.float32)}
    _L0_attn_all = _L0_attn_setup()
    _L0_attn_in = {k: v for k, v in _L0_attn_all.items() if k in ('qkv_w', 'out_w', 'gate_w', 'norm_w')}
    del _L0_attn_all

    def _L0_ffn_setup():
        import jax, jax.numpy as jnp
        import numpy as np
        LORA_R = 16
        SCALE = 16.0 / np.sqrt(16.0)
        NUM_EXPERTS = 4
        TOP_K = 2
        IN_F = 1024
        OUT_F = 1024
        key = jax.random.key(seed)
        k_x, k_a, k_b, k_r = jax.random.split(key, 4)
        x = jax.random.normal(k_x, (2, 512, IN_F), dtype=jnp.float32)
        A = jax.random.normal(k_a, (NUM_EXPERTS, LORA_R, IN_F), dtype=jnp.float32) * (1.0 / np.sqrt(IN_F))
        B = jax.random.normal(k_b, (NUM_EXPERTS, OUT_F, LORA_R), dtype=jnp.float32) * 0.02
        Wr = jax.random.normal(k_r, (NUM_EXPERTS, IN_F), dtype=jnp.float32) * 0.02
        return {'x': x, 'A': A, 'B': B, 'Wr': Wr}
    _L0_ffn_all = _L0_ffn_setup()
    _L0_ffn_in = {k: v for k, v in _L0_ffn_all.items() if k in ('A', 'B', 'Wr')}
    del _L0_ffn_all
    return {'x': x, 'ctx_4096': ctx_4096, 'L0_xattn_Wq': _L0_xattn_in['Wq'], 'L0_xattn_Wk': _L0_xattn_in['Wk'], 'L0_xattn_Wv': _L0_xattn_in['Wv'], 'L0_xattn_Wo': _L0_xattn_in['Wo'], 'L0_attn_qkv_w': _L0_attn_in['qkv_w'], 'L0_attn_out_w': _L0_attn_in['out_w'], 'L0_attn_gate_w': _L0_attn_in['gate_w'], 'L0_attn_norm_w': _L0_attn_in['norm_w'], 'L0_ffn_A': _L0_ffn_in['A'], 'L0_ffn_B': _L0_ffn_in['B'], 'L0_ffn_Wr': _L0_ffn_in['Wr']}

def reference(x, ctx_4096, L0_xattn_Wq, L0_xattn_Wk, L0_xattn_Wv, L0_xattn_Wo, L0_attn_qkv_w, L0_attn_out_w, L0_attn_gate_w, L0_attn_norm_w, L0_ffn_A, L0_ffn_B, L0_ffn_Wr):
    import jax
    import jax.numpy as jnp

    def _L0_xattn_ref(latents, context, Wq, Wk, Wv, Wo):
        import jax, jax.numpy as jnp
        import numpy as np
        import math
        HIDDEN = 1024
        N_HEADS = 32
        HEAD_DIM = 128
        N_KV_HEADS = 4
        N_GROUPS = N_HEADS // N_KV_HEADS
        b, q_len, _ = latents.shape
        kv_len = q_len + context.shape[1]
        hidden_states = jnp.concatenate([context, latents], axis=1)
        q = (latents @ Wq).reshape(b, q_len, N_KV_HEADS, N_GROUPS, HEAD_DIM)
        k = (hidden_states @ Wk).reshape(b, kv_len, N_KV_HEADS, HEAD_DIM)
        v = (hidden_states @ Wv).reshape(b, kv_len, N_KV_HEADS, HEAD_DIM)
        scale = 1.0 / math.sqrt(HEAD_DIM)
        scores = jnp.einsum('bqhgd,bkhd->bhgqk', q, k) * scale
        attn = jax.nn.softmax(scores.astype(jnp.float32), axis=-1).astype(q.dtype)
        out = jnp.einsum('bhgqk,bkhd->bqhgd', attn, v)
        out = out.reshape(b, q_len, N_HEADS * HEAD_DIM)
        return out @ Wo

    def _L0_attn_ref(hidden_states, qkv_w, out_w, gate_w, norm_w):
        import jax, jax.numpy as jnp
        import numpy as np
        BATCH, SEQ, HIDDEN = (2, 1024, 1024)
        HEADS, HEAD_DIM, BLOCK = (32, 128, 64)
        LAYER_IDX, N_LAYERS = (1, 32)
        EPS = 1e-05

        def _decays():
            base = 1.0 / 2.0 ** (8.0 / HEADS)
            exponent = jnp.arange(HEADS, dtype=jnp.float32) + 1.0
            factor = 1.0 - LAYER_IDX / (N_LAYERS - 1 + 1e-05) + 1e-05
            slope = (base ** exponent * factor)[:, None, None]
            r = jnp.arange(BLOCK, dtype=jnp.float32) + 1.0
            q_decay = jnp.exp(-slope * r[:, None])
            k_decay = jnp.exp(-slope * (BLOCK - r)[:, None])
            diff = r[:, None] - r[None, :]
            diag = slope[None] * diff[None, None]
            diag = jnp.where(diag >= 0, -diag, -jnp.inf)
            diag_decay = jnp.exp(diag)
            block_decay = jnp.exp(-slope * BLOCK)
            return (q_decay, k_decay, diag_decay, block_decay)
        b, s, _ = hidden_states.shape
        h, d, bs = (HEADS, HEAD_DIM, BLOCK)
        nb = s // bs
        q_decay, k_decay, diag_decay, block_decay = _decays()
        qkv = jax.nn.silu(hidden_states @ qkv_w.T)
        qkv = qkv.reshape(b, s, h, 3, d)
        q = jnp.moveaxis(qkv[:, :, :, 0], 2, 1)
        k = jnp.moveaxis(qkv[:, :, :, 1], 2, 1)
        v = jnp.moveaxis(qkv[:, :, :, 2], 2, 1)

        def to_blocks(x):
            return jnp.moveaxis(x.reshape(b, h, nb, bs, d), 2, 0)
        qb, kb, vb = (to_blocks(q), to_blocks(k), to_blocks(v))

        def step(kv, blk):
            cq, ck, cv = blk
            scores = jnp.einsum('bhnd,bhmd->bhnm', cq, ck) * diag_decay
            intra = jnp.einsum('bhnm,bhmd->bhnd', scores, cv)
            inter = jnp.einsum('bhnd,bhde->bhne', cq * q_decay, kv)
            kv_next = kv * block_decay + jnp.einsum('bhnd,bhne->bhde', ck * k_decay, cv)
            return (kv_next, intra + inter)
        kv0 = jnp.zeros((b, h, d, d), hidden_states.dtype)
        _, out_blocks = jax.lax.scan(step, kv0, (qb, kb, vb))
        attn = jnp.moveaxis(out_blocks, 0, 2)
        attn = attn.reshape(b, h, s, d).transpose(0, 2, 1, 3).reshape(b, s, h * d)
        xf = attn.astype(jnp.float32)
        xf = xf * jax.lax.rsqrt(jnp.mean(xf * xf, axis=-1, keepdims=True) + EPS)
        normed = norm_w * xf.astype(attn.dtype)
        gate = jax.nn.sigmoid(hidden_states @ gate_w.T)
        return gate * normed @ out_w.T

    def _L0_ffn_ref(x, A, B, Wr):
        import jax, jax.numpy as jnp
        import numpy as np
        LORA_R = 16
        SCALE = 16.0 / np.sqrt(16.0)
        NUM_EXPERTS = 4
        TOP_K = 2
        IN_F = 1024
        OUT_F = 1024
        orig_shape = x.shape
        flat = x.reshape(-1, orig_shape[-1])
        logits = flat @ Wr.T
        topk_vals, topk_idx = jax.lax.top_k(logits, TOP_K)
        T = flat.shape[0]
        neg_inf = jnp.finfo(logits.dtype).min
        sparse = jnp.full_like(logits, neg_inf)
        rows = jnp.arange(T)[:, None]
        sparse = sparse.at[rows, topk_idx].set(topk_vals)
        gates = jax.nn.softmax(sparse, axis=-1)
        mid = jnp.einsum('tf,erf->ter', flat, A)
        all_deltas = jnp.einsum('ter,eor->teo', mid, B) * SCALE
        delta = jnp.sum(gates[:, :, None] * all_deltas, axis=1)
        return delta.reshape(*orig_shape[:-1], -1)
    x = x + _L0_xattn_ref(_layernorm(x, axis=-1), ctx_4096, L0_xattn_Wq, L0_xattn_Wk, L0_xattn_Wv, L0_xattn_Wo)
    x = x + _L0_attn_ref(_layernorm(x, axis=-1), L0_attn_qkv_w, L0_attn_out_w, L0_attn_gate_w, L0_attn_norm_w)
    x = x + _L0_ffn_ref(_layernorm(x, axis=-1), L0_ffn_A, L0_ffn_B, L0_ffn_Wr)
    return x

_drawn_inputs = setup_inputs


def setup_inputs(seed=0):
    import zlib

    import numpy as np

    out = dict(_drawn_inputs(seed))
    spreads = {'L0_attn_norm_w': (1.0, 0.2)}
    factors = {}
    for name, (base, spread) in spreads.items():
        noise = np.random.default_rng([zlib.crc32(name.encode()), seed]).standard_normal(out[name].shape)
        drawn = base * np.exp(spread * noise) if base else spread * noise
        out[name] = jnp.asarray(drawn.astype(out[name].dtype))
    for name, factor in factors.items():
        out[name] = (out[name] * factor).astype(out[name].dtype)
    return out
```

```python
from contextlib import ExitStack

import numpy as np

import concourse.bass as bass
from concourse import mybir

F32 = mybir.dt.float32
F32R = mybir.dt.float32r
ALU = mybir.AluOpType
ACT = mybir.ActivationFunctionType
AX = mybir.AxisListType

P = 128
HIDDEN = 1024
KT = HIDDEN // P
TOK = 256
QT = TOK // P
CTX = 4096
KV = CTX + TOK
KVT = KV // P
HEADS = 32
D = 128
KVH = 4
GROUP = HEADS // KVH
SCALE = 1.0 / float(np.sqrt(D))
EPS = 1e-5
BANK = 512
CCHUNK = 512
NCHUNK = CTX // CCHUNK
EXPERTS = 4
LORA = 16
ER = EXPERTS * LORA


class Alloc:

    def __init__(self, nc, ctx, prefix):
        self.nc, self.ctx, self.prefix = nc, ctx, prefix

    def sb(self, name, shape, dt=F32):
        return self.ctx.enter_context(self.nc.sbuf_tensor(self.prefix + name, shape, dt))

    def ps(self, name, shape, dt=F32):
        return self.ctx.enter_context(self.nc.psum_tensor(self.prefix + name, shape, dt))

    def sem(self, name):
        return self.ctx.enter_context(self.nc.semaphore(self.prefix + name))


def f32(ap):
    return ap.bitcast(F32)


def three_pass(pe, out, w_hi, w_lo, m_hi, m_lo, first, last):
    pe.matmul(out, w_hi, m_hi, start=first, stop=False)
    pe.matmul(out, w_hi, m_lo, start=False, stop=False)
    return pe.matmul(out, w_lo, m_hi, start=False, stop=last)


def layernorm_and_turn(nc, name, x_sb, hT_hi, hT_lo, ident, x_dram=None):
    with ExitStack() as ctx:
        a = Alloc(nc, ctx, name)
        stats = a.sb("stats", [P, QT, 2, 6])
        mv = a.sb("mv", [P, QT, 2])
        ve = a.sb("ve", [P, QT])
        root = a.sb("root", [P, QT])
        r0 = a.sb("r0", [P, QT])
        t0 = a.sb("t0", [P, QT])
        rstd = a.sb("rstd", [P, QT])
        h = a.sb("h", [P, QT, HIDDEN])
        turned = a.ps("turned", [P, KT, TOK])
        x_in = a.sem("x_in")
        small = a.sem("small")
        root_ready = a.sem("root_ready")
        h_ready = a.sem("h_ready")
        turned_ready = a.sem("turned_ready")
        hi_ready = a.sem("hi_ready")
        block = ctx.enter_context(nc.Block())

        @block.sync
        def _(sp):
            if x_dram is not None:
                sp.dma_start(x_sb[:, :, :], x_dram).then_inc(x_in, 16)

        @block.vector
        def _(dve):
            if x_dram is not None:
                dve.wait_ge(x_in, 16)
            for t in range(QT):
                for half in range(2):
                    dve.bn_stats(stats[:, t, half, :], x_sb[:, t, half * 512:(half + 1) * 512]).then_inc(small, 1)
            dve.wait_ge(small, 2 * QT)
            for t in range(QT):
                dve.bn_aggr(mv[:, t, :], stats[:, t, :, :].rearrange("p a b -> p (a b)")).then_inc(small, 1)
            dve.wait_ge(small, 3 * QT)
            dve.tensor_scalar(ve[:, :], mv[:, :, 1], EPS, None, ALU.add).then_inc(small, 1)
            dve.wait_ge(root_ready, 1)
            dve.reciprocal(r0[:, :], root[:, :]).then_inc(small, 1)
            dve.wait_ge(small, 3 * QT + 2)
            dve.tensor_tensor(t0[:, :], r0[:, :], r0[:, :], ALU.mult).then_inc(small, 1)
            dve.wait_ge(small, 3 * QT + 3)
            dve.tensor_tensor(t0[:, :], t0[:, :], ve[:, :], ALU.mult).then_inc(small, 1)
            dve.wait_ge(small, 3 * QT + 4)
            dve.tensor_scalar(t0[:, :], t0[:, :], -0.5, 1.5, ALU.mult, ALU.add).then_inc(small, 1)
            dve.wait_ge(small, 3 * QT + 5)
            dve.tensor_tensor(rstd[:, :], r0[:, :], t0[:, :], ALU.mult).then_inc(small, 1)
            dve.wait_ge(small, 3 * QT + 6)
            for t in range(QT):
                dve.tensor_scalar(h[:, t, :], x_sb[:, t, :], mv[:, t, 0:1], rstd[:, t:t + 1],
                                  ALU.subtract, ALU.mult).then_inc(h_ready, 1)
            if hT_lo is not None:
                for b in range(KT // 2):
                    dve.wait_ge(hi_ready, b + 1)
                    dve.tensor_tensor(hT_lo[:, 2 * b:2 * b + 2, :], turned[:, 2 * b:2 * b + 2, :],
                                      f32(hT_hi[:, 2 * b:2 * b + 2, :]), ALU.subtract)

        @block.scalar
        def _(act):
            act.wait_ge(small, 3 * QT + 1)
            act.activation(root[:, :], ve[:, :], ACT.Sqrt).then_inc(root_ready, 1)
            for b in range(KT // 2):
                act.wait_ge(turned_ready, b + 1)
                act.activation(hT_hi[:, 2 * b:2 * b + 2, :], turned[:, 2 * b:2 * b + 2, :],
                               ACT.Copy).then_inc(hi_ready, 1)

        @block.tensor
        def _(pe):
            pe.wait_ge(h_ready, QT)
            for b in range(KT // 2):
                for k in (2 * b, 2 * b + 1):
                    for t in range(QT):
                        last = pe.transpose(turned[:, k, t * P:(t + 1) * P], h[:, t, k * P:(k + 1) * P], ident[:, :])
                last.then_inc(turned_ready, 1)


def project_keys_values(nc, ctxT, wk, wv, hT_hi, hT_lo, kT_dram, v_dram):
    with ExitStack() as ctx:
        a = Alloc(nc, ctx, "kv_")
        w_raw = a.sb("w_raw", [P, KT, KVH * D])
        wk_hi = a.sb("wk_hi", [P, KT, KVH * D], F32R)
        wk_lo = a.sb("wk_lo", [P, KT, KVH * D], F32R)
        wv_hi = a.sb("wv_hi", [P, KT, KVH * D], F32R)
        wv_lo = a.sb("wv_lo", [P, KT, KVH * D], F32R)
        c_raw = a.sb("c_raw", [P, KT, CCHUNK])
        c_hi = [a.sb(f"c_hi{i}", [P, KT, CCHUNK], F32R) for i in range(2)]
        c_lo = [a.sb(f"c_lo{i}", [P, KT, CCHUNK], F32R) for i in range(2)]
        k_out = a.sb("k_out", [P, KVH, CCHUNK])
        v_out = a.sb("v_out", [P, KVH, CCHUNK // P, D])
        k_ps = a.ps("k_ps", [P, KVH, BANK])
        v_ps = a.ps("v_ps", [P, CCHUNK // P, BANK])
        w_in = a.sem("w_in")
        w_hi_ready = a.sem("w_hi_ready")
        w_lo_ready = a.sem("w_lo_ready")
        c_in = a.sem("c_in")
        c_hi_ready = a.sem("c_hi_ready")
        c_lo_ready = a.sem("c_lo_ready")
        k_ready = a.sem("k_ready")
        v_ready = a.sem("v_ready")
        k_copied = a.sem("k_copied")
        v_copied = a.sem("v_copied")
        k_stored = a.sem("k_stored")
        v_stored = a.sem("v_stored")
        VT = CCHUNK // P
        block = ctx.enter_context(nc.Block())

        def load(sp, c):
            sp.dma_start(c_raw[:, :, :], ctxT[bass.ds(c, 1)].rearrange("c p k n -> p (c k) n")).then_inc(c_in, 16)

        def store(sp, c, tiles):
            n = tiles * P
            sp.wait_ge(k_copied, KVH + KVH * (c + 1))
            sp.dma_start(kT_dram[:, :, bass.ds(c * CCHUNK, n)].rearrange("g p n -> p g n"),
                         k_out[:, :, 0:n]).then_inc(k_stored, 16)
            sp.wait_ge(v_copied, VT * (c + 1) + tiles)
            sp.dma_start(v_dram[:, :, bass.ds(c * VT, tiles), :].rearrange("g p t d -> p g t d"),
                         v_out[:, :, 0:tiles, :]).then_inc(v_stored, 16)

        @block.sync
        def _(sp):
            sp.sem_inc(k_stored, 16)
            sp.sem_inc(v_stored, 16)
            sp.dma_start(w_raw[:, :, :], wk).then_inc(w_in, 16)
            load(sp, 0)
            sp.wait_ge(w_lo_ready, 1)
            sp.dma_start(w_raw[:, :, :], wv).then_inc(w_in, 16)
            sp.wait_ge(c_lo_ready, 1)
            load(sp, 1)
            with sp.Fori(0, NCHUNK - 2) as c:
                sp.wait_ge(c_lo_ready, c + 2)
                load(sp, c + 2)
                store(sp, c, VT)
            store(sp, NCHUNK - 2, VT)
            store(sp, NCHUNK - 1, VT)
            store(sp, NCHUNK, QT)
            sp.wait_ge(k_stored, 16 * (NCHUNK + 2))
            sp.wait_ge(v_stored, 16 * (NCHUNK + 2))

        def copy_keys(act, c, n):
            act.wait_ge(k_stored, 16 * (c + 1))
            for g in range(KVH):
                act.wait_ge(k_ready, KVH * c + g + 1)
                act.activation(k_out[:, g, 0:n], k_ps[:, g, 0:n], ACT.Copy).then_inc(k_copied, 1)

        @block.scalar
        def _(act):
            act.sem_inc(k_copied, KVH)
            for i, w_hi in enumerate((wk_hi, wv_hi)):
                act.wait_ge(w_in, 16 * (i + 1))
                act.activation(w_hi[:, :, :], w_raw[:, :, :], ACT.Copy).then_inc(w_hi_ready, 1)
                if i == 0:
                    act.wait_ge(c_in, 16)
                    act.activation(c_hi[0][:, :, :], c_raw[:, :, :], ACT.Copy).then_inc(c_hi_ready, 1)
            act.wait_ge(c_in, 32)
            act.activation(c_hi[1][:, :, :], c_raw[:, :, :], ACT.Copy).then_inc(c_hi_ready, 1)
            with act.Fori(0, NCHUNK // 2 - 1) as i:
                for par in range(2):
                    c = 2 * i + par
                    copy_keys(act, c, CCHUNK)
                    act.wait_ge(c_in, 16 * (c + 3))
                    act.wait_ge(v_ready, VT * (c + 1))
                    act.activation(c_hi[par][:, :, :], c_raw[:, :, :], ACT.Copy).then_inc(c_hi_ready, 1)
            copy_keys(act, NCHUNK - 2, CCHUNK)
            copy_keys(act, NCHUNK - 1, CCHUNK)
            copy_keys(act, NCHUNK, TOK)

        def copy_values(dve, c, tiles):
            dve.wait_ge(v_stored, 16 * (c + 1))
            for t in range(tiles):
                dve.wait_ge(v_ready, VT * c + t + 1)
                dve.tensor_copy(v_out[:, :, t, :], v_ps[:, t, :].rearrange("p (g d) -> p g d", d=D)).then_inc(v_copied, 1)

        def split_low(dve, c, par):
            dve.wait_ge(c_hi_ready, c + 1)
            dve.tensor_tensor(c_lo[par][:, :, :], c_raw[:, :, :], f32(c_hi[par][:, :, :]),
                              ALU.subtract).then_inc(c_lo_ready, 1)

        @block.vector
        def _(dve):
            dve.sem_inc(v_copied, VT)
            for i, (w_hi, w_lo) in enumerate(((wk_hi, wk_lo), (wv_hi, wv_lo))):
                dve.wait_ge(w_hi_ready, i + 1)
                dve.tensor_tensor(w_lo[:, :, :], w_raw[:, :, :], f32(w_hi[:, :, :]), ALU.subtract).then_inc(w_lo_ready, 1)
                if i == 0:
                    split_low(dve, 0, 0)
            split_low(dve, 1, 1)
            with dve.Fori(0, NCHUNK // 2 - 1) as i:
                for par in range(2):
                    c = 2 * i + par
                    copy_values(dve, c, VT)
                    split_low(dve, c + 2, par)
            copy_values(dve, NCHUNK - 2, VT)
            copy_values(dve, NCHUNK - 1, VT)
            copy_values(dve, NCHUNK, QT)

        def chunk(pe, c, hi, lo, tiles):
            n = tiles * P
            for g in range(KVH):
                pe.wait_ge(k_copied, KVH * c + g + 1)
                for k in range(KT):
                    w = slice(g * D, (g + 1) * D)
                    last = three_pass(pe, k_ps[:, g, 0:n], wk_hi[:, k, w], wk_lo[:, k, w],
                                      hi[:, k, 0:n], lo[:, k, 0:n], k == 0, k == KT - 1)
                last.then_inc(k_ready, 1)
            for t in range(tiles):
                pe.wait_ge(v_copied, VT * c + t + 1)
                for k in range(KT):
                    s = slice(t * P, (t + 1) * P)
                    last = three_pass(pe, v_ps[:, t, :], hi[:, k, s], lo[:, k, s],
                                      wv_hi[:, k, :], wv_lo[:, k, :], k == 0, k == KT - 1)
                last.then_inc(v_ready, 1)

        @block.tensor
        def _(pe):
            pe.wait_ge(w_lo_ready, 2)
            with pe.Fori(0, NCHUNK // 2) as i:
                for par in range(2):
                    c = 2 * i + par
                    pe.wait_ge(c_lo_ready, c + 1)
                    chunk(pe, c, c_hi[par], c_lo[par], VT)
            chunk(pe, NCHUNK, hT_hi, hT_lo, QT)


PAIRS = KVT // 2
PIECES = 4
PIECE = KV // PIECES
UNITS = [(qt, c0, min(2 * BANK, KV - c0)) for qt in range(QT) for c0 in range(0, KV, 2 * BANK)]
NU = len(UNITS)
UPR = NU // QT
NPT = 3
LAG = 2
PV_PRIME = NPT


def cross_attention(nc, wq, kT_dram, v_dram, hT_hi, hT_lo, ident, ones, oT_dram):
    with ExitStack() as ctx:
        a = Alloc(nc, ctx, "xa_")
        kT_hi = a.sb("kT_hi", [P, KV], F32R)
        kT_lo = a.sb("kT_lo", [P, KV], F32R)
        v_hi = a.sb("v_hi", [P, KV], F32R)
        v_lo = a.sb("v_lo", [P, KV], F32R)
        rows = [[a.sb(f"rows{i}{t}", [P, KV]) for t in range(QT)] for i in range(2)]
        stage = [a.sb(f"stage{i}", [P, PIECE]) for i in range(2)]
        w_raw = a.sb("w_raw", [P, KT, D])
        w_hi = a.sb("w_hi", [P, KT, D], F32R)
        w_lo = a.sb("w_lo", [P, KT, D], F32R)
        qT_hi = a.sb("qT_hi", [P, TOK], F32R)
        qT_lo = a.sb("qT_lo", [P, TOK], F32R)
        pT_hi = [a.sb(f"pT_hi{i}", [P, 2, TOK], F32R) for i in range(NPT)]
        pT_lo = [a.sb(f"pT_lo{i}", [P, 2, TOK], F32R) for i in range(NPT)]
        maxima = a.sb("maxima", [P, 2, QT, UPR])
        neg_max = a.sb("neg_max", [P, 2, QT])
        sums = a.sb("sums", [P, 2, QT, PIECES])
        total = a.sb("total", [P, QT])
        inverse = a.sb("inverse", [P, QT])
        diag = a.sb("diag", [P, TOK])
        scale_rows = a.sb("scale_rows", [P, TOK])
        o_out = [a.sb(f"o_out{i}", [P, TOK]) for i in range(2)]
        s_ps = a.ps("s_ps", [P, 2, 2 * BANK])
        t_ps = a.ps("t_ps", [P, 2, 2, TOK])
        o_ps = a.ps("o_ps", [P, 2, TOK])
        m_ps = a.ps("m_ps", [P, 2, TOK])

        piece_asked = a.sem("piece_asked")
        piece_in = [a.sem(f"piece_in{i}") for i in range(2)]
        piece_hi = a.sem("piece_hi")
        piece_lo = a.sem("piece_lo")
        w_in = a.sem("w_in")
        w_hi_ready = a.sem("w_hi_ready")
        w_lo_ready = a.sem("w_lo_ready")
        q_ready = a.sem("q_ready")
        q_hi_ready = a.sem("q_hi_ready")
        q_lo_ready = a.sem("q_lo_ready")
        s_ready = a.sem("s_ready")
        s_drained = a.sem("s_drained")
        max_ready = a.sem("max_ready")
        exp_done = a.sem("exp_done")
        turned = a.sem("turned")
        pT_hi_ready = a.sem("pT_hi_ready")
        pT_lo_ready = a.sem("pT_lo_ready")
        pv_done = a.sem("pv_done")
        sum_ready = a.sem("sum_ready")
        diag_ready = a.sem("diag_ready")
        spread = a.sem("spread")
        spread_copied = a.sem("spread_copied")
        o_ready = a.sem("o_ready")
        o_stored = [a.sem(f"o_stored{i}") for i in range(2)]
        block = ctx.enter_context(nc.Block())

        def pt_free(n, j):
            last = j - NPT if j >= NPT else max(x for x in range(PAIRS) if x % NPT == j) - PAIRS
            return PV_PRIME + PAIRS * n + last + 1

        def load_weight(sp, n):
            sp.wait_ge(w_lo_ready, n + 1)
            sp.dma_start(w_raw[:, :, :], wq[bass.ds(n, 1)].rearrange("h p k d -> p (h k) d")).then_inc(w_in, 16)

        def load_piece(sp, g, i):
            sp.wait_ge(piece_lo, 2 * PIECES * g + i + 1)
            sp.sem_inc(piece_asked, 1)
            source = (kT_dram[bass.ds(g, 1)].rearrange("g p n -> (g p) n") if i < PIECES else
                      v_dram[bass.ds(g, 1)].rearrange("g p t d -> (g p) (t d)"))
            c0 = i % PIECES * PIECE
            sp.dma_start(stage[i % 2][:, :], source[:, c0:c0 + PIECE]).then_inc(piece_in[i % 2], 16)

        def store_o(sp, n, par):
            sp.wait_ge(o_ready, n + 1)
            sp.dma_start(oT_dram[bass.ds(n, 1)].rearrange("h p n -> (h p) n"), o_out[par][:, :]).then_inc(o_stored[par], 16)

        def sync_kv_head(sp, g, prefetch):
            first = GROUP * g
            for i in range(2, 2 * PIECES):
                if i == PIECES:
                    load_weight(sp, first + 1)
                load_piece(sp, g, i)
            for u in range(GROUP - 2):
                load_weight(sp, first + u + 2)
                store_o(sp, first + u, u % 2)
            store_o(sp, first + GROUP - 2, 0)
            if prefetch:
                load_weight(sp, first + GROUP)
                load_piece(sp, g + 1, 0)
                load_piece(sp, g + 1, 1)
            store_o(sp, first + GROUP - 1, 1)

        @block.sync
        def _(sp):
            sp.sem_inc(o_stored[0], 16)
            sp.sem_inc(o_stored[1], 16)
            load_weight(sp, 0)
            load_piece(sp, 0, 0)
            load_piece(sp, 0, 1)
            with sp.Fori(0, KVH - 1) as g:
                sync_kv_head(sp, g, True)
            sync_kv_head(sp, KVH - 1, False)
            for par in range(2):
                sp.wait_ge(o_stored[par], 16 * (HEADS // 2 + 1))

        def act_piece(act, g, i):
            act.wait_ge(piece_in[i % 2], 16 * (PIECES * g + i // 2 + 1))
            if i < PIECES:
                act.wait_ge(s_ready, NU * GROUP * g + 1)
            else:
                act.wait_ge(pv_done, PV_PRIME + PAIRS * GROUP * g)
            to = (kT_hi if i < PIECES else v_hi)[:, i % PIECES * PIECE:(i % PIECES + 1) * PIECE]
            act.activation(to, stage[i % 2][:, :], ACT.Copy).then_inc(piece_hi, 1)

        def act_weight(act, n):
            act.wait_ge(w_in, 16 * (n + 1))
            act.wait_ge(q_ready, n + 1)
            act.activation(w_hi[:, :, :], w_raw[:, :, :], ACT.Copy).then_inc(w_hi_ready, 1)

        def act_query(act, n):
            act.wait_ge(q_ready, n + 2)
            act.activation(qT_hi[:, :], m_ps[:, 0, :], ACT.Copy).then_inc(q_hi_ready, 1)

        def act_exp(act, n, par, qt, e):
            row = rows[par][qt][:, e * PIECE:(e + 1) * PIECE]
            act.wait_ge(max_ready, QT * n + qt + 1)
            act.activation(row, row, ACT.Exp, bias=neg_max[:, par, qt:qt + 1],
                           accum_out=sums[:, par, qt, e:e + 1]).then_inc(exp_done, 1)

        def act_slot(act, n, par, has_next, has_weight):
            for j in range(PAIRS):
                act.wait_ge(turned, PAIRS * n + j + 1)
                act.wait_ge(pv_done, pt_free(n, j))
                act.activation(pT_hi[j % NPT][:, :, :], t_ps[:, (par * PAIRS + j) % 2, :, :],
                               ACT.Copy).then_inc(pT_hi_ready, 1)
                if has_next and j == 0:
                    act_query(act, n + 1)
                if j == 5:
                    act.wait_ge(spread, n + 1)
                    act.activation(scale_rows[:, :], m_ps[:, 1, :], ACT.Copy).then_inc(spread_copied, 1)
                if has_next and 7 <= j <= 10:
                    act_exp(act, n + 1, 1 - par, 0, j - 7)
                if has_weight and j == 11:
                    act_weight(act, n + 2)
                if has_next and 12 <= j <= 15:
                    act_exp(act, n + 1, 1 - par, 1, j - 12)

        @block.scalar
        def _(act):
            act.sem_inc(spread_copied, 1)
            with act.Fori(0, KVH) as g:
                first = GROUP * g
                act_weight(act, first)
                for i in range(PIECES):
                    act_piece(act, g, i)
                act_query(act, first)
                act_weight(act, first + 1)
                for i in range(PIECES, 2 * PIECES):
                    act_piece(act, g, i)
                for qt in range(QT):
                    for e in range(PIECES):
                        act_exp(act, first, 0, qt, e)
                with act.Fori(0, GROUP // 2 - 1) as i:
                    act_slot(act, first + 2 * i, 0, True, True)
                    act_slot(act, first + 2 * i + 1, 1, True, True)
                act_slot(act, first + GROUP - 2, 0, True, False)
                act_slot(act, first + GROUP - 1, 1, False, False)

        def dve_piece(dve, g, i):
            n = 2 * PIECES * g + i
            dve.wait_ge(piece_hi, n + 1)
            at = slice(i % PIECES * PIECE, (i % PIECES + 1) * PIECE)
            hi, lo = (kT_hi, kT_lo) if i < PIECES else (v_hi, v_lo)
            dve.tensor_tensor(lo[:, at], stage[i % 2][:, :], f32(hi[:, at]), ALU.subtract).then_inc(piece_lo, 1)

        def dve_weight(dve, n):
            dve.wait_ge(w_hi_ready, n + 1)
            dve.tensor_tensor(w_lo[:, :, :], w_raw[:, :, :], f32(w_hi[:, :, :]), ALU.subtract).then_inc(w_lo_ready, 1)

        def dve_query(dve, n):
            dve.wait_ge(q_hi_ready, n + 1)
            dve.tensor_tensor(qT_lo[:, :], m_ps[:, 0, :], f32(qT_hi[:, :]), ALU.subtract).then_inc(q_lo_ready, 1)

        def dve_scores(dve, n, par, k):
            qt, c0, width = UNITS[k]
            dve.wait_ge(s_ready, NU * n + k + 2)
            dve.tensor_scalar(rows[par][qt][:, c0:c0 + width], s_ps[:, k % 2, 0:width], SCALE, None,
                              ALU.mult, ALU.max, accum_out=maxima[:, par, qt, k % UPR:k % UPR + 1]).then_inc(s_drained, 1)
            if k % UPR == UPR - 1:
                dve.wait_ge(s_drained, 2 + NU * n + k + 1)
                dve.tensor_reduce(neg_max[:, par, qt:qt + 1], maxima[:, par, qt, :], AX.X, ALU.max,
                                  negate=True).then_inc(max_ready, 1)

        def dve_inverse(dve, n, par):
            dve.wait_ge(exp_done, QT * PIECES * (n + 1))
            dve.tensor_reduce(total[:, :], sums[:, par, :, :], AX.X, ALU.add).then_inc(sum_ready, 1)
            dve.wait_ge(sum_ready, 2 * n + 1)
            dve.reciprocal(inverse[:, :], total[:, :]).then_inc(sum_ready, 1)
            dve.wait_ge(sum_ready, 2 * n + 2)
            for qt in range(QT):
                dve.tensor_scalar(diag[:, qt * P:(qt + 1) * P], ident[:, :], inverse[:, qt:qt + 1], None,
                                  ALU.mult).then_inc(diag_ready, 1)

        def dve_slot(dve, n, half, par, has_next, has_weight):
            for j in range(PAIRS):
                dve.wait_ge(pT_hi_ready, PAIRS * n + j + 1)
                dve.tensor_tensor(pT_lo[j % NPT][:, :, :], t_ps[:, (par * PAIRS + j) % 2, :, :],
                                  f32(pT_hi[j % NPT][:, :, :]), ALU.subtract).then_inc(pT_lo_ready, 1)
                if has_next and j == 0:
                    dve_query(dve, n + 1)
                if has_next and 1 <= j <= NU:
                    dve_scores(dve, n + 1, 1 - par, j - 1)
                if j == 2:
                    dve_inverse(dve, n, par)
                if has_weight and j == 12:
                    dve_weight(dve, n + 2)
            dve.wait_ge(spread_copied, n + 2)
            dve.wait_ge(o_stored[par], 16 * (half + 1))
            dve.wait_ge(pv_done, PV_PRIME + PAIRS * (n + 1))
            dve.tensor_tensor(o_out[par][:, :], o_ps[:, par, :], scale_rows[:, :], ALU.mult).then_inc(o_ready, 1)

        @block.vector
        def _(dve):
            dve.sem_inc(w_lo_ready, 1)
            dve.sem_inc(piece_lo, 2)
            dve.sem_inc(s_drained, 2)
            dve.sem_inc(pT_lo_ready, 2)
            with dve.Fori(0, KVH) as g:
                first = GROUP * g
                dve_weight(dve, first)
                for i in range(PIECES):
                    dve_piece(dve, g, i)
                dve_query(dve, first)
                dve_scores(dve, first, 0, 0)
                dve_scores(dve, first, 0, 1)
                dve_weight(dve, first + 1)
                for i in range(PIECES, 2 * PIECES):
                    dve_piece(dve, g, i)
                    dve_scores(dve, first, 0, 2 + i - PIECES)
                for k in range(2 + PIECES, NU):
                    dve_scores(dve, first, 0, k)
                with dve.Fori(0, GROUP // 2 - 1) as i:
                    dve_slot(dve, first + 2 * i, GROUP // 2 * g + i, 0, True, True)
                    dve_slot(dve, first + 2 * i + 1, GROUP // 2 * g + i, 1, True, True)
                dve_slot(dve, first + GROUP - 2, GROUP // 2 * (g + 1) - 1, 0, True, False)
                dve_slot(dve, first + GROUP - 1, GROUP // 2 * (g + 1) - 1, 1, False, False)

        def pe_query(pe, n):
            pe.wait_ge(w_lo_ready, n + 2)
            for k in range(KT):
                last = three_pass(pe, m_ps[:, 0, :], w_hi[:, k, :], w_lo[:, k, :], hT_hi[:, k, :], hT_lo[:, k, :],
                                  k == 0, k == KT - 1)
            last.then_inc(q_ready, 1)

        def pe_scores(pe, n, k):
            qt, c0, width = UNITS[k]
            if k == 0:
                pe.wait_ge(q_lo_ready, n + 1)
            pe.wait_ge(s_drained, NU * n + k + 1)
            q = slice(qt * P, (qt + 1) * P)
            for b in range(0, width, BANK):
                w = min(BANK, width - b)
                key = slice(c0 + b, c0 + b + w)
                last = three_pass(pe, s_ps[:, k % 2, b:b + w], qT_hi[:, q], qT_lo[:, q], kT_hi[:, key], kT_lo[:, key],
                                  True, True)
            last.then_inc(s_ready, 1)

        def pe_turn(pe, n, par, j):
            need = (2 * P * (j + 1) - 1) // PIECE + 1
            pe.wait_ge(exp_done, QT * PIECES * n + PIECES * (QT - 1) + need)
            pe.wait_ge(pT_lo_ready, PAIRS * n + j + 1)
            for t in range(2):
                at = slice((2 * j + t) * P, (2 * j + t + 1) * P)
                for qt in range(QT):
                    last = pe.transpose(t_ps[:, (par * PAIRS + j) % 2, t, qt * P:(qt + 1) * P],
                                        rows[par][qt][:, at], ident[:, :])
            last.then_inc(turned, 1)

        def pe_values(pe, g, n, par, j):
            if g is not None and j == 0:
                pe.wait_ge(piece_lo, 2 + 2 * PIECES * (g + 1))
            pe.wait_ge(pT_lo_ready, 2 + PAIRS * n + j + 1)
            for t in range(2):
                at = slice((2 * j + t) * P, (2 * j + t + 1) * P)
                last = three_pass(pe, o_ps[:, par, :], v_hi[:, at], v_lo[:, at], pT_hi[j % NPT][:, t, :],
                                  pT_lo[j % NPT][:, t, :], j == 0 and t == 0, j == PAIRS - 1 and t == 1)
            last.then_inc(pv_done, 1)

        def pe_slot(pe, g, n, par, has_next):
            for j in range(PAIRS):
                pe_turn(pe, n, par, j)
                if has_next and j == 0:
                    pe_query(pe, n + 1)
                if has_next and 1 <= j <= NU:
                    pe_scores(pe, n + 1, j - 1)
                if j == 4:
                    pe.wait_ge(diag_ready, QT * (n + 1))
                    pe.wait_ge(spread_copied, n + 1)
                    pe.matmul(m_ps[:, 1, :], ones[:, :], diag[:, :], start=True, stop=True).then_inc(spread, 1)
                if j >= LAG:
                    pe_values(pe, g, n, par, j - LAG)
            for j in range(PAIRS - LAG, PAIRS):
                pe_values(pe, g, n, par, j)

        @block.tensor
        def _(pe):
            pe.sem_inc(s_ready, 1)
            pe.sem_inc(q_ready, 1)
            pe.sem_inc(pv_done, PV_PRIME)
            with pe.Fori(0, KVH) as g:
                first = GROUP * g
                pe_query(pe, first)
                pe.wait_ge(piece_lo, 2 + 2 * PIECES * g + PIECES)
                for k in range(NU):
                    pe_scores(pe, first, k)
                with pe.Fori(0, GROUP // 2 - 1) as i:
                    pe_slot(pe, g, first + 2 * i, 0, True)
                    pe_slot(pe, g, first + 2 * i + 1, 1, True)
                pe_slot(pe, g, first + GROUP - 2, 0, True)
                pe_slot(pe, g, first + GROUP - 1, 1, False)


def project_out(nc, name, srcT_dram, w, x_in_sb, x_out_sb, row_scale):
    HP = 2
    STEPS = HEADS // HP
    with ExitStack() as ctx:
        a = Alloc(nc, ctx, name)
        w_raw = [a.sb(f"w_raw{i}", [P, HP, HIDDEN]) for i in range(2)]
        w_hi = [a.sb(f"w_hi{i}", [P, HP, HIDDEN], F32R) for i in range(2)]
        w_lo = [a.sb(f"w_lo{i}", [P, HP, HIDDEN], F32R) for i in range(2)]
        s_raw = [a.sb(f"s_raw{i}", [P, HP, TOK]) for i in range(2)]
        s_hi = [a.sb(f"s_hi{i}", [P, HP, TOK], F32R) for i in range(2)]
        s_lo = [a.sb(f"s_lo{i}", [P, HP, TOK], F32R) for i in range(2)]
        y_ps = a.ps("y_ps", [P, QT, 2, BANK])
        step_in = [a.sem(f"step_in{i}") for i in range(2)]
        hi_ready = a.sem("hi_ready")
        lo_ready = a.sem("lo_ready")
        mm_done = a.sem("mm_done")
        block = ctx.enter_context(nc.Block())

        @block.sync
        def _(sp):
            with sp.Fori(0, STEPS // 2) as i:
                for par in range(2):
                    s = 2 * i + par
                    sp.wait_ge(lo_ready, 2 * s + 2)
                    sp.dma_start(w_raw[par][:, :, :], w[bass.ds(HP * s, HP)].rearrange("h p n -> p h n")).then_inc(step_in[par], 16)
                    sp.dma_start(s_raw[par][:, :, :], srcT_dram[bass.ds(HP * s, HP)].rearrange("h p n -> p h n")).then_inc(step_in[par], 16)

        @block.scalar
        def _(act):
            with act.Fori(0, STEPS // 2) as i:
                for par in range(2):
                    s = 2 * i + par
                    act.wait_ge(step_in[par], 32 * (i + 1))
                    act.wait_ge(mm_done, s + 1)
                    act.activation(w_hi[par][:, :, :], w_raw[par][:, :, :], ACT.Copy).then_inc(hi_ready, 1)
                    act.activation(s_hi[par][:, :, :], s_raw[par][:, :, :], ACT.Copy).then_inc(hi_ready, 1)

        @block.vector
        def _(dve):
            dve.sem_inc(lo_ready, 4)
            with dve.Fori(0, STEPS // 2) as i:
                for par in range(2):
                    s = 2 * i + par
                    dve.wait_ge(hi_ready, 2 * s + 2)
                    dve.tensor_tensor(w_lo[par][:, :, :], w_raw[par][:, :, :], f32(w_hi[par][:, :, :]), ALU.subtract).then_inc(lo_ready, 1)
                    dve.tensor_tensor(s_lo[par][:, :, :], s_raw[par][:, :, :], f32(s_hi[par][:, :, :]), ALU.subtract).then_inc(lo_ready, 1)
            dve.wait_ge(mm_done, 2 + STEPS)
            for t in range(QT):
                y = y_ps[:, t, :, :].rearrange("p a b -> p (a b)")
                if row_scale is None:
                    dve.tensor_tensor(x_out_sb[:, t, :], y, x_in_sb[:, t, :], ALU.add)
                else:
                    dve.scalar_tensor_tensor(out=x_out_sb[:, t, :], in0=y, scalar=row_scale[:, t:t + 1],
                                             in1=x_in_sb[:, t, :], op0=ALU.mult, op1=ALU.add)

        def step(pe, s, par, first, last_step):
            pe.wait_ge(lo_ready, 4 + 2 * s + 2)
            for h in range(HP):
                for t in range(QT):
                    tok = slice(t * P, (t + 1) * P)
                    for b in range(2):
                        col = slice(b * BANK, (b + 1) * BANK)
                        last = three_pass(pe, y_ps[:, t, b, :], s_hi[par][:, h, tok], s_lo[par][:, h, tok],
                                          w_hi[par][:, h, col], w_lo[par][:, h, col],
                                          first and h == 0, last_step and h == HP - 1)
            last.then_inc(mm_done, 1)

        @block.tensor
        def _(pe):
            pe.sem_inc(mm_done, 2)
            step(pe, 0, 0, True, False)
            step(pe, 1, 1, False, False)
            with pe.Fori(1, STEPS // 2 - 1) as i:
                step(pe, 2 * i, 0, False, False)
                step(pe, 2 * i + 1, 1, False, False)
            step(pe, STEPS - 2, 0, False, False)
            step(pe, STEPS - 1, 1, False, True)


HPAIRS = HEADS // 2


def linear_attention(nc, w_qk, w_gv, decay, norm_w, hT_hi, hT_lo, zT_dram, square_sum):
    with ExitStack() as ctx:
        a = Alloc(nc, ctx, "la_")
        raw = [a.sb(f"raw{i}", [P, KT, 4 * D]) for i in range(2)]
        w_hi = [a.sb(f"w_hi{i}", [P, KT, 4 * D], F32R) for i in range(2)]
        w_lo = [a.sb(f"w_lo{i}", [P, KT, 4 * D], F32R) for i in range(2)]
        norm = a.sb("norm", [P, HEADS])
        dec = a.sb("dec", [P, 2, TOK])
        sig_qk = a.sb("sig_qk", [P, 2, 2, TOK])
        qk = a.sb("qk", [P, 2, 2, TOK])
        qk_hi = a.sb("qk_hi", [P, 2, 2, TOK], F32R)
        qk_lo = a.sb("qk_lo", [P, 2, 2, TOK], F32R)
        sig_v = a.sb("sig_v", [P, QT, 2 * D])
        v = a.sb("v", [P, QT, 2 * D])
        v_hi = a.sb("v_hi", [P, QT, 2 * D], F32R)
        v_lo = a.sb("v_lo", [P, QT, 2 * D], F32R)
        gate = a.sb("gate", [P, 2, TOK])
        m = a.sb("m", [P, 2, QT, TOK])
        m_hi = a.sb("m_hi", [P, 2, QT, TOK], F32R)
        m_lo = a.sb("m_lo", [P, 2, QT, TOK], F32R)
        squares = a.sb("squares", [P, 2, TOK])
        z = a.sb("z", [P, 2, TOK])
        qk_ps = a.ps("qk_ps", [P, 2, 2, TOK])
        g_ps = a.ps("g_ps", [P, 2, TOK])
        v_ps = a.ps("v_ps", [P, QT, 2 * D])
        a_ps = a.ps("a_ps", [P, 2, QT, TOK])
        o_ps = a.ps("o_ps", [P, 2, TOK])

        norm_in = a.sem("norm_in")
        w_in = [a.sem(f"w_in{i}") for i in range(2)]
        w_hi_ready = [a.sem(f"w_hi_ready{i}") for i in range(2)]
        w_lo_ready = [a.sem(f"w_lo_ready{i}") for i in range(2)]
        dec_in = a.sem("dec_in")
        qk_ready = a.sem("qk_ready")
        qk_sig = a.sem("qk_sig")
        qk_done = a.sem("qk_done")
        qk_hi_ready = a.sem("qk_hi_ready")
        qk_lo_ready = a.sem("qk_lo_ready")
        g_ready = a.sem("g_ready")
        gate_ready = a.sem("gate_ready")
        v_ready = a.sem("v_ready")
        v_sig = a.sem("v_sig")
        v_done = a.sem("v_done")
        v_hi_ready = a.sem("v_hi_ready")
        v_lo_ready = a.sem("v_lo_ready")
        a_ready = a.sem("a_ready")
        m_ready = a.sem("m_ready")
        m_hi_ready = a.sem("m_hi_ready")
        m_lo_ready = a.sem("m_lo_ready")
        o_ready = a.sem("o_ready")
        sq_ready = a.sem("sq_ready")
        sq_added = a.sem("sq_added")
        z_ready = a.sem("z_ready")
        z_stored = a.sem("z_stored")
        zeroed = a.sem("zeroed")
        block = ctx.enter_context(nc.Block())
        parts = ((0, slice(0, TOK)), (1, slice(P, TOK)))

        def load_weight(sp, part, p):
            w = (w_qk, w_gv)[part]
            sp.dma_start(raw[part][:, :, :], w[bass.ds(p, 1)].rearrange("h p k n -> p (h k) n")).then_inc(w_in[part], 16)

        def load_decay(sp, p):
            sp.dma_start(dec[:, :, :], decay[bass.ds(p, 1)].rearrange("g p h n -> p (g h) n")).then_inc(dec_in, 16)

        def store_z(sp, p):
            sp.wait_ge(z_ready, 2 * p + 4)
            sp.dma_start(zT_dram[bass.ds(2 * p, 2)].rearrange("h p n -> p h n"), z[:, :, :]).then_inc(z_stored, 16)

        @block.sync
        def _(sp):
            sp.sem_inc(z_stored, 16)
            load_weight(sp, 0, 0)
            load_weight(sp, 1, 0)
            sp.dma_start(norm[:, :], norm_w).then_inc(norm_in, 16)
            load_decay(sp, 0)
            for part in range(2):
                sp.wait_ge(w_lo_ready[part], 1)
                load_weight(sp, part, 1)
            with sp.Fori(1, HPAIRS - 1) as p:
                sp.wait_ge(w_lo_ready[0], p + 1)
                load_weight(sp, 0, p + 1)
                sp.wait_ge(m_ready, 4 * p)
                load_decay(sp, p)
                sp.wait_ge(w_lo_ready[1], p + 1)
                load_weight(sp, 1, p + 1)
                store_z(sp, p - 1)
            sp.wait_ge(m_ready, 4 * (HPAIRS - 1))
            load_decay(sp, HPAIRS - 1)
            store_z(sp, HPAIRS - 2)
            store_z(sp, HPAIRS - 1)
            sp.wait_ge(z_stored, 16 * (HPAIRS + 1))

        @block.gpsimd
        def _(pool):
            pool.memset(square_sum[:, :, :], 0.0).then_inc(sq_added, 1)
            for h in range(2):
                pool.memset(f32(m_hi[:, h, 1, 0:P]), 0.0).then_inc(zeroed, 1)
                pool.memset(f32(m_lo[:, h, 1, 0:P]), 0.0).then_inc(zeroed, 1)
            with pool.Fori(0, HPAIRS) as p:
                pool.wait_ge(sq_ready, p + 2)
                pool.wait_ge(sq_added, p + 1)
                pool.tensor_tensor(square_sum[:, :, :], square_sum[:, :, :], squares[:, :, :], ALU.add).then_inc(sq_added, 1)

        def act_split(act, part, p):
            act.wait_ge(w_in[part], 16 * (p + 1))
            act.activation(w_hi[part][:, :, :], raw[part][:, :, :], ACT.Copy).then_inc(w_hi_ready[part], 1)

        def act_qk(act, p):
            for h in range(2):
                act.wait_ge(qk_ready, 2 * p + h + 1)
                act.activation(sig_qk[:, h, :, :], qk_ps[:, h, :, :], ACT.Sigmoid).then_inc(qk_sig, 1)
            for h in range(2):
                act.wait_ge(qk_done, 2 * p + h + 1)
                act.activation(qk_hi[:, h, :, :], qk[:, h, :, :], ACT.Copy).then_inc(qk_hi_ready, 1)

        def act_gate_v(act, p):
            act.wait_ge(z_ready, 2 * p + 2)
            act.wait_ge(g_ready, p + 1)
            act.activation(gate[:, :, :], g_ps[:, :, :], ACT.Sigmoid).then_inc(gate_ready, 1)
            act.wait_ge(v_ready, p + 1)
            act.activation(sig_v[:, :, :], v_ps[:, :, :], ACT.Sigmoid).then_inc(v_sig, 1)
            act.wait_ge(v_done, p + 1)
            act.activation(v_hi[:, :, :], v[:, :, :], ACT.Copy).then_inc(v_hi_ready, 1)

        def act_decayed(act, p):
            for h in range(2):
                act.wait_ge(m_ready, 4 * p + 2 * h + 2)
                for jt, at in parts:
                    act.activation(m_hi[:, h, jt, at], m[:, h, jt, at], ACT.Copy).then_inc(m_hi_ready, 1)

        def act_squares(act, p):
            act.wait_ge(o_ready, p + 1)
            act.wait_ge(sq_added, p + 1)
            act.activation(squares[:, :, :], o_ps[:, :, :], ACT.Square).then_inc(sq_ready, 1)

        def act_pair(act, p, prefetch):
            act_decayed(act, p - 1)
            act.wait_ge(v_ready, p)
            act_split(act, 1, p)
            act_qk(act, p)
            act_squares(act, p - 1)
            if prefetch:
                act.wait_ge(qk_ready, 2 * p + 2)
                act_split(act, 0, p + 1)
            act_gate_v(act, p)

        @block.scalar
        def _(act):
            act_split(act, 0, 0)
            act_split(act, 1, 0)
            act_qk(act, 0)
            act.wait_ge(qk_ready, 2)
            act_split(act, 0, 1)
            act_gate_v(act, 0)
            with act.Fori(1, HPAIRS - 1) as p:
                act_pair(act, p, True)
            act_pair(act, HPAIRS - 1, False)
            act_decayed(act, HPAIRS - 1)
            act_squares(act, HPAIRS - 1)

        def dve_split(dve, part, p):
            dve.wait_ge(w_hi_ready[part], p + 1)
            dve.tensor_tensor(w_lo[part][:, :, :], raw[part][:, :, :], f32(w_hi[part][:, :, :]),
                              ALU.subtract).then_inc(w_lo_ready[part], 1)

        def dve_qk(dve, p):
            for h in range(2):
                dve.wait_ge(qk_sig, 2 * p + h + 1)
                dve.tensor_tensor(qk[:, h, :, :], qk_ps[:, h, :, :], sig_qk[:, h, :, :], ALU.mult).then_inc(qk_done, 1)
            for h in range(2):
                dve.wait_ge(qk_hi_ready, 2 * p + h + 1)
                dve.tensor_tensor(qk_lo[:, h, :, :], qk[:, h, :, :], f32(qk_hi[:, h, :, :]), ALU.subtract).then_inc(qk_lo_ready, 1)

        def dve_v(dve, p):
            dve.wait_ge(v_sig, p + 1)
            dve.tensor_tensor(v[:, :, :], v_ps[:, :, :], sig_v[:, :, :], ALU.mult).then_inc(v_done, 1)
            dve.wait_ge(v_hi_ready, p + 1)
            dve.tensor_tensor(v_lo[:, :, :], v[:, :, :], f32(v_hi[:, :, :]), ALU.subtract).then_inc(v_lo_ready, 1)

        def dve_decayed(dve, p):
            dve.wait_ge(dec_in, 16 * (p + 1))
            for h in range(2):
                dve.wait_ge(a_ready, 2 * p + h + 1)
                for jt, at in parts:
                    dve.tensor_tensor(m[:, h, jt, at], a_ps[:, h, jt, at], dec[:, h, 0:TOK - jt * P], ALU.mult).then_inc(m_ready, 1)
            for h in range(2):
                dve.wait_ge(m_hi_ready, 4 * p + 2 * h + 2)
                for jt, at in parts:
                    dve.tensor_tensor(m_lo[:, h, jt, at], m[:, h, jt, at], f32(m_hi[:, h, jt, at]), ALU.subtract).then_inc(m_lo_ready, 1)

        def dve_z(dve, p):
            dve.wait_ge(sq_ready, p + 2)
            dve.wait_ge(gate_ready, p + 1)
            dve.wait_ge(z_stored, 16 * (p + 1))
            for h in range(2):
                dve.scalar_tensor_tensor(out=z[:, h, :], in0=gate[:, h, :], scalar=norm[:, bass.ds(2 * p + h, 1)],
                                         in1=o_ps[:, h, :], op0=ALU.mult, op1=ALU.mult).then_inc(z_ready, 1)

        def dve_pair(dve, p, prefetch):
            dve_decayed(dve, p - 1)
            dve_split(dve, 1, p)
            dve_qk(dve, p)
            dve_z(dve, p - 1)
            if prefetch:
                dve_split(dve, 0, p + 1)
            dve_v(dve, p)

        @block.vector
        def _(dve):
            dve.sem_inc(z_ready, 2)
            dve.sem_inc(sq_ready, 1)
            dve.wait_ge(norm_in, 16)
            dve_split(dve, 0, 0)
            dve_split(dve, 1, 0)
            dve_qk(dve, 0)
            dve_split(dve, 0, 1)
            dve_v(dve, 0)
            with dve.Fori(1, HPAIRS - 1) as p:
                dve_pair(dve, p, True)
            dve_pair(dve, HPAIRS - 1, False)
            dve_decayed(dve, HPAIRS - 1)
            dve_z(dve, HPAIRS - 1)

        def pe_features(pe, out, part, col):
            for k in range(KT):
                c = slice(col * D, (col + 1) * D)
                last = three_pass(pe, out, w_hi[part][:, k, c], w_lo[part][:, k, c], hT_hi[:, k, :], hT_lo[:, k, :],
                                  k == 0, k == KT - 1)
            return last

        def pe_qk(pe, p, wait=True):
            pe.wait_ge(w_lo_ready[0], p + 1)
            for h in range(2):
                if wait:
                    pe.wait_ge(qk_done, 2 * p + h - 1)
                for part in range(2):
                    last = pe_features(pe, qk_ps[:, h, part, :], 0, 2 * h + part)
                last.then_inc(qk_ready, 1)

        def pe_gate_v(pe, p, wait=True):
            pe.wait_ge(w_lo_ready[1], p + 1)
            if wait:
                pe.wait_ge(gate_ready, p)
            for h in range(2):
                last = pe_features(pe, g_ps[:, h, :], 1, h)
            last.then_inc(g_ready, 1)
            if wait:
                pe.wait_ge(v_done, p)
            for t in range(QT):
                for k in range(KT):
                    tok = slice(t * P, (t + 1) * P)
                    last = three_pass(pe, v_ps[:, t, :], hT_hi[:, k, tok], hT_lo[:, k, tok], w_hi[1][:, k, 2 * D:4 * D],
                                      w_lo[1][:, k, 2 * D:4 * D], k == 0, k == KT - 1)
            last.then_inc(v_ready, 1)

        def pe_scores(pe, p):
            for h in range(2):
                pe.wait_ge(qk_lo_ready, 2 * p + h + 1)
                for jt in range(QT):
                    key = slice(jt * P, (jt + 1) * P)
                    last = three_pass(pe, a_ps[:, h, jt, :], qk_hi[:, h, 1, key], qk_lo[:, h, 1, key],
                                      qk_hi[:, h, 0, :], qk_lo[:, h, 0, :], True, True)
                last.then_inc(a_ready, 1)

        def pe_values(pe, p):
            pe.wait_ge(v_lo_ready, p + 1)
            pe.wait_ge(z_ready, 2 * p + 2)
            pe.wait_ge(sq_ready, p + 1)
            for h in range(2):
                pe.wait_ge(m_lo_ready, 4 * p + 2 * h + 2)
                for jt in range(QT):
                    f = slice(h * D, (h + 1) * D)
                    last = three_pass(pe, o_ps[:, h, :], v_hi[:, jt, f], v_lo[:, jt, f], m_hi[:, h, jt, :],
                                      m_lo[:, h, jt, :], jt == 0, jt == QT - 1)
            last.then_inc(o_ready, 1)

        @block.tensor
        def _(pe):
            pe.wait_ge(zeroed, 4)
            pe_qk(pe, 0, False)
            pe_gate_v(pe, 0, False)
            with pe.Fori(1, HPAIRS) as p:
                pe_scores(pe, p - 1)
                pe_qk(pe, p)
                pe_values(pe, p - 1)
                pe_gate_v(pe, p)
            pe_scores(pe, HPAIRS - 1)
            pe_values(pe, HPAIRS - 1)


def norm_factor(nc, square_sum, ones, row_scale):
    with ExitStack() as ctx:
        a = Alloc(nc, ctx, "nf_")
        ve = a.sb("ve", [P, QT])
        root = a.sb("root", [P, QT])
        t0 = a.sb("t0", [P, QT])
        r0 = a.sb("r0", [P, QT])
        ss = a.ps("ss", [P, QT])
        summed = a.sem("summed")
        small = a.sem("small")
        root_ready = a.sem("root_ready")
        block = ctx.enter_context(nc.Block())

        @block.tensor
        def _(pe):
            for t in range(QT):
                for h in range(2):
                    last = pe.matmul(ss[:, t:t + 1], square_sum[:, h, t * P:(t + 1) * P], ones[:, 0:1],
                                     start=h == 0, stop=h == 1)
            last.then_inc(summed, 1)

        @block.scalar
        def _(act):
            act.wait_ge(small, 1)
            act.activation(root[:, :], ve[:, :], ACT.Sqrt).then_inc(root_ready, 1)

        @block.vector
        def _(dve):
            dve.wait_ge(summed, 1)
            dve.tensor_scalar(ve[:, :], ss[:, :], 1.0 / (HEADS * D), EPS, ALU.mult, ALU.add).then_inc(small, 1)
            dve.wait_ge(root_ready, 1)
            dve.reciprocal(r0[:, :], root[:, :]).then_inc(small, 1)
            dve.wait_ge(small, 2)
            dve.tensor_tensor(t0[:, :], r0[:, :], r0[:, :], ALU.mult).then_inc(small, 1)
            dve.wait_ge(small, 3)
            dve.tensor_tensor(t0[:, :], t0[:, :], ve[:, :], ALU.mult).then_inc(small, 1)
            dve.wait_ge(small, 4)
            dve.tensor_scalar(t0[:, :], t0[:, :], -0.5, 1.5, ALU.mult, ALU.add).then_inc(small, 1)
            dve.wait_ge(small, 5)
            dve.tensor_tensor(row_scale[:, :], r0[:, :], t0[:, :], ALU.mult)


def lora_mixture(nc, w_router_a, w_b, hT, ident, x_sb, out):
    LORA_SCALE = 16.0 / float(np.sqrt(16.0))
    with ExitStack() as ctx:
        a = Alloc(nc, ctx, "mix_")
        wra = a.sb("wra", [P, KT, EXPERTS + ER])
        wb = a.sb("wb", [ER, HIDDEN])
        lm = a.sb("lm", [P, QT, EXPERTS + ER])
        beaten = a.sb("beaten", [P, QT, EXPERTS, EXPERTS])
        rank = a.sb("rank", [P, QT, EXPERTS])
        chosen = a.sb("chosen", [P, QT, EXPERTS])
        neg_max = a.sb("neg_max", [P, QT])
        e = a.sb("e", [P, QT, EXPERTS])
        ec = a.sb("ec", [P, QT, EXPERTS])
        total = a.sb("total", [P, QT])
        inverse = a.sb("inverse", [P, QT])
        gates = a.sb("gates", [P, QT, EXPERTS])
        gm = a.sb("gm", [P, QT, ER])
        gmT = a.sb("gmT", [ER, TOK])
        res = a.sb("res", [P, QT, HIDDEN])
        lm_ps = a.ps("lm_ps", [P, QT, BANK])
        gmT_ps = a.ps("gmT_ps", [ER, TOK])
        y_ps = a.ps("y_ps", [P, QT, 2, BANK])
        w_in = a.sem("w_in")
        lm_ready = a.sem("lm_ready")
        lm_copied = a.sem("lm_copied")
        small = a.sem("small")
        exp_ready = a.sem("exp_ready")
        gm_ready = a.sem("gm_ready")
        turned = a.sem("turned")
        gmT_ready = a.sem("gmT_ready")
        y_ready = a.sem("y_ready")
        res_ready = a.sem("res_ready")
        stored = a.sem("stored")
        block = ctx.enter_context(nc.Block())

        @block.sync
        def _(sp):
            sp.dma_start(wra[:, :, :], w_router_a).then_inc(w_in, 16)
            sp.dma_start(wb[:, :], w_b).then_inc(w_in, 16)
            for t in range(QT):
                sp.wait_ge(res_ready, t + 1)
                sp.dma_start(out[t], res[:, t, :]).then_inc(stored, 16)
            sp.wait_ge(stored, 16 * QT)

        @block.tensor
        def _(pe):
            pe.wait_ge(w_in, 32)
            for t in range(QT):
                for k in range(KT):
                    last = pe.matmul(lm_ps[:, t, 0:EXPERTS + ER], hT[:, k, t * P:(t + 1) * P], wra[:, k, :],
                                     start=k == 0, stop=k == KT - 1)
            last.then_inc(lm_ready, 1)
            pe.wait_ge(gm_ready, QT * EXPERTS)
            for t in range(QT):
                last = pe.transpose(gmT_ps[:, t * P:(t + 1) * P], gm[:, t, :], ident[:, :])
            last.then_inc(turned, 1)
            pe.wait_ge(gmT_ready, 1)
            for t in range(QT):
                for b in range(2):
                    last = pe.matmul(y_ps[:, t, b, :], gmT[:, t * P:(t + 1) * P], wb[:, b * BANK:(b + 1) * BANK],
                                     start=True, stop=True)
                last.then_inc(y_ready, 1)

        @block.scalar
        def _(act):
            act.wait_ge(small, 1)
            for t in range(QT):
                act.activation(e[:, t, :], lm[:, t, 0:EXPERTS], ACT.Exp, bias=neg_max[:, t:t + 1]).then_inc(exp_ready, 1)
            act.wait_ge(turned, 1)
            act.activation(gmT[:, :], gmT_ps[:, :], ACT.Copy).then_inc(gmT_ready, 1)

        @block.vector
        def _(dve):
            dve.memset(beaten[:, :, :, :], 0.0).then_inc(lm_copied, 1)
            dve.wait_ge(lm_ready, 1)
            dve.tensor_copy(lm[:, :, :], lm_ps[:, :, 0:EXPERTS + ER]).then_inc(lm_copied, 1)
            dve.wait_ge(lm_copied, 2)
            dve.tensor_reduce(neg_max[:, :], lm[:, :, 0:EXPERTS], AX.X, ALU.max, negate=True).then_inc(small, 1)
            count = 1
            for t in range(QT):
                for j in range(EXPERTS):
                    for rows, op in ((slice(j + 1, EXPERTS), ALU.is_le), (slice(0, j), ALU.is_lt)):
                        if rows.start < rows.stop:
                            dve.tensor_scalar(beaten[:, t, rows, j], lm[:, t, rows], lm[:, t, j:j + 1], None, op).then_inc(small, 1)
                            count += 1
            dve.wait_ge(small, count)
            dve.tensor_reduce(rank[:, :, :], beaten[:, :, :, :], AX.X, ALU.add).then_inc(small, 1)
            dve.wait_ge(small, count + 1)
            dve.tensor_scalar(chosen[:, :, :], rank[:, :, :], 2.0, None, ALU.is_lt).then_inc(small, 1)
            dve.wait_ge(small, count + 2)
            dve.wait_ge(exp_ready, QT)
            dve.tensor_tensor(ec[:, :, :], e[:, :, :], chosen[:, :, :], ALU.mult).then_inc(small, 1)
            dve.wait_ge(small, count + 3)
            dve.tensor_reduce(total[:, :], ec[:, :, :], AX.X, ALU.add).then_inc(small, 1)
            dve.wait_ge(small, count + 4)
            dve.reciprocal(inverse[:, :], total[:, :]).then_inc(small, 1)
            dve.wait_ge(small, count + 5)
            for t in range(QT):
                dve.tensor_scalar(gates[:, t, :], ec[:, t, :], inverse[:, t:t + 1], LORA_SCALE,
                                  ALU.mult, ALU.mult).then_inc(small, 1)
            dve.wait_ge(small, count + 5 + QT)
            for t in range(QT):
                for x in range(EXPERTS):
                    r = slice(x * LORA, (x + 1) * LORA)
                    dve.tensor_scalar(gm[:, t, r], lm[:, t, EXPERTS + r.start:EXPERTS + r.stop], gates[:, t, x:x + 1],
                                      None, ALU.mult).then_inc(gm_ready, 1)
            for t in range(QT):
                dve.wait_ge(y_ready, t + 1)
                dve.tensor_tensor(res[:, t, :], y_ps[:, t, :, :].rearrange("p a b -> p (a b)"), x_sb[:, t, :],
                                  ALU.add).then_inc(res_ready, 1)


def perceiver_layer(nc, x, ctxT, wk, wv, wq, wo, w_qk, w_gv, decay, norm_w, w_out, w_router_a, w_b, out):
    kT_dram = nc.dram_tensor("kT_scratch", (KVH, D, KV), F32, kind="Internal").ap()
    v_dram = nc.dram_tensor("v_scratch", (KVH, P, KVT, D), F32, kind="Internal").ap()
    oT_dram = nc.dram_tensor("oT_scratch", (HEADS, D, TOK), F32, kind="Internal").ap()
    zT_dram = nc.dram_tensor("zT_scratch", (HEADS, D, TOK), F32, kind="Internal").ap()
    with ExitStack() as ctx:
        a = Alloc(nc, ctx, "")
        ident = a.sb("ident", [P, P])
        ones = a.sb("ones", [P, P])
        x_sb = a.sb("x_sb", [P, QT, HIDDEN])
        zero_done = a.sem("zero_done")
        with ExitStack() as setup, nc.Block() as block:
            @block.gpsimd
            def _(pool):
                pool.memset(ones[:, :], 1.0)
                pool.memset(ident[:, :], 0.0).then_inc(zero_done, 1)
                pool.wait_ge(zero_done, 1)
                pool.affine_select(out=ident[:, :], in_=ident[:, :], compare_op=ALU.not_equal, fill=1.0, base=0,
                                   pattern=[[-1, P]], channel_multiplier=1)
        with ExitStack() as inner:
            b = Alloc(nc, inner, "x_")
            hT_hi = b.sb("hT_hi", [P, KT, TOK], F32R)
            hT_lo = b.sb("hT_lo", [P, KT, TOK], F32R)
            layernorm_and_turn(nc, "ln1_", x_sb, hT_hi, hT_lo, ident, x_dram=x)
            project_keys_values(nc, ctxT, wk, wv, hT_hi, hT_lo, kT_dram, v_dram)
            cross_attention(nc, wq, kT_dram, v_dram, hT_hi, hT_lo, ident, ones, oT_dram)
        project_out(nc, "wo_", oT_dram, wo, x_sb, x_sb, None)
        square_sum = a.sb("square_sum", [P, 2, TOK])
        row_scale = a.sb("row_scale", [P, QT])
        with ExitStack() as inner:
            b = Alloc(nc, inner, "l_")
            hT_hi = b.sb("hT_hi", [P, KT, TOK], F32R)
            hT_lo = b.sb("hT_lo", [P, KT, TOK], F32R)
            layernorm_and_turn(nc, "ln2_", x_sb, hT_hi, hT_lo, ident)
            linear_attention(nc, w_qk, w_gv, decay, norm_w, hT_hi, hT_lo, zT_dram, square_sum)
        norm_factor(nc, square_sum, ones, row_scale)
        project_out(nc, "lo_", zT_dram, w_out, x_sb, x_sb, row_scale)
        with ExitStack() as inner:
            b = Alloc(nc, inner, "m_")
            hT = b.sb("hT", [P, KT, TOK])
            layernorm_and_turn(nc, "ln3_", x_sb, hT, None, ident)
            lora_mixture(nc, w_router_a, w_b, hT, ident, x_sb, out)


def decay_table():
    layer, layers = 1, 32
    factor = 1.0 - layer / (layers - 1 + 1e-05) + 1e-05
    slope = (2.0 ** (-8.0 / HEADS)) ** (np.arange(HEADS) + 1.0) * factor
    dist = np.arange(TOK)[None, :] - np.arange(P)[:, None]
    table = np.where(dist >= 0, np.exp(-slope[:, None, None] * np.maximum(dist, 0)), 0.0)
    return np.ascontiguousarray(table.reshape(HPAIRS, 2, P, TOK).transpose(0, 2, 1, 3)).astype(np.float32)


def kernel(x, ctx_4096, L0_xattn_Wq, L0_xattn_Wk, L0_xattn_Wv, L0_xattn_Wo, L0_attn_qkv_w, L0_attn_out_w,
           L0_attn_gate_w, L0_attn_norm_w, L0_ffn_A, L0_ffn_B, L0_ffn_Wr):
    import concourse.bacc as bacc
    from concourse.bass_utils import run_bass_kernel_spmd

    def turned(w):
        return np.asarray(w).T.reshape(KT, P, -1).transpose(1, 0, 2)

    qkv = turned(L0_attn_qkv_w).reshape(P, KT, HPAIRS, 2, 3, D)
    gate = turned(L0_attn_gate_w).reshape(P, KT, HPAIRS, 2, D)
    w_gv = np.stack([gate, qkv[:, :, :, :, 2]], axis=3)
    data = {
        "x": np.asarray(x).reshape(QT, P, HIDDEN).transpose(1, 0, 2),
        "ctxT": np.asarray(ctx_4096).reshape(NCHUNK, CCHUNK, KT, P).transpose(0, 3, 2, 1),
        "wk": np.asarray(L0_xattn_Wk).reshape(KT, P, KVH * D).transpose(1, 0, 2),
        "wv": np.asarray(L0_xattn_Wv).reshape(KT, P, KVH * D).transpose(1, 0, 2),
        "wq": np.asarray(L0_xattn_Wq).reshape(KT, P, HEADS, D).transpose(2, 1, 0, 3),
        "wo": np.asarray(L0_xattn_Wo).reshape(HEADS, D, HIDDEN),
        "w_qk": qkv[:, :, :, :, 0:2].transpose(2, 0, 1, 3, 4, 5).reshape(HPAIRS, P, KT, 4 * D),
        "w_gv": w_gv.transpose(2, 0, 1, 3, 4, 5).reshape(HPAIRS, P, KT, 4 * D),
        "decay": decay_table(),
        "norm_w": np.asarray(L0_attn_norm_w).reshape(HEADS, D).T,
        "w_out": np.asarray(L0_attn_out_w).T.reshape(HEADS, D, HIDDEN),
        "w_router_a": np.concatenate([turned(L0_ffn_Wr), turned(np.asarray(L0_ffn_A).reshape(ER, HIDDEN))], axis=2),
        "w_b": np.asarray(L0_ffn_B).transpose(0, 2, 1).reshape(ER, HIDDEN),
    }
    nc = bacc.Bacc("TRN2", target_bir_lowering=False, num_devices=1)
    arrays, args = {}, []
    for name, value in data.items():
        value = np.ascontiguousarray(value)
        arrays[f"in_{name}"] = value
        args.append(nc.dram_tensor(f"in_{name}", value.shape, mybir.dt.from_np(value.dtype), kind="ExternalInput").ap())
    out = nc.dram_tensor("out", (QT, P, HIDDEN), F32, kind="ExternalOutput").ap()
    perceiver_layer(nc, *args, out)
    result = run_bass_kernel_spmd(nc, [arrays], core_ids=[0])
    return result.results[0]["out"].reshape(1, TOK, HIDDEN)
```

```python
from contextlib import ExitStack

import numpy as np

import concourse.bass as bass
from concourse import mybir

F32 = mybir.dt.float32
F32R = mybir.dt.float32r
ALU = mybir.AluOpType
ACT = mybir.ActivationFunctionType
AX = mybir.AxisListType

P = 128
HIDDEN = 1024
KT = HIDDEN // P
TOK = 256
QT = TOK // P
CTX = 4096
KV = CTX + TOK
KVT = KV // P
HEADS = 32
D = 128
KVH = 4
GROUP = HEADS // KVH
SCALE = 1.0 / float(np.sqrt(D))
EPS = 1e-5
BANK = 512
CCHUNK = 512
NCHUNK = CTX // CCHUNK
EXPERTS = 4
LORA = 16
ER = EXPERTS * LORA


class Alloc:

    def __init__(self, nc, ctx, prefix):
        self.nc, self.ctx, self.prefix = nc, ctx, prefix

    def sb(self, name, shape, dt=F32):
        return self.ctx.enter_context(self.nc.sbuf_tensor(self.prefix + name, shape, dt))

    def ps(self, name, shape, dt=F32):
        return self.ctx.enter_context(self.nc.psum_tensor(self.prefix + name, shape, dt))

    def sem(self, name):
        return self.ctx.enter_context(self.nc.semaphore(self.prefix + name))


def f32(ap):
    return ap.bitcast(F32)


def three_pass(pe, out, w_hi, w_lo, m_hi, m_lo, first, last):
    pe.matmul(out, w_hi, m_hi, start=first, stop=False)
    pe.matmul(out, w_hi, m_lo, start=False, stop=False)
    return pe.matmul(out, w_lo, m_hi, start=False, stop=last)


def layernorm_and_turn(nc, name, x_sb, hT_hi, hT_lo, ident, x_dram=None):
    with ExitStack() as ctx:
        a = Alloc(nc, ctx, name)
        stats = a.sb("stats", [P, QT, 2, 6])
        mv = a.sb("mv", [P, QT, 2])
        ve = a.sb("ve", [P, QT])
        root = a.sb("root", [P, QT])
        r0 = a.sb("r0", [P, QT])
        t0 = a.sb("t0", [P, QT])
        rstd = a.sb("rstd", [P, QT])
        h = a.sb("h", [P, QT, HIDDEN])
        turned = a.ps("turned", [P, KT, TOK])
        x_in = a.sem("x_in")
        small = a.sem("small")
        root_ready = a.sem("root_ready")
        h_ready = a.sem("h_ready")
        turned_ready = a.sem("turned_ready")
        hi_ready = a.sem("hi_ready")
        block = ctx.enter_context(nc.Block())

        @block.sync
        def _(sp):
            if x_dram is not None:
                sp.dma_start(x_sb[:, :, :], x_dram).then_inc(x_in, 16)

        @block.vector
        def _(dve):
            if x_dram is not None:
                dve.wait_ge(x_in, 16)
            for t in range(QT):
                for half in range(2):
                    dve.bn_stats(stats[:, t, half, :], x_sb[:, t, half * 512:(half + 1) * 512]).then_inc(small, 1)
            dve.wait_ge(small, 2 * QT)
            for t in range(QT):
                dve.bn_aggr(mv[:, t, :], stats[:, t, :, :].rearrange("p a b -> p (a b)")).then_inc(small, 1)
            dve.wait_ge(small, 3 * QT)
            dve.tensor_scalar(ve[:, :], mv[:, :, 1], EPS, None, ALU.add).then_inc(small, 1)
            dve.wait_ge(root_ready, 1)
            dve.reciprocal(r0[:, :], root[:, :]).then_inc(small, 1)
            dve.wait_ge(small, 3 * QT + 2)
            dve.tensor_tensor(t0[:, :], r0[:, :], r0[:, :], ALU.mult).then_inc(small, 1)
            dve.wait_ge(small, 3 * QT + 3)
            dve.tensor_tensor(t0[:, :], t0[:, :], ve[:, :], ALU.mult).then_inc(small, 1)
            dve.wait_ge(small, 3 * QT + 4)
            dve.tensor_scalar(t0[:, :], t0[:, :], -0.5, 1.5, ALU.mult, ALU.add).then_inc(small, 1)
            dve.wait_ge(small, 3 * QT + 5)
            dve.tensor_tensor(rstd[:, :], r0[:, :], t0[:, :], ALU.mult).then_inc(small, 1)
            dve.wait_ge(small, 3 * QT + 6)
            for t in range(QT):
                dve.tensor_scalar(h[:, t, :], x_sb[:, t, :], mv[:, t, 0:1], rstd[:, t:t + 1],
                                  ALU.subtract, ALU.mult).then_inc(h_ready, 1)
            if hT_lo is not None:
                for b in range(KT // 2):
                    dve.wait_ge(hi_ready, b + 1)
                    dve.tensor_tensor(hT_lo[:, 2 * b:2 * b + 2, :], turned[:, 2 * b:2 * b + 2, :],
                                      f32(hT_hi[:, 2 * b:2 * b + 2, :]), ALU.subtract)

        @block.scalar
        def _(act):
            act.wait_ge(small, 3 * QT + 1)
            act.activation(root[:, :], ve[:, :], ACT.Sqrt).then_inc(root_ready, 1)
            for b in range(KT // 2):
                act.wait_ge(turned_ready, b + 1)
                act.activation(hT_hi[:, 2 * b:2 * b + 2, :], turned[:, 2 * b:2 * b + 2, :],
                               ACT.Copy).then_inc(hi_ready, 1)

        @block.tensor
        def _(pe):
            pe.wait_ge(h_ready, QT)
            for b in range(KT // 2):
                for k in (2 * b, 2 * b + 1):
                    for t in range(QT):
                        last = pe.transpose(turned[:, k, t * P:(t + 1) * P], h[:, t, k * P:(k + 1) * P], ident[:, :])
                last.then_inc(turned_ready, 1)


def project_keys_values(nc, ctxT, wk, wv, hT_hi, hT_lo, kT_dram, v_dram):
    with ExitStack() as ctx:
        a = Alloc(nc, ctx, "kv_")
        w_raw = a.sb("w_raw", [P, KT, KVH * D])
        wk_hi = a.sb("wk_hi", [P, KT, KVH * D], F32R)
        wk_lo = a.sb("wk_lo", [P, KT, KVH * D], F32R)
        wv_hi = a.sb("wv_hi", [P, KT, KVH * D], F32R)
        wv_lo = a.sb("wv_lo", [P, KT, KVH * D], F32R)
        c_raw = a.sb("c_raw", [P, KT, CCHUNK])
        c_hi = [a.sb(f"c_hi{i}", [P, KT, CCHUNK], F32R) for i in range(2)]
        c_lo = [a.sb(f"c_lo{i}", [P, KT, CCHUNK], F32R) for i in range(2)]
        k_out = a.sb("k_out", [P, KVH, CCHUNK])
        v_out = a.sb("v_out", [P, KVH, CCHUNK // P, D])
        k_ps = a.ps("k_ps", [P, KVH, BANK])
        v_ps = a.ps("v_ps", [P, CCHUNK // P, BANK])
        w_in = a.sem("w_in")
        w_hi_ready = a.sem("w_hi_ready")
        w_lo_ready = a.sem("w_lo_ready")
        c_in = a.sem("c_in")
        c_hi_ready = a.sem("c_hi_ready")
        c_lo_ready = a.sem("c_lo_ready")
        k_ready = a.sem("k_ready")
        v_ready = a.sem("v_ready")
        k_copied = a.sem("k_copied")
        v_copied = a.sem("v_copied")
        k_stored = a.sem("k_stored")
        v_stored = a.sem("v_stored")
        VT = CCHUNK // P
        block = ctx.enter_context(nc.Block())

        def load(sp, c):
            sp.dma_start(c_raw[:, :, :], ctxT[bass.ds(c, 1)].rearrange("c p k n -> p (c k) n")).then_inc(c_in, 16)

        def store(sp, c, tiles):
            n = tiles * P
            sp.wait_ge(k_copied, KVH + KVH * (c + 1))
            sp.dma_start(kT_dram[:, :, bass.ds(c * CCHUNK, n)].rearrange("g p n -> p g n"),
                         k_out[:, :, 0:n]).then_inc(k_stored, 16)
            sp.wait_ge(v_copied, VT * (c + 1) + tiles)
            sp.dma_start(v_dram[:, :, bass.ds(c * VT, tiles), :].rearrange("g p t d -> p g t d"),
                         v_out[:, :, 0:tiles, :]).then_inc(v_stored, 16)

        @block.sync
        def _(sp):
            sp.sem_inc(k_stored, 16)
            sp.sem_inc(v_stored, 16)
            sp.dma_start(w_raw[:, :, :], wk).then_inc(w_in, 16)
            load(sp, 0)
            sp.wait_ge(w_lo_ready, 1)
            sp.dma_start(w_raw[:, :, :], wv).then_inc(w_in, 16)
            sp.wait_ge(c_lo_ready, 1)
            load(sp, 1)
            with sp.Fori(0, NCHUNK - 2) as c:
                sp.wait_ge(c_lo_ready, c + 2)
                load(sp, c + 2)
                store(sp, c, VT)
            store(sp, NCHUNK - 2, VT)
            store(sp, NCHUNK - 1, VT)
            store(sp, NCHUNK, QT)
            sp.wait_ge(k_stored, 16 * (NCHUNK + 2))
            sp.wait_ge(v_stored, 16 * (NCHUNK + 2))

        def copy_keys(act, c, n):
            act.wait_ge(k_stored, 16 * (c + 1))
            for g in range(KVH):
                act.wait_ge(k_ready, KVH * c + g + 1)
                act.activation(k_out[:, g, 0:n], k_ps[:, g, 0:n], ACT.Copy).then_inc(k_copied, 1)

        @block.scalar
        def _(act):
            act.sem_inc(k_copied, KVH)
            for i, w_hi in enumerate((wk_hi, wv_hi)):
                act.wait_ge(w_in, 16 * (i + 1))
                act.activation(w_hi[:, :, :], w_raw[:, :, :], ACT.Copy).then_inc(w_hi_ready, 1)
                if i == 0:
                    act.wait_ge(c_in, 16)
                    act.activation(c_hi[0][:, :, :], c_raw[:, :, :], ACT.Copy).then_inc(c_hi_ready, 1)
            act.wait_ge(c_in, 32)
            act.activation(c_hi[1][:, :, :], c_raw[:, :, :], ACT.Copy).then_inc(c_hi_ready, 1)
            with act.Fori(0, NCHUNK // 2 - 1) as i:
                for par in range(2):
                    c = 2 * i + par
                    copy_keys(act, c, CCHUNK)
                    act.wait_ge(c_in, 16 * (c + 3))
                    act.wait_ge(v_ready, VT * (c + 1))
                    act.activation(c_hi[par][:, :, :], c_raw[:, :, :], ACT.Copy).then_inc(c_hi_ready, 1)
            copy_keys(act, NCHUNK - 2, CCHUNK)
            copy_keys(act, NCHUNK - 1, CCHUNK)
            copy_keys(act, NCHUNK, TOK)

        def copy_values(dve, c, tiles):
            dve.wait_ge(v_stored, 16 * (c + 1))
            for t in range(tiles):
                dve.wait_ge(v_ready, VT * c + t + 1)
                dve.tensor_copy(v_out[:, :, t, :], v_ps[:, t, :].rearrange("p (g d) -> p g d", d=D)).then_inc(v_copied, 1)

        def split_low(dve, c, par):
            dve.wait_ge(c_hi_ready, c + 1)
            dve.tensor_tensor(c_lo[par][:, :, :], c_raw[:, :, :], f32(c_hi[par][:, :, :]),
                              ALU.subtract).then_inc(c_lo_ready, 1)

        @block.vector
        def _(dve):
            dve.sem_inc(v_copied, VT)
            for i, (w_hi, w_lo) in enumerate(((wk_hi, wk_lo), (wv_hi, wv_lo))):
                dve.wait_ge(w_hi_ready, i + 1)
                dve.tensor_tensor(w_lo[:, :, :], w_raw[:, :, :], f32(w_hi[:, :, :]), ALU.subtract).then_inc(w_lo_ready, 1)
                if i == 0:
                    split_low(dve, 0, 0)
            split_low(dve, 1, 1)
            with dve.Fori(0, NCHUNK // 2 - 1) as i:
                for par in range(2):
                    c = 2 * i + par
                    copy_values(dve, c, VT)
                    split_low(dve, c + 2, par)
            copy_values(dve, NCHUNK - 2, VT)
            copy_values(dve, NCHUNK - 1, VT)
            copy_values(dve, NCHUNK, QT)

        def chunk(pe, c, hi, lo, tiles):
            n = tiles * P
            for g in range(KVH):
                pe.wait_ge(k_copied, KVH * c + g + 1)
                for k in range(KT):
                    w = slice(g * D, (g + 1) * D)
                    last = three_pass(pe, k_ps[:, g, 0:n], wk_hi[:, k, w], wk_lo[:, k, w],
                                      hi[:, k, 0:n], lo[:, k, 0:n], k == 0, k == KT - 1)
                last.then_inc(k_ready, 1)
            for t in range(tiles):
                pe.wait_ge(v_copied, VT * c + t + 1)
                for k in range(KT):
                    s = slice(t * P, (t + 1) * P)
                    last = three_pass(pe, v_ps[:, t, :], hi[:, k, s], lo[:, k, s],
                                      wv_hi[:, k, :], wv_lo[:, k, :], k == 0, k == KT - 1)
                last.then_inc(v_ready, 1)

        @block.tensor
        def _(pe):
            pe.wait_ge(w_lo_ready, 2)
            with pe.Fori(0, NCHUNK // 2) as i:
                for par in range(2):
                    c = 2 * i + par
                    pe.wait_ge(c_lo_ready, c + 1)
                    chunk(pe, c, c_hi[par], c_lo[par], VT)
            chunk(pe, NCHUNK, hT_hi, hT_lo, QT)


PAIRS = KVT // 2
PIECES = 4
PIECE = KV // PIECES
UNITS = [(qt, c0, min(BANK, KV - c0)) for qt in range(QT) for c0 in range(0, KV, BANK)]
NU = len(UNITS)
UPR = NU // QT
NS = 4
NPT = 3
LAG = 2
S_LAST = 12
DOUBLE = NU - 1 - S_LAST
UNITS_OF_STEP = [range(2 * j, 2 * j + 2) if j < DOUBLE else range(j + DOUBLE, j + DOUBLE + 1) if j <= S_LAST
                 else range(0) for j in range(PAIRS)]
Q_STEPS = range(S_LAST + 1, PAIRS)


def piece_of(end):
    return (end - 1) // PIECE


def cross_attention(nc, wq, kT_dram, v_dram, hT_hi, hT_lo, ident, ones, oT_dram):
    with ExitStack() as ctx:
        a = Alloc(nc, ctx, "xa_")
        kT_hi = a.sb("kT_hi", [P, KV], F32R)
        kT_lo = a.sb("kT_lo", [P, KV], F32R)
        v_hi = a.sb("v_hi", [P, KV], F32R)
        v_lo = a.sb("v_lo", [P, KV], F32R)
        rows = [[a.sb(f"rows{i}{t}", [P, KV]) for t in range(QT)] for i in range(2)]
        stage = [a.sb(f"stage{i}", [P, PIECE]) for i in range(2)]
        w_raw = a.sb("w_raw", [P, KT, D])
        w_hi = a.sb("w_hi", [P, KT, D], F32R)
        w_lo = a.sb("w_lo", [P, KT, D], F32R)
        qT_hi = a.sb("qT_hi", [P, TOK], F32R)
        qT_lo = a.sb("qT_lo", [P, TOK], F32R)
        pT_hi = [a.sb(f"pT_hi{i}", [P, 2, TOK], F32R) for i in range(NPT)]
        pT_lo = [a.sb(f"pT_lo{i}", [P, 2, TOK], F32R) for i in range(NPT)]
        maxima = a.sb("maxima", [P, 2, QT, UPR])
        neg_max = a.sb("neg_max", [P, 2, QT])
        sums = a.sb("sums", [P, 2, QT, PIECES])
        total = a.sb("total", [P, QT])
        inverse = a.sb("inverse", [P, QT])
        diag = a.sb("diag", [P, TOK])
        scale_rows = a.sb("scale_rows", [P, TOK])
        o_out = [a.sb(f"o_out{i}", [P, TOK]) for i in range(2)]
        s_ps = a.ps("s_ps", [P, NS, BANK])
        t_ps = a.ps("t_ps", [P, 2, 2, TOK])
        o_ps = a.ps("o_ps", [P, 2, TOK])
        m_ps = a.ps("m_ps", [P, 2, TOK])

        piece_asked = a.sem("piece_asked")
        piece_in = [a.sem(f"piece_in{i}") for i in range(2)]
        piece_hi = a.sem("piece_hi")
        piece_lo = a.sem("piece_lo")
        w_in = a.sem("w_in")
        w_hi_ready = a.sem("w_hi_ready")
        w_lo_ready = a.sem("w_lo_ready")
        q_ready = a.sem("q_ready")
        q_hi_ready = a.sem("q_hi_ready")
        q_lo_ready = a.sem("q_lo_ready")
        s_ready = a.sem("s_ready")
        s_drained = a.sem("s_drained")
        max_ready = a.sem("max_ready")
        exp_done = a.sem("exp_done")
        turned = a.sem("turned")
        pT_hi_ready = a.sem("pT_hi_ready")
        pT_lo_ready = a.sem("pT_lo_ready")
        pv_done = a.sem("pv_done")
        sum_ready = a.sem("sum_ready")
        diag_ready = a.sem("diag_ready")
        spread = a.sem("spread")
        spread_copied = a.sem("spread_copied")
        o_ready = a.sem("o_ready")
        o_stored = [a.sem(f"o_stored{i}") for i in range(2)]
        block = ctx.enter_context(nc.Block())

        def slots(eng, kv_head_slot):
            def kv_head(g, last):
                for u in range(2):
                    kv_head_slot(eng, g, GROUP * g + u, u, last)
                with eng.Fori(1, GROUP // 2 - 1) as i:
                    for par in range(2):
                        kv_head_slot(eng, g, GROUP * g + 2 * i + par, 2 + par, last)
                for u in range(GROUP - 2, GROUP):
                    kv_head_slot(eng, g, GROUP * g + u, u, last)

            with eng.Fori(0, KVH - 1) as g:
                kv_head(g, False)
            kv_head(KVH - 1, True)

        def flags(u, last):
            return not (last and u == GROUP - 1), not (last and u >= GROUP - 2)

        def ahead(n, par, j):
            return (n, par, j + LAG) if j + LAG < PAIRS else (n + 1, 1 - par, j + LAG - PAIRS)

        def pt_free(n, j):
            last = j - NPT if j >= NPT else max(x for x in range(PAIRS) if x % NPT == j) - PAIRS
            return NPT + PAIRS * n + last + 1

        def load_weight(sp, n):
            sp.wait_ge(w_lo_ready, n + 1)
            sp.dma_start(w_raw[:, :, :], wq[bass.ds(n, 1)].rearrange("h p k d -> p (h k) d")).then_inc(w_in, 16)

        def load_piece(sp, g, i):
            sp.wait_ge(piece_lo, 2 * PIECES * g + i + 1)
            sp.sem_inc(piece_asked, 1)
            source = (kT_dram[bass.ds(g, 1)].rearrange("g p n -> (g p) n") if i < PIECES else
                      v_dram[bass.ds(g, 1)].rearrange("g p t d -> (g p) (t d)"))
            c0 = i % PIECES * PIECE
            sp.dma_start(stage[i % 2][:, :], source[:, c0:c0 + PIECE]).then_inc(piece_in[i % 2], 16)

        def store_o(sp, n, par):
            sp.wait_ge(o_ready, n + 2)
            sp.dma_start(oT_dram[bass.ds(n, 1)].rearrange("h p n -> (h p) n"), o_out[par][:, :]).then_inc(o_stored[par], 16)

        def sync_slot(sp, g, n, u, last):
            if flags(u, last)[1]:
                load_weight(sp, n + 2)
            if not last and u == GROUP - 2:
                for i in range(PIECES):
                    load_piece(sp, g + 1, i)
            if not last and u == GROUP - 1:
                for i in range(PIECES, 2 * PIECES):
                    load_piece(sp, g + 1, i)
            store_o(sp, n, u % 2)

        @block.sync
        def _(sp):
            for par in range(2):
                sp.sem_inc(o_stored[par], 16)
            load_weight(sp, 0)
            for i in range(PIECES):
                load_piece(sp, 0, i)
            load_weight(sp, 1)
            load_piece(sp, 0, 4)
            load_piece(sp, 0, 5)
            load_piece(sp, 0, 6)
            load_piece(sp, 0, 7)
            slots(sp, sync_slot)
            for par in range(2):
                sp.wait_ge(o_stored[par], 16 * (HEADS // 2 + 1))

        def act_piece(act, g, i, first=False):
            act.wait_ge(piece_in[i % 2], 16 * (PIECES * g + i // 2 + 1))
            end = (i % PIECES + 1) * PIECE
            if not first and i < PIECES:
                act.wait_ge(s_ready, NU * (GROUP * g - 1) + UPR + -(-end // BANK))
            if not first and i >= PIECES:
                act.wait_ge(pv_done, NPT + PAIRS * (GROUP * g - 1) + -(-end // (2 * P)))
            to = (kT_hi if i < PIECES else v_hi)[:, end - PIECE:end]
            act.activation(to, stage[i % 2][:, :], ACT.Copy).then_inc(piece_hi, 1)

        def act_weight(act, n):
            act.wait_ge(w_in, 16 * (n + 1))
            act.wait_ge(q_ready, n + 1)
            act.activation(w_hi[:, :, :], w_raw[:, :, :], ACT.Copy).then_inc(w_hi_ready, 1)

        def act_query(act, n):
            act.wait_ge(q_ready, n + 2)
            act.activation(qT_hi[:, :], m_ps[:, 0, :], ACT.Copy).then_inc(q_hi_ready, 1)

        def act_exp(act, n, par, qt, e):
            row = rows[par][qt][:, e * PIECE:(e + 1) * PIECE]
            act.wait_ge(max_ready, QT * n + qt + 1)
            act.activation(row, row, ACT.Exp, bias=neg_max[:, par, qt:qt + 1],
                           accum_out=sums[:, par, qt, e:e + 1]).then_inc(exp_done, 1)

        def act_turned(act, n, par, j):
            act.wait_ge(turned, PAIRS * n + j + 1)
            act.wait_ge(pv_done, pt_free(n, j))
            act.activation(pT_hi[j % NPT][:, :, :], t_ps[:, (par * PAIRS + j) % 2, :, :],
                           ACT.Copy).then_inc(pT_hi_ready, 1)

        def act_slot(act, g, n, u, last):
            par = u % 2
            has_next, has_after = flags(u, last)
            for j in range(PAIRS):
                if has_next or j + LAG < PAIRS:
                    act_turned(act, *ahead(n, par, j))
                if u == 0 and j == 1:
                    act_piece(act, g, 7)
                if j in (1, 3):
                    act_exp(act, n, par, 1, 2 + j // 2)
                if has_after and j == 5:
                    act_weight(act, n + 2)
                if has_next and 7 <= j <= 10:
                    act_exp(act, n + 1, 1 - par, 0, j - 7)
                if j == 12:
                    act.wait_ge(spread, n + 1)
                    act.activation(scale_rows[:, :], m_ps[:, 1, :], ACT.Copy).then_inc(spread_copied, 1)
                if not last and u == GROUP - 2 and j in (8, 10, 12, 14):
                    act_piece(act, g + 1, (j - 8) // 2)
                if not last and u == GROUP - 1 and j in (6, 10, 14):
                    act_piece(act, g + 1, PIECES + (j - 6) // 4)
                if has_next and 13 <= j <= 14:
                    act_exp(act, n + 1, 1 - par, 1, j - 13)
                if has_after and j == 16:
                    act_query(act, n + 2)

        @block.scalar
        def _(act):
            act.sem_inc(spread_copied, 1)
            act_weight(act, 0)
            for i in range(PIECES):
                act_piece(act, 0, i, first=True)
            act_query(act, 0)
            act_weight(act, 1)
            for i in range(PIECES, 2 * PIECES - 1):
                act_piece(act, 0, i, first=True)
            for e in range(PIECES):
                act_exp(act, 0, 0, 0, e)
            for e in range(2):
                act_exp(act, 0, 0, 1, e)
            act_query(act, 1)
            for j in range(LAG):
                act_turned(act, 0, 0, j)
            slots(act, act_slot)

        def pool_piece(pool, g, i):
            pool.wait_ge(piece_hi, 2 * PIECES * g + i + 1)
            at = slice(i % PIECES * PIECE, (i % PIECES + 1) * PIECE)
            hi, lo = (kT_hi, kT_lo) if i < PIECES else (v_hi, v_lo)
            pool.tensor_tensor(lo[:, at], stage[i % 2][:, :], f32(hi[:, at]), ALU.subtract).then_inc(piece_lo, 1)

        def pool_weight(pool, n):
            pool.wait_ge(w_hi_ready, n + 1)
            pool.tensor_tensor(w_lo[:, :, :], w_raw[:, :, :], f32(w_hi[:, :, :]), ALU.subtract).then_inc(w_lo_ready, 1)

        def pool_slot(pool, g, n, u, last):
            if u == 0:
                pool_piece(pool, g, 7)
            if flags(u, last)[1]:
                pool_weight(pool, n + 2)
            if not last and u == GROUP - 2:
                for i in range(PIECES):
                    pool_piece(pool, g + 1, i)
            if not last and u == GROUP - 1:
                for i in range(PIECES, 2 * PIECES - 1):
                    pool_piece(pool, g + 1, i)

        @block.gpsimd
        def _(pool):
            pool.sem_inc(w_lo_ready, 1)
            pool.sem_inc(piece_lo, 2)
            pool_weight(pool, 0)
            for i in range(PIECES):
                pool_piece(pool, 0, i)
            pool_weight(pool, 1)
            for i in range(PIECES, 2 * PIECES - 1):
                pool_piece(pool, 0, i)
            slots(pool, pool_slot)

        def dve_query(dve, n):
            dve.wait_ge(q_hi_ready, n + 1)
            dve.tensor_tensor(qT_lo[:, :], m_ps[:, 0, :], f32(qT_hi[:, :]), ALU.subtract).then_inc(q_lo_ready, 1)

        def dve_scores(dve, n, par, k):
            qt, c0, width = UNITS[k]
            dve.wait_ge(s_ready, NU * n + k + 1)
            dve.tensor_scalar(rows[par][qt][:, c0:c0 + width], s_ps[:, (par * NU + k) % NS, 0:width], SCALE, None,
                              ALU.mult, ALU.max, accum_out=maxima[:, par, qt, k % UPR:k % UPR + 1]).then_inc(s_drained, 1)
            if k % UPR == UPR - 1:
                dve.wait_ge(s_drained, NS + NU * n + k + 1)
                dve.tensor_reduce(neg_max[:, par, qt:qt + 1], maxima[:, par, qt, :], AX.X, ALU.max,
                                  negate=True).then_inc(max_ready, 1)

        def dve_inverse(dve, n, par):
            dve.wait_ge(exp_done, QT * PIECES * (n + 1))
            dve.tensor_reduce(total[:, :], sums[:, par, :, :], AX.X, ALU.add).then_inc(sum_ready, 1)
            dve.wait_ge(sum_ready, 2 * n + 1)
            dve.reciprocal(inverse[:, :], total[:, :]).then_inc(sum_ready, 1)
            dve.wait_ge(sum_ready, 2 * n + 2)
            for qt in range(QT):
                dve.tensor_scalar(diag[:, qt * P:(qt + 1) * P], ident[:, :], inverse[:, qt:qt + 1], None,
                                  ALU.mult).then_inc(diag_ready, 1)

        def dve_turned(dve, n, par, j):
            dve.wait_ge(pT_hi_ready, PAIRS * n + j + 1)
            dve.tensor_tensor(pT_lo[j % NPT][:, :, :], t_ps[:, (par * PAIRS + j) % 2, :, :],
                              f32(pT_hi[j % NPT][:, :, :]), ALU.subtract).then_inc(pT_lo_ready, 1)

        def dve_slot(dve, g, n, u, last):
            par = u % 2
            has_next, has_after = flags(u, last)
            for j in range(PAIRS):
                if has_next or j + LAG < PAIRS:
                    dve_turned(dve, *ahead(n, par, j))
                if has_next:
                    for k in UNITS_OF_STEP[j]:
                        dve_scores(dve, n + 1, 1 - par, k)
                if j == 9:
                    dve_inverse(dve, n, par)
                if has_after and j == 16:
                    dve_query(dve, n + 2)
            dve.wait_ge(spread_copied, n + 2)
            dve.wait_ge(o_stored[par], 8 * (n - par) + 16)
            dve.wait_ge(pv_done, NPT + PAIRS * (n + 1))
            dve.tensor_tensor(o_out[par][:, :], o_ps[:, par, :], scale_rows[:, :], ALU.mult).then_inc(o_ready, 1)

        @block.vector
        def _(dve):
            dve.sem_inc(s_drained, NS)
            dve.sem_inc(pT_lo_ready, 2)
            dve.sem_inc(o_ready, 1)
            dve_query(dve, 0)
            for k in range(NU):
                dve_scores(dve, 0, 0, k)
            dve_query(dve, 1)
            for j in range(LAG):
                dve_turned(dve, 0, 0, j)
            slots(dve, dve_slot)

        def pe_query(pe, n, k0, k1):
            if k0 == 0:
                pe.wait_ge(w_lo_ready, n + 2)
            for k in range(k0, k1):
                last = three_pass(pe, m_ps[:, 0, :], w_hi[:, k, :], w_lo[:, k, :], hT_hi[:, k, :], hT_lo[:, k, :],
                                  k == 0, k == KT - 1)
            if k1 == KT:
                last.then_inc(q_ready, 1)

        def pe_scores(pe, g, n, par, k):
            qt, c0, width = UNITS[k]
            if k == 0:
                pe.wait_ge(q_lo_ready, n + 1)
            if g is not None and qt == 0:
                pe.wait_ge(piece_lo, 2 + 2 * PIECES * g + piece_of(c0 + width) + 1)
            pe.wait_ge(s_drained, NU * n + k + 1)
            q, key = slice(qt * P, (qt + 1) * P), slice(c0, c0 + width)
            three_pass(pe, s_ps[:, (par * NU + k) % NS, 0:width], qT_hi[:, q], qT_lo[:, q],
                       kT_hi[:, key], kT_lo[:, key], True, True).then_inc(s_ready, 1)

        def pe_turn(pe, n, par, j):
            done = piece_of(2 * P * (j + 1)) + 1
            pe.wait_ge(exp_done, QT * PIECES * n + PIECES * (QT - 1) + done)
            pe.wait_ge(pT_lo_ready, PAIRS * n + j + 1)
            for t in range(2):
                at = slice((2 * j + t) * P, (2 * j + t + 1) * P)
                for qt in range(QT):
                    last = pe.transpose(t_ps[:, (par * PAIRS + j) % 2, t, qt * P:(qt + 1) * P],
                                        rows[par][qt][:, at], ident[:, :])
            last.then_inc(turned, 1)

        def pe_values(pe, g, n, par, j):
            if g is not None and (j == 0 or piece_of(2 * P * (j + 1)) > piece_of(2 * P * j)):
                pe.wait_ge(piece_lo, 2 + 2 * PIECES * g + PIECES + piece_of(2 * P * (j + 1)) + 1)
            if j == 0:
                pe.wait_ge(o_ready, n + 1)
            pe.wait_ge(pT_lo_ready, 2 + PAIRS * n + j + 1)
            for t in range(2):
                at = slice((2 * j + t) * P, (2 * j + t + 1) * P)
                last = three_pass(pe, o_ps[:, par, :], v_hi[:, at], v_lo[:, at], pT_hi[j % NPT][:, t, :],
                                  pT_lo[j % NPT][:, t, :], j == 0 and t == 0, j == PAIRS - 1 and t == 1)
            last.then_inc(pv_done, 1)

        def pe_slot(pe, g, n, u, last):
            par = u % 2
            has_next, has_after = flags(u, last)
            for j in range(PAIRS):
                if has_next or j + LAG < PAIRS:
                    pe_turn(pe, *ahead(n, par, j))
                if has_next:
                    for k in UNITS_OF_STEP[j]:
                        pe_scores(pe, g + 1 if u == GROUP - 1 else None, n + 1, 1 - par, k)
                if j == 11:
                    pe.wait_ge(diag_ready, QT * (n + 1))
                    pe.matmul(m_ps[:, 1, :], ones[:, :], diag[:, :], start=True, stop=True).then_inc(spread, 1)
                if has_after and j in Q_STEPS:
                    if j == Q_STEPS[0]:
                        pe.wait_ge(spread_copied, n + 2)
                    k = 2 * (j - Q_STEPS[0])
                    pe_query(pe, n + 2, k, k + 2)
                pe_values(pe, g if u == 0 else None, n, par, j)

        @block.tensor
        def _(pe):
            pe.sem_inc(q_ready, 1)
            pe.sem_inc(pv_done, NPT)
            pe_query(pe, 0, 0, KT)
            for k in range(NU):
                pe_scores(pe, 0, 0, 0, k)
            pe_query(pe, 1, 0, KT)
            for j in range(LAG):
                pe_turn(pe, 0, 0, j)
            slots(pe, pe_slot)


def project_out(nc, name, srcT_dram, w, x_in_sb, x_out_sb, row_scale):
    HP = 2
    STEPS = HEADS // HP
    with ExitStack() as ctx:
        a = Alloc(nc, ctx, name)
        w_raw = [a.sb(f"w_raw{i}", [P, HP, HIDDEN]) for i in range(2)]
        w_hi = [a.sb(f"w_hi{i}", [P, HP, HIDDEN], F32R) for i in range(2)]
        w_lo = [a.sb(f"w_lo{i}", [P, HP, HIDDEN], F32R) for i in range(2)]
        s_raw = [a.sb(f"s_raw{i}", [P, HP, TOK]) for i in range(2)]
        s_hi = [a.sb(f"s_hi{i}", [P, HP, TOK], F32R) for i in range(2)]
        s_lo = [a.sb(f"s_lo{i}", [P, HP, TOK], F32R) for i in range(2)]
        y_ps = a.ps("y_ps", [P, QT, 2, BANK])
        step_in = [a.sem(f"step_in{i}") for i in range(2)]
        hi_ready = a.sem("hi_ready")
        lo_ready = a.sem("lo_ready")
        mm_done = a.sem("mm_done")
        block = ctx.enter_context(nc.Block())

        @block.sync
        def _(sp):
            with sp.Fori(0, STEPS // 2) as i:
                for par in range(2):
                    s = 2 * i + par
                    sp.wait_ge(lo_ready, 2 * s + 2)
                    sp.dma_start(w_raw[par][:, :, :], w[bass.ds(HP * s, HP)].rearrange("h p n -> p h n")).then_inc(step_in[par], 16)
                    sp.dma_start(s_raw[par][:, :, :], srcT_dram[bass.ds(HP * s, HP)].rearrange("h p n -> p h n")).then_inc(step_in[par], 16)

        @block.scalar
        def _(act):
            with act.Fori(0, STEPS // 2) as i:
                for par in range(2):
                    s = 2 * i + par
                    act.wait_ge(step_in[par], 32 * (i + 1))
                    act.wait_ge(mm_done, s + 1)
                    act.activation(w_hi[par][:, :, :], w_raw[par][:, :, :], ACT.Copy).then_inc(hi_ready, 1)
                    act.activation(s_hi[par][:, :, :], s_raw[par][:, :, :], ACT.Copy).then_inc(hi_ready, 1)

        @block.vector
        def _(dve):
            dve.sem_inc(lo_ready, 4)
            with dve.Fori(0, STEPS // 2) as i:
                for par in range(2):
                    s = 2 * i + par
                    dve.wait_ge(hi_ready, 2 * s + 2)
                    dve.tensor_tensor(w_lo[par][:, :, :], w_raw[par][:, :, :], f32(w_hi[par][:, :, :]), ALU.subtract).then_inc(lo_ready, 1)
                    dve.tensor_tensor(s_lo[par][:, :, :], s_raw[par][:, :, :], f32(s_hi[par][:, :, :]), ALU.subtract).then_inc(lo_ready, 1)
            dve.wait_ge(mm_done, 2 + STEPS)
            for t in range(QT):
                y = y_ps[:, t, :, :].rearrange("p a b -> p (a b)")
                if row_scale is None:
                    dve.tensor_tensor(x_out_sb[:, t, :], y, x_in_sb[:, t, :], ALU.add)
                else:
                    dve.scalar_tensor_tensor(out=x_out_sb[:, t, :], in0=y, scalar=row_scale[:, t:t + 1],
                                             in1=x_in_sb[:, t, :], op0=ALU.mult, op1=ALU.add)

        def step(pe, s, par, first, last_step):
            pe.wait_ge(lo_ready, 4 + 2 * s + 2)
            for h in range(HP):
                for t in range(QT):
                    tok = slice(t * P, (t + 1) * P)
                    for b in range(2):
                        col = slice(b * BANK, (b + 1) * BANK)
                        last = three_pass(pe, y_ps[:, t, b, :], s_hi[par][:, h, tok], s_lo[par][:, h, tok],
                                          w_hi[par][:, h, col], w_lo[par][:, h, col],
                                          first and h == 0, last_step and h == HP - 1)
            last.then_inc(mm_done, 1)

        @block.tensor
        def _(pe):
            pe.sem_inc(mm_done, 2)
            step(pe, 0, 0, True, False)
            step(pe, 1, 1, False, False)
            with pe.Fori(1, STEPS // 2 - 1) as i:
                step(pe, 2 * i, 0, False, False)
                step(pe, 2 * i + 1, 1, False, False)
            step(pe, STEPS - 2, 0, False, False)
            step(pe, STEPS - 1, 1, False, True)


HPAIRS = HEADS // 2


def linear_attention(nc, w_qk, w_gv, decay, norm_w, hT_hi, hT_lo, zT_dram, square_sum):
    with ExitStack() as ctx:
        a = Alloc(nc, ctx, "la_")
        raw = [a.sb(f"raw{i}", [P, KT, 4 * D]) for i in range(2)]
        w_hi = [a.sb(f"w_hi{i}", [P, KT, 4 * D], F32R) for i in range(2)]
        w_lo = [a.sb(f"w_lo{i}", [P, KT, 4 * D], F32R) for i in range(2)]
        norm = a.sb("norm", [P, HEADS])
        dec = a.sb("dec", [P, 2, TOK])
        sig_qk = a.sb("sig_qk", [P, 2, 2, TOK])
        qk = a.sb("qk", [P, 2, 2, TOK])
        qk_hi = a.sb("qk_hi", [P, 2, 2, TOK], F32R)
        qk_lo = a.sb("qk_lo", [P, 2, 2, TOK], F32R)
        sig_v = a.sb("sig_v", [P, QT, 2 * D])
        v = a.sb("v", [P, QT, 2 * D])
        v_hi = a.sb("v_hi", [P, QT, 2 * D], F32R)
        v_lo = a.sb("v_lo", [P, QT, 2 * D], F32R)
        gate = a.sb("gate", [P, 2, TOK])
        m = a.sb("m", [P, 2, QT, TOK])
        m_hi = a.sb("m_hi", [P, 2, QT, TOK], F32R)
        m_lo = a.sb("m_lo", [P, 2, QT, TOK], F32R)
        squares = a.sb("squares", [P, 2, TOK])
        z = a.sb("z", [P, 2, TOK])
        qk_ps = a.ps("qk_ps", [P, 2, 2, TOK])
        g_ps = a.ps("g_ps", [P, 2, TOK])
        v_ps = a.ps("v_ps", [P, QT, 2 * D])
        a_ps = a.ps("a_ps", [P, 2, QT, TOK])
        o_ps = a.ps("o_ps", [P, 2, TOK])

        norm_in = a.sem("norm_in")
        w_in = [a.sem(f"w_in{i}") for i in range(2)]
        w_hi_ready = [a.sem(f"w_hi_ready{i}") for i in range(2)]
        w_lo_ready = [a.sem(f"w_lo_ready{i}") for i in range(2)]
        dec_in = a.sem("dec_in")
        qk_ready = a.sem("qk_ready")
        qk_sig = a.sem("qk_sig")
        qk_done = a.sem("qk_done")
        qk_hi_ready = a.sem("qk_hi_ready")
        qk_lo_ready = a.sem("qk_lo_ready")
        g_ready = a.sem("g_ready")
        gate_ready = a.sem("gate_ready")
        v_ready = a.sem("v_ready")
        v_sig = a.sem("v_sig")
        v_done = a.sem("v_done")
        v_hi_ready = a.sem("v_hi_ready")
        v_lo_ready = a.sem("v_lo_ready")
        a_ready = a.sem("a_ready")
        m_ready = a.sem("m_ready")
        m_hi_ready = a.sem("m_hi_ready")
        m_lo_ready = a.sem("m_lo_ready")
        o_ready = a.sem("o_ready")
        sq_ready = a.sem("sq_ready")
        sq_added = a.sem("sq_added")
        z_ready = a.sem("z_ready")
        z_stored = a.sem("z_stored")
        zeroed = a.sem("zeroed")
        block = ctx.enter_context(nc.Block())
        parts = ((0, slice(0, TOK)), (1, slice(P, TOK)))

        def load_weight(sp, part, p):
            w = (w_qk, w_gv)[part]
            sp.dma_start(raw[part][:, :, :], w[bass.ds(p, 1)].rearrange("h p k n -> p (h k) n")).then_inc(w_in[part], 16)

        def load_decay(sp, p):
            sp.dma_start(dec[:, :, :], decay[bass.ds(p, 1)].rearrange("g p h n -> p (g h) n")).then_inc(dec_in, 16)

        def store_z(sp, p):
            sp.wait_ge(z_ready, 2 * p + 4)
            sp.dma_start(zT_dram[bass.ds(2 * p, 2)].rearrange("h p n -> p h n"), z[:, :, :]).then_inc(z_stored, 16)

        @block.sync
        def _(sp):
            sp.sem_inc(z_stored, 16)
            load_weight(sp, 0, 0)
            load_weight(sp, 1, 0)
            sp.dma_start(norm[:, :], norm_w).then_inc(norm_in, 16)
            load_decay(sp, 0)
            for part in range(2):
                sp.wait_ge(w_lo_ready[part], 1)
                load_weight(sp, part, 1)
            with sp.Fori(1, HPAIRS - 1) as p:
                sp.wait_ge(w_lo_ready[0], p + 1)
                load_weight(sp, 0, p + 1)
                sp.wait_ge(m_ready, 4 * p)
                load_decay(sp, p)
                sp.wait_ge(w_lo_ready[1], p + 1)
                load_weight(sp, 1, p + 1)
                store_z(sp, p - 1)
            sp.wait_ge(m_ready, 4 * (HPAIRS - 1))
            load_decay(sp, HPAIRS - 1)
            store_z(sp, HPAIRS - 2)
            store_z(sp, HPAIRS - 1)
            sp.wait_ge(z_stored, 16 * (HPAIRS + 1))

        @block.gpsimd
        def _(pool):
            pool.memset(square_sum[:, :, :], 0.0).then_inc(sq_added, 1)
            for h in range(2):
                pool.memset(f32(m_hi[:, h, 1, 0:P]), 0.0).then_inc(zeroed, 1)
                pool.memset(f32(m_lo[:, h, 1, 0:P]), 0.0).then_inc(zeroed, 1)
            with pool.Fori(0, HPAIRS) as p:
                pool.wait_ge(sq_ready, p + 2)
                pool.wait_ge(sq_added, p + 1)
                pool.tensor_tensor(square_sum[:, :, :], square_sum[:, :, :], squares[:, :, :], ALU.add).then_inc(sq_added, 1)

        def act_split(act, part, p):
            act.wait_ge(w_in[part], 16 * (p + 1))
            act.activation(w_hi[part][:, :, :], raw[part][:, :, :], ACT.Copy).then_inc(w_hi_ready[part], 1)

        def act_qk(act, p):
            for h in range(2):
                act.wait_ge(qk_ready, 2 * p + h + 1)
                act.activation(sig_qk[:, h, :, :], qk_ps[:, h, :, :], ACT.Sigmoid).then_inc(qk_sig, 1)
            for h in range(2):
                act.wait_ge(qk_done, 2 * p + h + 1)
                act.activation(qk_hi[:, h, :, :], qk[:, h, :, :], ACT.Copy).then_inc(qk_hi_ready, 1)

        def act_gate_v(act, p):
            act.wait_ge(z_ready, 2 * p + 2)
            act.wait_ge(g_ready, p + 1)
            act.activation(gate[:, :, :], g_ps[:, :, :], ACT.Sigmoid).then_inc(gate_ready, 1)
            act.wait_ge(v_ready, p + 1)
            act.activation(sig_v[:, :, :], v_ps[:, :, :], ACT.Sigmoid).then_inc(v_sig, 1)
            act.wait_ge(v_done, p + 1)
            act.activation(v_hi[:, :, :], v[:, :, :], ACT.Copy).then_inc(v_hi_ready, 1)

        def act_decayed(act, p):
            for h in range(2):
                act.wait_ge(m_ready, 4 * p + 2 * h + 2)
                for jt, at in parts:
                    act.activation(m_hi[:, h, jt, at], m[:, h, jt, at], ACT.Copy).then_inc(m_hi_ready, 1)

        def act_squares(act, p):
            act.wait_ge(o_ready, p + 1)
            act.wait_ge(sq_added, p + 1)
            act.activation(squares[:, :, :], o_ps[:, :, :], ACT.Square).then_inc(sq_ready, 1)

        def act_pair(act, p, prefetch):
            act_decayed(act, p - 1)
            act.wait_ge(v_ready, p)
            act_split(act, 1, p)
            act_qk(act, p)
            act_squares(act, p - 1)
            if prefetch:
                act.wait_ge(qk_ready, 2 * p + 2)
                act_split(act, 0, p + 1)
            act_gate_v(act, p)

        @block.scalar
        def _(act):
            act_split(act, 0, 0)
            act_split(act, 1, 0)
            act_qk(act, 0)
            act.wait_ge(qk_ready, 2)
            act_split(act, 0, 1)
            act_gate_v(act, 0)
            with act.Fori(1, HPAIRS - 1) as p:
                act_pair(act, p, True)
            act_pair(act, HPAIRS - 1, False)
            act_decayed(act, HPAIRS - 1)
            act_squares(act, HPAIRS - 1)

        def dve_split(dve, part, p):
            dve.wait_ge(w_hi_ready[part], p + 1)
            dve.tensor_tensor(w_lo[part][:, :, :], raw[part][:, :, :], f32(w_hi[part][:, :, :]),
                              ALU.subtract).then_inc(w_lo_ready[part], 1)

        def dve_qk(dve, p):
            for h in range(2):
                dve.wait_ge(qk_sig, 2 * p + h + 1)
                dve.tensor_tensor(qk[:, h, :, :], qk_ps[:, h, :, :], sig_qk[:, h, :, :], ALU.mult).then_inc(qk_done, 1)
            for h in range(2):
                dve.wait_ge(qk_hi_ready, 2 * p + h + 1)
                dve.tensor_tensor(qk_lo[:, h, :, :], qk[:, h, :, :], f32(qk_hi[:, h, :, :]), ALU.subtract).then_inc(qk_lo_ready, 1)

        def dve_v(dve, p):
            dve.wait_ge(v_sig, p + 1)
            dve.tensor_tensor(v[:, :, :], v_ps[:, :, :], sig_v[:, :, :], ALU.mult).then_inc(v_done, 1)
            dve.wait_ge(v_hi_ready, p + 1)
            dve.tensor_tensor(v_lo[:, :, :], v[:, :, :], f32(v_hi[:, :, :]), ALU.subtract).then_inc(v_lo_ready, 1)

        def dve_decayed(dve, p):
            dve.wait_ge(dec_in, 16 * (p + 1))
            for h in range(2):
                dve.wait_ge(a_ready, 2 * p + h + 1)
                for jt, at in parts:
                    dve.tensor_tensor(m[:, h, jt, at], a_ps[:, h, jt, at], dec[:, h, 0:TOK - jt * P], ALU.mult).then_inc(m_ready, 1)
            for h in range(2):
                dve.wait_ge(m_hi_ready, 4 * p + 2 * h + 2)
                for jt, at in parts:
                    dve.tensor_tensor(m_lo[:, h, jt, at], m[:, h, jt, at], f32(m_hi[:, h, jt, at]), ALU.subtract).then_inc(m_lo_ready, 1)

        def dve_z(dve, p):
            dve.wait_ge(sq_ready, p + 2)
            dve.wait_ge(gate_ready, p + 1)
            dve.wait_ge(z_stored, 16 * (p + 1))
            for h in range(2):
                dve.scalar_tensor_tensor(out=z[:, h, :], in0=gate[:, h, :], scalar=norm[:, bass.ds(2 * p + h, 1)],
                                         in1=o_ps[:, h, :], op0=ALU.mult, op1=ALU.mult).then_inc(z_ready, 1)

        def dve_pair(dve, p, prefetch):
            dve_decayed(dve, p - 1)
            dve_split(dve, 1, p)
            dve_qk(dve, p)
            dve_z(dve, p - 1)
            if prefetch:
                dve_split(dve, 0, p + 1)
            dve_v(dve, p)

        @block.vector
        def _(dve):
            dve.sem_inc(z_ready, 2)
            dve.sem_inc(sq_ready, 1)
            dve.wait_ge(norm_in, 16)
            dve_split(dve, 0, 0)
            dve_split(dve, 1, 0)
            dve_qk(dve, 0)
            dve_split(dve, 0, 1)
            dve_v(dve, 0)
            with dve.Fori(1, HPAIRS - 1) as p:
                dve_pair(dve, p, True)
            dve_pair(dve, HPAIRS - 1, False)
            dve_decayed(dve, HPAIRS - 1)
            dve_z(dve, HPAIRS - 1)

        def pe_features(pe, out, part, col):
            for k in range(KT):
                c = slice(col * D, (col + 1) * D)
                last = three_pass(pe, out, w_hi[part][:, k, c], w_lo[part][:, k, c], hT_hi[:, k, :], hT_lo[:, k, :],
                                  k == 0, k == KT - 1)
            return last

        def pe_qk(pe, p, wait=True):
            pe.wait_ge(w_lo_ready[0], p + 1)
            for h in range(2):
                if wait:
                    pe.wait_ge(qk_done, 2 * p + h - 1)
                for part in range(2):
                    last = pe_features(pe, qk_ps[:, h, part, :], 0, 2 * h + part)
                last.then_inc(qk_ready, 1)

        def pe_gate_v(pe, p, wait=True):
            pe.wait_ge(w_lo_ready[1], p + 1)
            if wait:
                pe.wait_ge(gate_ready, p)
            for h in range(2):
                last = pe_features(pe, g_ps[:, h, :], 1, h)
            last.then_inc(g_ready, 1)
            if wait:
                pe.wait_ge(v_done, p)
            for t in range(QT):
                for k in range(KT):
                    tok = slice(t * P, (t + 1) * P)
                    last = three_pass(pe, v_ps[:, t, :], hT_hi[:, k, tok], hT_lo[:, k, tok], w_hi[1][:, k, 2 * D:4 * D],
                                      w_lo[1][:, k, 2 * D:4 * D], k == 0, k == KT - 1)
            last.then_inc(v_ready, 1)

        def pe_scores(pe, p):
            for h in range(2):
                pe.wait_ge(qk_lo_ready, 2 * p + h + 1)
                for jt in range(QT):
                    key = slice(jt * P, (jt + 1) * P)
                    last = three_pass(pe, a_ps[:, h, jt, :], qk_hi[:, h, 1, key], qk_lo[:, h, 1, key],
                                      qk_hi[:, h, 0, :], qk_lo[:, h, 0, :], True, True)
                last.then_inc(a_ready, 1)

        def pe_values(pe, p):
            pe.wait_ge(v_lo_ready, p + 1)
            pe.wait_ge(z_ready, 2 * p + 2)
            pe.wait_ge(sq_ready, p + 1)
            for h in range(2):
                pe.wait_ge(m_lo_ready, 4 * p + 2 * h + 2)
                for jt in range(QT):
                    f = slice(h * D, (h + 1) * D)
                    last = three_pass(pe, o_ps[:, h, :], v_hi[:, jt, f], v_lo[:, jt, f], m_hi[:, h, jt, :],
                                      m_lo[:, h, jt, :], jt == 0, jt == QT - 1)
            last.then_inc(o_ready, 1)

        @block.tensor
        def _(pe):
            pe.wait_ge(zeroed, 4)
            pe_qk(pe, 0, False)
            pe_gate_v(pe, 0, False)
            with pe.Fori(1, HPAIRS) as p:
                pe_scores(pe, p - 1)
                pe_qk(pe, p)
                pe_values(pe, p - 1)
                pe_gate_v(pe, p)
            pe_scores(pe, HPAIRS - 1)
            pe_values(pe, HPAIRS - 1)


def norm_factor(nc, square_sum, ones, row_scale):
    with ExitStack() as ctx:
        a = Alloc(nc, ctx, "nf_")
        ve = a.sb("ve", [P, QT])
        root = a.sb("root", [P, QT])
        t0 = a.sb("t0", [P, QT])
        r0 = a.sb("r0", [P, QT])
        ss = a.ps("ss", [P, QT])
        summed = a.sem("summed")
        small = a.sem("small")
        root_ready = a.sem("root_ready")
        block = ctx.enter_context(nc.Block())

        @block.tensor
        def _(pe):
            for t in range(QT):
                for h in range(2):
                    last = pe.matmul(ss[:, t:t + 1], square_sum[:, h, t * P:(t + 1) * P], ones[:, 0:1],
                                     start=h == 0, stop=h == 1)
            last.then_inc(summed, 1)

        @block.scalar
        def _(act):
            act.wait_ge(small, 1)
            act.activation(root[:, :], ve[:, :], ACT.Sqrt).then_inc(root_ready, 1)

        @block.vector
        def _(dve):
            dve.wait_ge(summed, 1)
            dve.tensor_scalar(ve[:, :], ss[:, :], 1.0 / (HEADS * D), EPS, ALU.mult, ALU.add).then_inc(small, 1)
            dve.wait_ge(root_ready, 1)
            dve.reciprocal(r0[:, :], root[:, :]).then_inc(small, 1)
            dve.wait_ge(small, 2)
            dve.tensor_tensor(t0[:, :], r0[:, :], r0[:, :], ALU.mult).then_inc(small, 1)
            dve.wait_ge(small, 3)
            dve.tensor_tensor(t0[:, :], t0[:, :], ve[:, :], ALU.mult).then_inc(small, 1)
            dve.wait_ge(small, 4)
            dve.tensor_scalar(t0[:, :], t0[:, :], -0.5, 1.5, ALU.mult, ALU.add).then_inc(small, 1)
            dve.wait_ge(small, 5)
            dve.tensor_tensor(row_scale[:, :], r0[:, :], t0[:, :], ALU.mult)


def lora_mixture(nc, w_router_a, w_b, hT, ident, x_sb, out):
    LORA_SCALE = 16.0 / float(np.sqrt(16.0))
    with ExitStack() as ctx:
        a = Alloc(nc, ctx, "mix_")
        wra = a.sb("wra", [P, KT, EXPERTS + ER])
        wb = a.sb("wb", [ER, HIDDEN])
        lm = a.sb("lm", [P, QT, EXPERTS + ER])
        beaten = a.sb("beaten", [P, QT, EXPERTS, EXPERTS])
        rank = a.sb("rank", [P, QT, EXPERTS])
        chosen = a.sb("chosen", [P, QT, EXPERTS])
        neg_max = a.sb("neg_max", [P, QT])
        e = a.sb("e", [P, QT, EXPERTS])
        ec = a.sb("ec", [P, QT, EXPERTS])
        total = a.sb("total", [P, QT])
        inverse = a.sb("inverse", [P, QT])
        gates = a.sb("gates", [P, QT, EXPERTS])
        gm = a.sb("gm", [P, QT, ER])
        gmT = a.sb("gmT", [ER, TOK])
        res = a.sb("res", [P, QT, HIDDEN])
        lm_ps = a.ps("lm_ps", [P, QT, BANK])
        gmT_ps = a.ps("gmT_ps", [ER, TOK])
        y_ps = a.ps("y_ps", [P, QT, 2, BANK])
        w_in = a.sem("w_in")
        lm_ready = a.sem("lm_ready")
        lm_copied = a.sem("lm_copied")
        small = a.sem("small")
        exp_ready = a.sem("exp_ready")
        gm_ready = a.sem("gm_ready")
        turned = a.sem("turned")
        gmT_ready = a.sem("gmT_ready")
        y_ready = a.sem("y_ready")
        res_ready = a.sem("res_ready")
        stored = a.sem("stored")
        block = ctx.enter_context(nc.Block())

        @block.sync
        def _(sp):
            sp.dma_start(wra[:, :, :], w_router_a).then_inc(w_in, 16)
            sp.dma_start(wb[:, :], w_b).then_inc(w_in, 16)
            for t in range(QT):
                sp.wait_ge(res_ready, t + 1)
                sp.dma_start(out[t], res[:, t, :]).then_inc(stored, 16)
            sp.wait_ge(stored, 16 * QT)

        @block.tensor
        def _(pe):
            pe.wait_ge(w_in, 32)
            for t in range(QT):
                for k in range(KT):
                    last = pe.matmul(lm_ps[:, t, 0:EXPERTS + ER], hT[:, k, t * P:(t + 1) * P], wra[:, k, :],
                                     start=k == 0, stop=k == KT - 1)
            last.then_inc(lm_ready, 1)
            pe.wait_ge(gm_ready, QT * EXPERTS)
            for t in range(QT):
                last = pe.transpose(gmT_ps[:, t * P:(t + 1) * P], gm[:, t, :], ident[:, :])
            last.then_inc(turned, 1)
            pe.wait_ge(gmT_ready, 1)
            for t in range(QT):
                for b in range(2):
                    last = pe.matmul(y_ps[:, t, b, :], gmT[:, t * P:(t + 1) * P], wb[:, b * BANK:(b + 1) * BANK],
                                     start=True, stop=True)
                last.then_inc(y_ready, 1)

        @block.scalar
        def _(act):
            act.wait_ge(small, 1)
            for t in range(QT):
                act.activation(e[:, t, :], lm[:, t, 0:EXPERTS], ACT.Exp, bias=neg_max[:, t:t + 1]).then_inc(exp_ready, 1)
            act.wait_ge(turned, 1)
            act.activation(gmT[:, :], gmT_ps[:, :], ACT.Copy).then_inc(gmT_ready, 1)

        @block.vector
        def _(dve):
            dve.memset(beaten[:, :, :, :], 0.0).then_inc(lm_copied, 1)
            dve.wait_ge(lm_ready, 1)
            dve.tensor_copy(lm[:, :, :], lm_ps[:, :, 0:EXPERTS + ER]).then_inc(lm_copied, 1)
            dve.wait_ge(lm_copied, 2)
            dve.tensor_reduce(neg_max[:, :], lm[:, :, 0:EXPERTS], AX.X, ALU.max, negate=True).then_inc(small, 1)
            count = 1
            for t in range(QT):
                for j in range(EXPERTS):
                    for rows, op in ((slice(j + 1, EXPERTS), ALU.is_le), (slice(0, j), ALU.is_lt)):
                        if rows.start < rows.stop:
                            dve.tensor_scalar(beaten[:, t, rows, j], lm[:, t, rows], lm[:, t, j:j + 1], None, op).then_inc(small, 1)
                            count += 1
            dve.wait_ge(small, count)
            dve.tensor_reduce(rank[:, :, :], beaten[:, :, :, :], AX.X, ALU.add).then_inc(small, 1)
            dve.wait_ge(small, count + 1)
            dve.tensor_scalar(chosen[:, :, :], rank[:, :, :], 2.0, None, ALU.is_lt).then_inc(small, 1)
            dve.wait_ge(small, count + 2)
            dve.wait_ge(exp_ready, QT)
            dve.tensor_tensor(ec[:, :, :], e[:, :, :], chosen[:, :, :], ALU.mult).then_inc(small, 1)
            dve.wait_ge(small, count + 3)
            dve.tensor_reduce(total[:, :], ec[:, :, :], AX.X, ALU.add).then_inc(small, 1)
            dve.wait_ge(small, count + 4)
            dve.reciprocal(inverse[:, :], total[:, :]).then_inc(small, 1)
            dve.wait_ge(small, count + 5)
            for t in range(QT):
                dve.tensor_scalar(gates[:, t, :], ec[:, t, :], inverse[:, t:t + 1], LORA_SCALE,
                                  ALU.mult, ALU.mult).then_inc(small, 1)
            dve.wait_ge(small, count + 5 + QT)
            for t in range(QT):
                for x in range(EXPERTS):
                    r = slice(x * LORA, (x + 1) * LORA)
                    dve.tensor_scalar(gm[:, t, r], lm[:, t, EXPERTS + r.start:EXPERTS + r.stop], gates[:, t, x:x + 1],
                                      None, ALU.mult).then_inc(gm_ready, 1)
            for t in range(QT):
                dve.wait_ge(y_ready, t + 1)
                dve.tensor_tensor(res[:, t, :], y_ps[:, t, :, :].rearrange("p a b -> p (a b)"), x_sb[:, t, :],
                                  ALU.add).then_inc(res_ready, 1)


def perceiver_layer(nc, x, ctxT, wk, wv, wq, wo, w_qk, w_gv, decay, norm_w, w_out, w_router_a, w_b, out):
    kT_dram = nc.dram_tensor("kT_scratch", (KVH, D, KV), F32, kind="Internal").ap()
    v_dram = nc.dram_tensor("v_scratch", (KVH, P, KVT, D), F32, kind="Internal").ap()
    oT_dram = nc.dram_tensor("oT_scratch", (HEADS, D, TOK), F32, kind="Internal").ap()
    zT_dram = nc.dram_tensor("zT_scratch", (HEADS, D, TOK), F32, kind="Internal").ap()
    with ExitStack() as ctx:
        a = Alloc(nc, ctx, "")
        ident = a.sb("ident", [P, P])
        ones = a.sb("ones", [P, P])
        x_sb = a.sb("x_sb", [P, QT, HIDDEN])
        zero_done = a.sem("zero_done")
        with ExitStack() as setup, nc.Block() as block:
            @block.gpsimd
            def _(pool):
                pool.memset(ones[:, :], 1.0)
                pool.memset(ident[:, :], 0.0).then_inc(zero_done, 1)
                pool.wait_ge(zero_done, 1)
                pool.affine_select(out=ident[:, :], in_=ident[:, :], compare_op=ALU.not_equal, fill=1.0, base=0,
                                   pattern=[[-1, P]], channel_multiplier=1)
        with ExitStack() as inner:
            b = Alloc(nc, inner, "x_")
            hT_hi = b.sb("hT_hi", [P, KT, TOK], F32R)
            hT_lo = b.sb("hT_lo", [P, KT, TOK], F32R)
            layernorm_and_turn(nc, "ln1_", x_sb, hT_hi, hT_lo, ident, x_dram=x)
            project_keys_values(nc, ctxT, wk, wv, hT_hi, hT_lo, kT_dram, v_dram)
            cross_attention(nc, wq, kT_dram, v_dram, hT_hi, hT_lo, ident, ones, oT_dram)
        project_out(nc, "wo_", oT_dram, wo, x_sb, x_sb, None)
        square_sum = a.sb("square_sum", [P, 2, TOK])
        row_scale = a.sb("row_scale", [P, QT])
        with ExitStack() as inner:
            b = Alloc(nc, inner, "l_")
            hT_hi = b.sb("hT_hi", [P, KT, TOK], F32R)
            hT_lo = b.sb("hT_lo", [P, KT, TOK], F32R)
            layernorm_and_turn(nc, "ln2_", x_sb, hT_hi, hT_lo, ident)
            linear_attention(nc, w_qk, w_gv, decay, norm_w, hT_hi, hT_lo, zT_dram, square_sum)
        norm_factor(nc, square_sum, ones, row_scale)
        project_out(nc, "lo_", zT_dram, w_out, x_sb, x_sb, row_scale)
        with ExitStack() as inner:
            b = Alloc(nc, inner, "m_")
            hT = b.sb("hT", [P, KT, TOK])
            layernorm_and_turn(nc, "ln3_", x_sb, hT, None, ident)
            lora_mixture(nc, w_router_a, w_b, hT, ident, x_sb, out)


def decay_table():
    layer, layers = 1, 32
    factor = 1.0 - layer / (layers - 1 + 1e-05) + 1e-05
    slope = (2.0 ** (-8.0 / HEADS)) ** (np.arange(HEADS) + 1.0) * factor
    dist = np.arange(TOK)[None, :] - np.arange(P)[:, None]
    table = np.where(dist >= 0, np.exp(-slope[:, None, None] * np.maximum(dist, 0)), 0.0)
    return np.ascontiguousarray(table.reshape(HPAIRS, 2, P, TOK).transpose(0, 2, 1, 3)).astype(np.float32)


def kernel(x, ctx_4096, L0_xattn_Wq, L0_xattn_Wk, L0_xattn_Wv, L0_xattn_Wo, L0_attn_qkv_w, L0_attn_out_w,
           L0_attn_gate_w, L0_attn_norm_w, L0_ffn_A, L0_ffn_B, L0_ffn_Wr):
    import concourse.bacc as bacc
    from concourse.bass_utils import run_bass_kernel_spmd

    def turned(w):
        return np.asarray(w).T.reshape(KT, P, -1).transpose(1, 0, 2)

    qkv = turned(L0_attn_qkv_w).reshape(P, KT, HPAIRS, 2, 3, D)
    gate = turned(L0_attn_gate_w).reshape(P, KT, HPAIRS, 2, D)
    w_gv = np.stack([gate, qkv[:, :, :, :, 2]], axis=3)
    data = {
        "x": np.asarray(x).reshape(QT, P, HIDDEN).transpose(1, 0, 2),
        "ctxT": np.asarray(ctx_4096).reshape(NCHUNK, CCHUNK, KT, P).transpose(0, 3, 2, 1),
        "wk": np.asarray(L0_xattn_Wk).reshape(KT, P, KVH * D).transpose(1, 0, 2),
        "wv": np.asarray(L0_xattn_Wv).reshape(KT, P, KVH * D).transpose(1, 0, 2),
        "wq": np.asarray(L0_xattn_Wq).reshape(KT, P, HEADS, D).transpose(2, 1, 0, 3),
        "wo": np.asarray(L0_xattn_Wo).reshape(HEADS, D, HIDDEN),
        "w_qk": qkv[:, :, :, :, 0:2].transpose(2, 0, 1, 3, 4, 5).reshape(HPAIRS, P, KT, 4 * D),
        "w_gv": w_gv.transpose(2, 0, 1, 3, 4, 5).reshape(HPAIRS, P, KT, 4 * D),
        "decay": decay_table(),
        "norm_w": np.asarray(L0_attn_norm_w).reshape(HEADS, D).T,
        "w_out": np.asarray(L0_attn_out_w).T.reshape(HEADS, D, HIDDEN),
        "w_router_a": np.concatenate([turned(L0_ffn_Wr), turned(np.asarray(L0_ffn_A).reshape(ER, HIDDEN))], axis=2),
        "w_b": np.asarray(L0_ffn_B).transpose(0, 2, 1).reshape(ER, HIDDEN),
    }
    nc = bacc.Bacc("TRN2", target_bir_lowering=False, num_devices=1)
    arrays, args = {}, []
    for name, value in data.items():
        value = np.ascontiguousarray(value)
        arrays[f"in_{name}"] = value
        args.append(nc.dram_tensor(f"in_{name}", value.shape, mybir.dt.from_np(value.dtype), kind="ExternalInput").ap())
    out = nc.dram_tensor("out", (QT, P, HIDDEN), F32, kind="ExternalOutput").ap()
    perceiver_layer(nc, *args, out)
    result = run_bass_kernel_spmd(nc, [arrays], core_ids=[0])
    return result.results[0]["out"].reshape(1, TOK, HIDDEN)
```

```python
from contextlib import ExitStack

import numpy as np

import concourse.bass as bass
from concourse import mybir

F32 = mybir.dt.float32
F32R = mybir.dt.float32r
ALU = mybir.AluOpType
ACT = mybir.ActivationFunctionType
AX = mybir.AxisListType

P = 128
HIDDEN = 1024
KT = HIDDEN // P
TOK = 256
QT = TOK // P
CTX = 4096
KV = CTX + TOK
KVT = KV // P
HEADS = 32
D = 128
KVH = 4
GROUP = HEADS // KVH
SCALE = 1.0 / float(np.sqrt(D))
EPS = 1e-5
BANK = 512
CCHUNK = 512
NCHUNK = CTX // CCHUNK
EXPERTS = 4
PIECES = 4
PIECE = KV // PIECES
FIRST = 3
LORA = 16
ER = EXPERTS * LORA


class Alloc:

    def __init__(self, nc, ctx, prefix):
        self.nc, self.ctx, self.prefix = nc, ctx, prefix

    def sb(self, name, shape, dt=F32):
        return self.ctx.enter_context(self.nc.sbuf_tensor(self.prefix + name, shape, dt))

    def ps(self, name, shape, dt=F32):
        return self.ctx.enter_context(self.nc.psum_tensor(self.prefix + name, shape, dt))

    def sem(self, name):
        return self.ctx.enter_context(self.nc.semaphore(self.prefix + name))


def f32(ap):
    return ap.bitcast(F32)


def carve(region, col, *shape):
    names = "abcd"[:len(shape)]
    return region[:, col:col + int(np.prod(shape))].rearrange(
        f"p ({' '.join(names)}) -> p {' '.join(names)}", **dict(zip(names, shape)))


class Shared:

    def __init__(self, a):
        self.r = [a.sb(f"split{i}", [P, KV], F32R) for i in range(2)]
        self.f = a.sb("full", [P, KV])
        self.stage = a.sb("stage", [P, 2 * PIECE])
        self.out = a.sb("head_out", [P, 2, TOK])
        self.last_keys = carve(self.f, 0, KVH, TOK)
        self.k_stored = a.sem("k_stored")
        self.v_stored = a.sem("v_stored")
        self.first_keys = [region[:, 0:FIRST * PIECE] for region in self.r]
        self.first_weight = [carve(region, FIRST * PIECE, KT, D) for region in self.r]


def three_pass(pe, out, w_hi, w_lo, m_hi, m_lo, first, last):
    pe.matmul(out, w_hi, m_hi, start=first, stop=False)
    pe.matmul(out, w_hi, m_lo, start=False, stop=False)
    return pe.matmul(out, w_lo, m_hi, start=False, stop=last)


def keep_clock(pe, out, w, m, count):
    for _ in range(count):
        pe.matmul(out, w, m, start=True, stop=True)


class LayerNorm:

    def __init__(self, a, x_sb, h, turned, hT_hi, hT_lo, ident):
        self.x_sb, self.h, self.turned = x_sb, h, turned
        self.hT_hi, self.hT_lo, self.ident = hT_hi, hT_lo, ident
        self.stats = a.sb("ln_stats", [P, QT, 2, 6])
        self.mv = a.sb("ln_mv", [P, QT, 2])
        self.ve = a.sb("ln_ve", [P, QT])
        self.root = a.sb("ln_root", [P, QT])
        self.r0 = a.sb("ln_r0", [P, QT])
        self.t0 = a.sb("ln_t0", [P, QT])
        self.rstd = a.sb("ln_rstd", [P, QT])
        self.small = [a.sem(f"ln_small{t}") for t in range(QT)]
        self.root_ready = a.sem("ln_root_ready")
        self.h_ready = a.sem("ln_h_ready")
        self.turned_ready = a.sem("ln_turned_ready")
        self.hi_ready = a.sem("ln_hi_ready")
        self.lo_ready = a.sem("ln_lo_ready")

    def dve_stats(self, dve, t, half):
        dve.bn_stats(self.stats[:, t, half, :], self.x_sb[:, t, half * 512:(half + 1) * 512]).then_inc(self.small[t], 1)

    def dve_variance(self, dve, t):
        one = slice(t, t + 1)
        dve.wait_ge(self.small[t], 2)
        dve.bn_aggr(self.mv[:, t, :], self.stats[:, t, :, :].rearrange("p a b -> p (a b)")).then_inc(self.small[t], 1)
        dve.wait_ge(self.small[t], 3)
        dve.tensor_scalar(self.ve[:, one], self.mv[:, t, 1:2], EPS, None, ALU.add).then_inc(self.small[t], 1)

    def dve_rows(self, dve, t):
        one = slice(t, t + 1)
        dve.wait_ge(self.root_ready, t + 1)
        dve.reciprocal(self.r0[:, one], self.root[:, one]).then_inc(self.small[t], 1)
        dve.wait_ge(self.small[t], 5)
        dve.tensor_tensor(self.t0[:, one], self.r0[:, one], self.r0[:, one], ALU.mult).then_inc(self.small[t], 1)
        dve.wait_ge(self.small[t], 6)
        dve.tensor_tensor(self.t0[:, one], self.t0[:, one], self.ve[:, one], ALU.mult).then_inc(self.small[t], 1)
        dve.wait_ge(self.small[t], 7)
        dve.tensor_scalar(self.t0[:, one], self.t0[:, one], -0.5, 1.5, ALU.mult, ALU.add).then_inc(self.small[t], 1)
        dve.wait_ge(self.small[t], 8)
        dve.tensor_tensor(self.rstd[:, one], self.r0[:, one], self.t0[:, one], ALU.mult).then_inc(self.small[t], 1)
        dve.wait_ge(self.small[t], 9)
        dve.tensor_scalar(self.h[:, t, :], self.x_sb[:, t, :], self.mv[:, t, 0:1], self.rstd[:, one],
                          ALU.subtract, ALU.mult).then_inc(self.h_ready, 1)

    def act_root(self, act, t):
        act.wait_ge(self.small[t], 4)
        act.activation(self.root[:, t:t + 1], self.ve[:, t:t + 1], ACT.Sqrt).then_inc(self.root_ready, 1)

    def pe_turn(self, pe, t):
        pe.wait_ge(self.h_ready, t + 1)
        for k in range(KT):
            last = pe.transpose(self.turned[:, k, t * P:(t + 1) * P], self.h[:, t, k * P:(k + 1) * P], self.ident[:, :])
            if t == QT - 1 and k % 2:
                last.then_inc(self.turned_ready, 1)

    def act_hi(self, act):
        for b in range(KT // 2):
            act.wait_ge(self.turned_ready, b + 1)
            act.activation(self.hT_hi[:, 2 * b:2 * b + 2, :], self.turned[:, 2 * b:2 * b + 2, :],
                           ACT.Copy).then_inc(self.hi_ready, 1)

    def dve_lo(self, dve):
        for b in range(KT // 2):
            dve.wait_ge(self.hi_ready, b + 1)
            dve.tensor_tensor(self.hT_lo[:, 2 * b:2 * b + 2, :], self.turned[:, 2 * b:2 * b + 2, :],
                              f32(self.hT_hi[:, 2 * b:2 * b + 2, :]), ALU.subtract).then_inc(self.lo_ready, 1)


def project_keys_values(nc, x, ctxT, wk, wv, wq, x_sb, hT_hi, hT_lo, ident, kT_dram, v_dram, shared):
    with ExitStack() as ctx:
        a = Alloc(nc, ctx, "kv_")
        w_raw = a.sb("w_raw", [P, KT, KVH * D])
        wk_hi = a.sb("wk_hi", [P, KT, KVH * D], F32R)
        wk_lo = a.sb("wk_lo", [P, KT, KVH * D], F32R)
        wv_hi = a.sb("wv_hi", [P, KT, KVH * D], F32R)
        wv_lo = a.sb("wv_lo", [P, KT, KVH * D], F32R)
        c_raw = carve(shared.f, 0, KT, CCHUNK)
        c_hi = [carve(shared.r[0], 0, KT, CCHUNK), a.sb("c_hi1", [P, KT, CCHUNK], F32R)]
        c_lo = [carve(shared.r[1], 0, KT, CCHUNK), a.sb("c_lo1", [P, KT, CCHUNK], F32R)]
        k_out = a.sb("k_out", [P, KVH, CCHUNK])
        v_out = carve(shared.stage, 0, KVH, CCHUNK // P, D)
        k_ps = a.ps("k_ps", [P, KVH, BANK])
        v_ps = a.ps("v_ps", [P, CCHUNK // P, BANK])
        ln = LayerNorm(a, x_sb, w_raw[:, 0:2 * QT, :].rearrange("p (t a) b -> p t (a b)", a=2),
                       k_ps[:, :, :].rearrange("p g (a n) -> p (g a) n", n=TOK), hT_hi, hT_lo, ident)
        x_in = a.sem("x_in")
        tile_in = [a.sem(f"tile_in{k}") for k in range(KT)]
        w_hi_ready = a.sem("w_hi_ready")
        w_lo_ready = a.sem("w_lo_ready")
        c0_hi_ready = a.sem("c0_hi_ready")
        c0_lo_ready = a.sem("c0_lo_ready")
        c_in = a.sem("c_in")
        c_hi_ready = a.sem("c_hi_ready")
        c_lo_ready = a.sem("c_lo_ready")
        k_ready = a.sem("k_ready")
        v_ready = a.sem("v_ready")
        k_copied = a.sem("k_copied")
        v_copied = a.sem("v_copied")
        first_in = a.sem("first_in")
        first_hi_ready = a.sem("first_hi_ready")
        first_lo_ready = a.sem("first_lo_ready")
        first_raw = (carve(shared.f, 0, KT, D), shared.f[:, KT * D:KT * D + FIRST * PIECE])
        first_split = list(zip(shared.first_weight, shared.first_keys))
        k_stored, v_stored = shared.k_stored, shared.v_stored
        VT = CCHUNK // P
        block = ctx.enter_context(nc.Block())

        def load(sp, c):
            sp.dma_start(c_raw[:, :, :], ctxT[bass.ds(c, 1)].rearrange("c p k n -> p (c k) n")).then_inc(c_in, 16)

        def store(sp, c, tiles, k_out):
            n = tiles * P
            sp.wait_ge(k_copied, KVH + KVH * (c + 1))
            sp.dma_start(kT_dram[:, :, bass.ds(c * CCHUNK, n)].rearrange("g p n -> p g n"),
                         k_out[:, :, 0:n]).then_inc(k_stored, 16)
            sp.wait_ge(v_copied, VT * (c + 1) + tiles)
            sp.dma_start(v_dram[:, :, bass.ds(c * VT, tiles), :].rearrange("g p t d -> p g t d"),
                         v_out[:, :, 0:tiles, :]).then_inc(v_stored, 16)

        @block.sync
        def _(sp):
            sp.sem_inc(k_stored, 16)
            sp.sem_inc(v_stored, 16)
            for k in range(KT):
                sp.dma_start(w_raw[:, k, :], wk[:, k, :]).then_inc(tile_in[k], 16)
                sp.dma_start(c_raw[:, k, :], ctxT[0, :, k, :]).then_inc(tile_in[k], 16)
            for k in range(KT):
                sp.wait_ge(w_lo_ready, k + 1)
                sp.dma_start(w_raw[:, k, :], wv[:, k, :]).then_inc(tile_in[k], 16)
            sp.wait_ge(c0_lo_ready, KT)
            load(sp, 1)
            sp.dma_start(x_sb[:, :, :], x).then_inc(x_in, 16)
            with sp.Fori(0, NCHUNK - 2) as c:
                sp.wait_ge(c_lo_ready, c + 1)
                load(sp, c + 2)
                store(sp, c, VT, k_out)
            store(sp, NCHUNK - 2, VT, k_out)
            sp.wait_ge(c_lo_ready, NCHUNK - 1)
            sp.dma_start(first_raw[0], wq[0]).then_inc(first_in, 16)
            sp.wait_ge(first_in, 16)
            sp.wait_ge(k_stored, 16 * NCHUNK)
            sp.dma_start(first_raw[1], kT_dram[0, :, 0:FIRST * PIECE]).then_inc(first_in, 16)
            store(sp, NCHUNK - 1, VT, k_out)
            store(sp, NCHUNK, QT, shared.last_keys)

        def copy_keys(act, c, n, k_out=k_out):
            for g in range(KVH):
                act.wait_ge(k_ready, KVH * c + g + 1)
                act.activation(k_out[:, g, 0:n], k_ps[:, g, 0:n], ACT.Copy).then_inc(k_copied, 1)

        def next_hi(act, c, par):
            act.wait_ge(c_in, 16 * (c + 1))
            act.wait_ge(v_ready, VT * c)
            act.activation(c_hi[par][:, :, :], c_raw[:, :, :], ACT.Copy).then_inc(c_hi_ready, 1)

        @block.scalar
        def _(act):
            act.sem_inc(k_copied, KVH)
            for k in range(KT):
                act.wait_ge(tile_in[k], 32)
                act.activation(wk_hi[:, k, :], w_raw[:, k, :], ACT.Copy).then_inc(w_hi_ready, 1)
                act.activation(c_hi[0][:, k, :], c_raw[:, k, :], ACT.Copy).then_inc(c0_hi_ready, 1)
            for k in range(KT):
                act.wait_ge(tile_in[k], 48)
                act.activation(wv_hi[:, k, :], w_raw[:, k, :], ACT.Copy).then_inc(w_hi_ready, 1)
            act.wait_ge(c_in, 16)
            act.activation(c_hi[1][:, :, :], c_raw[:, :, :], ACT.Copy).then_inc(c_hi_ready, 1)
            copy_keys(act, 0, CCHUNK)
            for t in range(QT):
                ln.act_root(act, t)
            with act.Fori(0, NCHUNK // 2 - 1) as i:
                for par in range(2):
                    c = 2 * i + 1 + par
                    next_hi(act, c, par)
                    act.wait_ge(k_stored, 16 * (c + 1))
                    copy_keys(act, c, CCHUNK)
            act.wait_ge(k_stored, 16 * NCHUNK)
            copy_keys(act, NCHUNK - 1, CCHUNK)
            ln.act_hi(act)
            act.wait_ge(v_ready, VT * (NCHUNK - 1))
            for i in range(2):
                act.wait_ge(first_in, 16 * (i + 1))
                act.activation(first_split[0][i], first_raw[i], ACT.Copy).then_inc(first_hi_ready, 1)
            act.wait_ge(first_lo_ready, 2)
            copy_keys(act, NCHUNK, TOK, shared.last_keys)

        @block.gpsimd
        def _(pool):
            for i in range(2):
                pool.wait_ge(first_hi_ready, i + 1)
                pool.tensor_tensor(first_split[1][i], first_raw[i], f32(first_split[0][i]),
                                   ALU.subtract).then_inc(first_lo_ready, 1)

        def copy_values(dve, c, tiles):
            dve.wait_ge(v_stored, 16 * (c + 1))
            for t in range(tiles):
                dve.wait_ge(v_ready, VT * c + t + 1)
                dve.tensor_copy(v_out[:, :, t, :], v_ps[:, t, :].rearrange("p (g d) -> p g d", d=D)).then_inc(v_copied, 1)

        def split_low(dve, c, par):
            dve.wait_ge(c_hi_ready, c)
            dve.tensor_tensor(c_lo[par][:, :, :], c_raw[:, :, :], f32(c_hi[par][:, :, :]),
                              ALU.subtract).then_inc(c_lo_ready, 1)

        @block.vector
        def _(dve):
            dve.sem_inc(v_copied, VT)
            for k in range(KT):
                dve.wait_ge(w_hi_ready, k + 1)
                dve.tensor_tensor(wk_lo[:, k, :], w_raw[:, k, :], f32(wk_hi[:, k, :]), ALU.subtract).then_inc(w_lo_ready, 1)
                dve.wait_ge(c0_hi_ready, k + 1)
                dve.tensor_tensor(c_lo[0][:, k, :], c_raw[:, k, :], f32(c_hi[0][:, k, :]), ALU.subtract).then_inc(c0_lo_ready, 1)
            for k in range(KT):
                dve.wait_ge(w_hi_ready, KT + k + 1)
                dve.tensor_tensor(wv_lo[:, k, :], w_raw[:, k, :], f32(wv_hi[:, k, :]), ALU.subtract).then_inc(w_lo_ready, 1)
            split_low(dve, 1, 1)
            dve.wait_ge(x_in, 16)
            dve.wait_ge(w_lo_ready, 2 * KT)
            for t in range(QT):
                for half in range(2):
                    ln.dve_stats(dve, t, half)
                ln.dve_variance(dve, t)
                ln.dve_rows(dve, t)
            copy_values(dve, 0, VT)
            with dve.Fori(0, NCHUNK // 2 - 1) as i:
                for par in range(2):
                    c = 2 * i + 1 + par
                    split_low(dve, c + 1, par)
                    copy_values(dve, c, VT)
            ln.dve_lo(dve)
            copy_values(dve, NCHUNK - 1, VT)
            copy_values(dve, NCHUNK, QT)

        def keys(pe, c, hi, lo, n):
            for g in range(KVH):
                pe.wait_ge(k_copied, KVH * c + g + 1)
                for k in range(KT):
                    w = slice(g * D, (g + 1) * D)
                    last = three_pass(pe, k_ps[:, g, 0:n], wk_hi[:, k, w], wk_lo[:, k, w],
                                      hi[:, k, 0:n], lo[:, k, 0:n], k == 0, k == KT - 1)
                last.then_inc(k_ready, 1)

        def values(pe, c, hi, lo, tiles, t0=0):
            for t in range(t0, tiles):
                pe.wait_ge(v_copied, VT * c + t + 1)
                for k in range(KT):
                    s = slice(t * P, (t + 1) * P)
                    last = three_pass(pe, v_ps[:, t, :], hi[:, k, s], lo[:, k, s],
                                      wv_hi[:, k, :], wv_lo[:, k, :], k == 0, k == KT - 1)
                last.then_inc(v_ready, 1)

        @block.tensor
        def _(pe):
            for k in range(KT):
                pe.wait_ge(c0_lo_ready, k + 1)
                pe.wait_ge(w_lo_ready, k + 1)
                for g in range(KVH):
                    w = slice(g * D, (g + 1) * D)
                    last = three_pass(pe, k_ps[:, g, :], wk_hi[:, k, w], wk_lo[:, k, w],
                                      c_hi[0][:, k, :], c_lo[0][:, k, :], k == 0, k == KT - 1)
                    if k == KT - 1:
                        last.then_inc(k_ready, 1)
            pe.wait_ge(w_lo_ready, 2 * KT)
            values(pe, 0, c_hi[0], c_lo[0], VT)
            with pe.Fori(0, NCHUNK // 2 - 1) as i:
                for par in range(2):
                    c = 2 * i + 1 + par
                    pe.wait_ge(c_lo_ready, c)
                    keys(pe, c, c_hi[1 - par], c_lo[1 - par], CCHUNK)
                    values(pe, c, c_hi[1 - par], c_lo[1 - par], VT)
            pe.wait_ge(c_lo_ready, NCHUNK - 1)
            keys(pe, NCHUNK - 1, c_hi[1], c_lo[1], CCHUNK)
            values(pe, NCHUNK - 1, c_hi[1], c_lo[1], 1)
            pe.wait_ge(k_copied, KVH * (NCHUNK + 1))
            for t in range(QT):
                ln.pe_turn(pe, t)
            values(pe, NCHUNK - 1, c_hi[1], c_lo[1], VT, 1)
            pe.wait_ge(ln.lo_ready, KT // 2)
            keys(pe, NCHUNK, hT_hi, hT_lo, TOK)
            values(pe, NCHUNK, hT_hi, hT_lo, QT)


PAIRS = KVT // 2
UNITS = [(qt, c0, min(BANK, KV - c0)) for qt in range(QT) for c0 in range(0, KV, BANK)]
NU = len(UNITS)
UPR = NU // QT
NS = 4
NPT = 3
LAG = 2
S_LAST = 11
DOUBLE = NU - 1 - S_LAST
UNITS_OF_STEP = [range(2 * j, 2 * j + 2) if j < DOUBLE else range(j + DOUBLE, j + DOUBLE + 1) if j <= S_LAST
                 else range(0) for j in range(PAIRS)]
Q_STEPS = range(S_LAST + 1, PAIRS - 1)


def piece_of(end):
    return (end - 1) // PIECE


def cross_attention(nc, wq, kT_dram, v_dram, hT_hi, hT_lo, ident, oT_dram, shared, proj):
    with ExitStack() as ctx:
        a = Alloc(nc, ctx, "xa_")
        v_hi = a.sb("v_hi", [P, KV], F32R)
        v_lo = a.sb("v_lo", [P, KV], F32R)
        kT_hi, kT_lo = shared.r
        rows = [[shared.f if (i, t) == (0, 0) else a.sb(f"rows{i}{t}", [P, KV]) for t in range(QT)] for i in range(2)]
        stage = [shared.stage[:, i * PIECE:(i + 1) * PIECE] for i in range(2)]
        w_raw = a.sb("w_raw", [P, KT, D])
        w_hi = a.sb("w_hi", [P, KT, D], F32R)
        w_lo = a.sb("w_lo", [P, KT, D], F32R)
        qT_hi = a.sb("qT_hi", [P, TOK], F32R)
        qT_lo = a.sb("qT_lo", [P, TOK], F32R)
        pT_hi = [a.sb(f"pT_hi{i}", [P, 2, TOK], F32R) for i in range(NPT)]
        pT_lo = [a.sb(f"pT_lo{i}", [P, 2, TOK], F32R) for i in range(NPT)]
        maxima = a.sb("maxima", [P, 2, QT, UPR])
        neg_max = a.sb("neg_max", [P, 2, QT])
        sums = a.sb("sums", [P, 2, QT, PIECES])
        total = a.sb("total", [P, QT])
        inverse = a.sb("inverse", [P, QT])
        ones = a.sb("ones", [P, P], F32R)
        diag_hi = a.sb("diag_hi", [P, TOK], F32R)
        diag_lo = a.sb("diag_lo", [P, TOK], F32R)
        scale_rows = a.sb("scale_rows", [P, TOK])
        o_out = [shared.out[:, i, :] for i in range(2)]
        s_ps = a.ps("s_ps", [P, NS, BANK])
        t_ps = a.ps("t_ps", [P, 2, 2, TOK])
        o_ps = a.ps("o_ps", [P, 2, TOK])
        m_ps = a.ps("m_ps", [P, 2, TOK])

        piece_asked = a.sem("piece_asked")
        piece_in = [a.sem(f"piece_in{i}") for i in range(2)]
        piece_hi = a.sem("piece_hi")
        piece_lo = a.sem("piece_lo")
        w_in = a.sem("w_in")
        w_hi_ready = a.sem("w_hi_ready")
        w_lo_ready = a.sem("w_lo_ready")
        q_ready = a.sem("q_ready")
        q_hi_ready = a.sem("q_hi_ready")
        q_lo_ready = a.sem("q_lo_ready")
        s_ready = a.sem("s_ready")
        s_drained = a.sem("s_drained")
        max_ready = a.sem("max_ready")
        exp_done = a.sem("exp_done")
        turned = a.sem("turned")
        pT_hi_ready = a.sem("pT_hi_ready")
        pT_lo_ready = a.sem("pT_lo_ready")
        pv_done = a.sem("pv_done")
        sum_ready = a.sem("sum_ready")
        ones_set = a.sem("ones_set")
        diag_ready = a.sem("diag_ready")
        spread = a.sem("spread")
        spread_copied = a.sem("spread_copied")
        o_ready = a.sem("o_ready")
        o_stored = proj.stored
        block = ctx.enter_context(nc.Block())

        def slots(eng, kv_head_slot):
            def kv_head(g, last):
                for u in range(2):
                    kv_head_slot(eng, g, GROUP * g + u, u, last)
                with eng.Fori(1, GROUP // 2 - 1) as i:
                    for par in range(2):
                        kv_head_slot(eng, g, GROUP * g + 2 * i + par, 2 + par, last)
                for u in range(GROUP - 2, GROUP):
                    kv_head_slot(eng, g, GROUP * g + u, u, last)

            with eng.Fori(0, KVH - 1) as g:
                kv_head(g, False)
            kv_head(KVH - 1, True)

        def flags(u, last):
            return not (last and u == GROUP - 1), not (last and u >= GROUP - 2)

        def ahead(n, par, j):
            return (n, par, j + LAG) if j + LAG < PAIRS else (n + 1, 1 - par, j + LAG - PAIRS)

        def pt_free(n, j):
            last = j - NPT if j >= NPT else max(x for x in range(PAIRS) if x % NPT == j) - PAIRS
            return NPT + PAIRS * n + last + 1

        def load_weight(sp, n):
            sp.wait_ge(w_lo_ready, n + 1)
            sp.dma_start(w_raw[:, :, :], wq[bass.ds(n, 1)].rearrange("h p k d -> p (h k) d")).then_inc(w_in, 16)

        def load_piece(sp, g, i):
            sp.wait_ge(piece_lo, 2 * PIECES * g + i + 1)
            sp.sem_inc(piece_asked, 1)
            source = (kT_dram[bass.ds(g, 1)].rearrange("g p n -> (g p) n") if i < PIECES else
                      v_dram[bass.ds(g, 1)].rearrange("g p t d -> (g p) (t d)"))
            c0 = i % PIECES * PIECE
            sp.dma_start(stage[i % 2][:, :], source[:, c0:c0 + PIECE]).then_inc(piece_in[i % 2], 16)

        def store_o(sp, n, par):
            sp.wait_ge(o_ready, n + 2)
            sp.dma_start(oT_dram[bass.ds(n, 1)].rearrange("h p n -> (h p) n"), o_out[par]).then_inc(o_stored[par], 16)

        def sync_slot(sp, g, n, u, last):
            if flags(u, last)[1]:
                load_weight(sp, n + 2)
            if not last and u == GROUP - 2:
                for i in range(PIECES):
                    load_piece(sp, g + 1, i)
            if not last and u == GROUP - 1:
                for i in range(PIECES, 2 * PIECES):
                    load_piece(sp, g + 1, i)
            if last and u == GROUP - 1:
                sp.wait_ge(s_ready, NU * HEADS)
                sp.wait_ge(turned, PAIRS * (HEADS - 1))
                sp.wait_ge(piece_lo, 2 + 2 * PIECES * KVH)
                for par in range(2):
                    sp.wait_ge(o_stored[par], 16 * (HEADS // 2))
                for step in range(2):
                    proj.load(sp, step, step)
            store_o(sp, n, u % 2)

        @block.sync
        def _(sp):
            for par in range(2):
                sp.sem_inc(o_stored[par], 16)
            sp.sem_inc(w_in, 16)
            for i in range(FIRST):
                sp.sem_inc(piece_in[i % 2], 16)
            sp.wait_ge(shared.k_stored, 16 * (NCHUNK + 2))
            sp.wait_ge(shared.v_stored, 16 * (NCHUNK + 2))
            for i in range(FIRST, PIECES):
                load_piece(sp, 0, i)
            load_weight(sp, 1)
            load_piece(sp, 0, 4)
            load_piece(sp, 0, 5)
            load_piece(sp, 0, 6)
            load_piece(sp, 0, 7)
            slots(sp, sync_slot)

        def act_piece(act, g, i, first=False):
            act.wait_ge(piece_in[i % 2], 16 * (PIECES * g + i // 2 + 1))
            end = (i % PIECES + 1) * PIECE
            if not first and i < PIECES:
                act.wait_ge(s_ready, NU * (GROUP * g - 1) + UPR + -(-end // BANK))
            if not first and PIECES <= i < 2 * PIECES - 2:
                act.wait_ge(pv_done, NPT + PAIRS * (GROUP * g - 1) + -(-end // (2 * P)))
            if i >= 2 * PIECES - 2:
                act.wait_ge(pv_done, NPT + PAIRS * GROUP * g)
            to = (kT_hi if i < PIECES else v_hi)[:, end - PIECE:end]
            act.activation(to, stage[i % 2][:, :], ACT.Copy).then_inc(piece_hi, 1)

        def act_weight(act, n):
            act.wait_ge(w_in, 16 * (n + 1))
            act.wait_ge(q_ready, n + 1)
            act.activation(w_hi[:, :, :], w_raw[:, :, :], ACT.Copy).then_inc(w_hi_ready, 1)

        def act_query(act, n):
            act.wait_ge(q_ready, n + 2)
            act.activation(qT_hi[:, :], m_ps[:, 0, :], ACT.Copy).then_inc(q_hi_ready, 1)

        def act_exp(act, n, par, qt, e):
            row = rows[par][qt][:, e * PIECE:(e + 1) * PIECE]
            act.wait_ge(max_ready, QT * n + qt + 1)
            act.activation(row, row, ACT.Exp, bias=neg_max[:, par, qt:qt + 1],
                           accum_out=sums[:, par, qt, e:e + 1]).then_inc(exp_done, 1)

        def act_turned(act, n, par, j):
            act.wait_ge(turned, PAIRS * n + j + 1)
            act.wait_ge(pv_done, pt_free(n, j))
            act.activation(pT_hi[j % NPT][:, :, :], t_ps[:, (par * PAIRS + j) % 2, :, :],
                           ACT.Copy).then_inc(pT_hi_ready, 1)

        def act_slot(act, g, n, u, last):
            par = u % 2
            has_next, has_after = flags(u, last)
            for j in range(PAIRS):
                if has_next or j + LAG < PAIRS:
                    act_turned(act, *ahead(n, par, j))
                if u == 0 and j in (0, 2):
                    act_piece(act, g, 2 * PIECES - 2 + j // 2)
                if j in (1, 3):
                    act_exp(act, n, par, 1, 2 + j // 2)
                if has_after and j == 5:
                    act_weight(act, n + 2)
                if has_next and 6 <= j <= 9:
                    act_exp(act, n + 1, 1 - par, 0, j - 6)
                if j == 10:
                    act.wait_ge(spread, n + 1)
                    act.activation(scale_rows[:, :], m_ps[:, 1, :], ACT.Copy).then_inc(spread_copied, 1)
                if not last and u == GROUP - 2 and j in (8, 10, 12, 14):
                    act_piece(act, g + 1, (j - 8) // 2)
                if not last and u == GROUP - 1 and j in (6, 10):
                    act_piece(act, g + 1, PIECES + (j - 6) // 4)
                if has_next and 12 <= j <= 13:
                    act_exp(act, n + 1, 1 - par, 1, j - 12)
                if has_after and j == Q_STEPS[-1]:
                    act_query(act, n + 2)
                if not has_next and j == 6:
                    proj.high(act, 0, 0)

        @block.scalar
        def _(act):
            act.sem_inc(spread_copied, 1)
            act.sem_inc(w_hi_ready, 1)
            act.sem_inc(piece_hi, FIRST)
            act_query(act, 0)
            for i in range(FIRST, PIECES):
                act_piece(act, 0, i, first=True)
            act_weight(act, 1)
            act_piece(act, 0, PIECES, first=True)
            for e in range(PIECES):
                act_exp(act, 0, 0, 0, e)
            act_piece(act, 0, PIECES + 1, first=True)
            act_exp(act, 0, 0, 1, 0)
            act_query(act, 1)
            act_exp(act, 0, 0, 1, 1)
            for j in range(LAG):
                act_turned(act, 0, 0, j)
            slots(act, act_slot)

        def pool_piece(pool, g, i):
            pool.wait_ge(piece_hi, 2 * PIECES * g + i + 1)
            at = slice(i % PIECES * PIECE, (i % PIECES + 1) * PIECE)
            hi, lo = (kT_hi, kT_lo) if i < PIECES else (v_hi, v_lo)
            pool.tensor_tensor(lo[:, at], stage[i % 2][:, :], f32(hi[:, at]), ALU.subtract).then_inc(piece_lo, 1)

        def pool_weight(pool, n):
            pool.wait_ge(w_hi_ready, n + 1)
            pool.tensor_tensor(w_lo[:, :, :], w_raw[:, :, :], f32(w_hi[:, :, :]), ALU.subtract).then_inc(w_lo_ready, 1)

        def pool_slot(pool, g, n, u, last):
            if u == 0:
                for i in range(2 * PIECES - 2, 2 * PIECES):
                    pool_piece(pool, g, i)
            if flags(u, last)[1]:
                pool_weight(pool, n + 2)
            if not last and u == GROUP - 2:
                for i in range(PIECES):
                    pool_piece(pool, g + 1, i)
            if not last and u == GROUP - 1:
                for i in range(PIECES, 2 * PIECES - 2):
                    pool_piece(pool, g + 1, i)
            if last and u == GROUP - 1:
                proj.low(pool, 0, 0)

        @block.gpsimd
        def _(pool):
            pool.memset(f32(ones[:, :]), 1.0).then_inc(ones_set, 1)
            pool.sem_inc(w_lo_ready, 1 + 1)
            pool.sem_inc(piece_lo, 2 + FIRST)
            for i in range(FIRST, PIECES):
                pool_piece(pool, 0, i)
            pool_weight(pool, 1)
            for i in range(PIECES, 2 * PIECES - 2):
                pool_piece(pool, 0, i)
            slots(pool, pool_slot)

        def dve_query(dve, n):
            dve.wait_ge(q_hi_ready, n + 1)
            dve.tensor_tensor(qT_lo[:, :], m_ps[:, 0, :], f32(qT_hi[:, :]), ALU.subtract).then_inc(q_lo_ready, 1)

        def dve_scores(dve, n, par, k):
            qt, c0, width = UNITS[k]
            dve.wait_ge(s_ready, NU * n + k + 1)
            dve.tensor_scalar(rows[par][qt][:, c0:c0 + width], s_ps[:, (par * NU + k) % NS, 0:width], SCALE, None,
                              ALU.mult, ALU.max, accum_out=maxima[:, par, qt, k % UPR:k % UPR + 1]).then_inc(s_drained, 1)
            if k % UPR == UPR - 1:
                dve.wait_ge(s_drained, NS + NU * n + k + 1)
                dve.tensor_reduce(neg_max[:, par, qt:qt + 1], maxima[:, par, qt, :], AX.X, ALU.max,
                                  negate=True).then_inc(max_ready, 1)

        def dve_inverse(dve, n, par):
            dve.wait_ge(exp_done, QT * PIECES * (n + 1))
            dve.tensor_reduce(total[:, :], sums[:, par, :, :], AX.X, ALU.add).then_inc(sum_ready, 1)
            dve.wait_ge(sum_ready, 2 * n + 1)
            dve.reciprocal(inverse[:, :], total[:, :]).then_inc(sum_ready, 1)
            dve.wait_ge(sum_ready, 2 * n + 2)
            for qt in range(QT):
                dve.tensor_scalar(diag_hi[:, qt * P:(qt + 1) * P], ident[:, :], inverse[:, qt:qt + 1], None,
                                  ALU.mult).then_inc(diag_ready, 1)
            for qt in range(QT):
                at = slice(qt * P, (qt + 1) * P)
                dve.wait_ge(diag_ready, 2 * QT * n + qt + 1)
                dve.scalar_tensor_tensor(out=diag_lo[:, at], in0=ident[:, :], scalar=inverse[:, qt:qt + 1],
                                         in1=f32(diag_hi[:, at]), op0=ALU.mult, op1=ALU.subtract).then_inc(diag_ready, 1)

        def dve_turned(dve, n, par, j):
            dve.wait_ge(pT_hi_ready, PAIRS * n + j + 1)
            dve.tensor_tensor(pT_lo[j % NPT][:, :, :], t_ps[:, (par * PAIRS + j) % 2, :, :],
                              f32(pT_hi[j % NPT][:, :, :]), ALU.subtract).then_inc(pT_lo_ready, 1)

        def dve_output(dve, n, par):
            dve.wait_ge(spread_copied, n + 2)
            dve.wait_ge(o_stored[par], 8 * (n - par) + 16)
            dve.wait_ge(pv_done, NPT + PAIRS * (n + 1))
            dve.tensor_tensor(o_out[par], o_ps[:, par, :], scale_rows[:, :], ALU.mult).then_inc(o_ready, 1)

        def dve_slot(dve, g, n, u, last):
            par = u % 2
            has_next, has_after = flags(u, last)
            for j in range(PAIRS):
                if j == PAIRS - 1:
                    dve_output(dve, n, par)
                if has_next or j + LAG < PAIRS:
                    dve_turned(dve, *ahead(n, par, j))
                if has_next:
                    for k in UNITS_OF_STEP[j]:
                        dve_scores(dve, n + 1, 1 - par, k)
                if j == 6:
                    dve_inverse(dve, n, par)
                if has_after and j == Q_STEPS[-1]:
                    dve_query(dve, n + 2)

        @block.vector
        def _(dve):
            dve.sem_inc(s_drained, NS)
            dve.sem_inc(pT_lo_ready, 2)
            dve.sem_inc(o_ready, 1)
            dve_query(dve, 0)
            dve.wait_ge(shared.k_stored, 16 * (NCHUNK + 2))
            for k in range(NU):
                dve_scores(dve, 0, 0, k)
            dve_query(dve, 1)
            for j in range(LAG):
                dve_turned(dve, 0, 0, j)
            slots(dve, dve_slot)

        def pe_query(pe, n, k0, k1, weight=(w_hi, w_lo)):
            hi, lo = weight
            if k0 == 0:
                pe.wait_ge(w_lo_ready, n + 2)
            for k in range(k0, k1):
                last = three_pass(pe, m_ps[:, 0, :], hi[:, k, :], lo[:, k, :], hT_hi[:, k, :], hT_lo[:, k, :],
                                  k == 0, k == KT - 1)
            if k1 == KT:
                last.then_inc(q_ready, 1)

        def pe_scores(pe, g, n, par, k):
            qt, c0, width = UNITS[k]
            if k == 0:
                pe.wait_ge(q_lo_ready, n + 1)
            if g is not None and qt == 0:
                pe.wait_ge(piece_lo, 2 + 2 * PIECES * g + piece_of(c0 + width) + 1)
            pe.wait_ge(s_drained, NU * n + k + 1)
            q, key = slice(qt * P, (qt + 1) * P), slice(c0, c0 + width)
            three_pass(pe, s_ps[:, (par * NU + k) % NS, 0:width], qT_hi[:, q], qT_lo[:, q],
                       kT_hi[:, key], kT_lo[:, key], True, True).then_inc(s_ready, 1)

        def pe_turn(pe, n, par, j):
            done = piece_of(2 * P * (j + 1)) + 1
            pe.wait_ge(exp_done, QT * PIECES * n + PIECES * (QT - 1) + done)
            pe.wait_ge(pT_lo_ready, PAIRS * n + j + 1)
            for t in range(2):
                at = slice((2 * j + t) * P, (2 * j + t + 1) * P)
                for qt in range(QT):
                    last = pe.transpose(t_ps[:, (par * PAIRS + j) % 2, t, qt * P:(qt + 1) * P],
                                        rows[par][qt][:, at], ident[:, :])
            last.then_inc(turned, 1)

        def pe_values(pe, g, n, par, j):
            if g is not None and (j == 0 or piece_of(2 * P * (j + 1)) > piece_of(2 * P * j)):
                pe.wait_ge(piece_lo, 2 + 2 * PIECES * g + PIECES + piece_of(2 * P * (j + 1)) + 1)
            if j == 0:
                pe.wait_ge(o_ready, n + 1)
            pe.wait_ge(pT_lo_ready, 2 + PAIRS * n + j + 1)
            for t in range(2):
                at = slice((2 * j + t) * P, (2 * j + t + 1) * P)
                last = three_pass(pe, o_ps[:, par, :], v_hi[:, at], v_lo[:, at], pT_hi[j % NPT][:, t, :],
                                  pT_lo[j % NPT][:, t, :], j == 0 and t == 0, j == PAIRS - 1 and t == 1)
            last.then_inc(pv_done, 1)

        def pe_slot(pe, g, n, u, last):
            par = u % 2
            has_next, has_after = flags(u, last)
            for j in range(PAIRS):
                if j >= PAIRS - LAG:
                    pe_values(pe, g if u == 0 else None, n, par, j)
                if has_next or j + LAG < PAIRS:
                    pe_turn(pe, *ahead(n, par, j))
                if has_next:
                    for k in UNITS_OF_STEP[j]:
                        pe_scores(pe, g + 1 if u == GROUP - 1 else None, n + 1, 1 - par, k)
                if j == 8:
                    pe.wait_ge(diag_ready, 2 * QT * (n + 1))
                    pe.matmul(m_ps[:, 1, :], ones[:, :], diag_hi[:, :], start=True, stop=False)
                    pe.matmul(m_ps[:, 1, :], ones[:, :], diag_lo[:, :], start=False, stop=True).then_inc(spread, 1)
                if has_after and j in Q_STEPS:
                    if j == Q_STEPS[0]:
                        pe.wait_ge(spread_copied, n + 2)
                    k = 2 * (j - Q_STEPS[0])
                    pe_query(pe, n + 2, k, k + 2)
                if j < PAIRS - LAG:
                    pe_values(pe, g if u == 0 else None, n, par, j)

        @block.tensor
        def _(pe):
            pe.sem_inc(q_ready, 1)
            pe.sem_inc(pv_done, NPT)
            pe.wait_ge(ones_set, 1)
            pe_query(pe, 0, 0, KT, shared.first_weight)
            for k in range(NU):
                pe_scores(pe, 0, 0, 0, k)
            pe_query(pe, 1, 0, KT)
            for j in range(LAG):
                pe_turn(pe, 0, 0, j)
            slots(pe, pe_slot)


HP = 2
STEPS = HEADS // HP
SPLITS = 1 + HP


class Projection:

    def __init__(self, a, srcT_dram, w, raw, s_raw, even):
        self.srcT_dram, self.w = srcT_dram, w
        self.w_raw = [raw[:, i] for i in range(2)]
        self.s_raw = [s_raw[:, i] for i in range(2)]
        self.w_hi, self.w_lo, self.s_hi, self.s_lo = [[tile] for tile in even]
        self.step_in = [a.sem(f"step_in{i}") for i in range(2)]
        self.stored = [a.sem(f"stored{i}") for i in range(2)]
        self.hi_ready = a.sem("hi_ready")
        self.lo_ready = a.sem("lo_ready")

    def set_odd(self, odd):
        for tiles, tile in zip((self.w_hi, self.w_lo, self.s_hi, self.s_lo), odd):
            tiles.append(tile)

    def load(self, sp, s, par):
        sp.dma_start(self.w_raw[par], self.w[bass.ds(HP * s, HP)].rearrange("h p n -> p h n")).then_inc(self.step_in[par], 16)
        sp.dma_start(self.s_raw[par], self.srcT_dram[bass.ds(HP * s, HP)].rearrange("h p n -> p h n")).then_inc(self.step_in[par], 16)

    def high(self, act, s, par):
        act.wait_ge(self.step_in[par], 16 * (s - par) + 32)
        act.activation(self.s_hi[par], self.s_raw[par], ACT.Copy).then_inc(self.hi_ready, 1)
        for h in range(HP):
            act.activation(self.w_hi[par][:, h, :], self.w_raw[par][:, h, :], ACT.Copy).then_inc(self.hi_ready, 1)

    def low(self, eng, s, par):
        eng.wait_ge(self.hi_ready, SPLITS * s + 1)
        eng.tensor_tensor(self.s_lo[par], self.s_raw[par], f32(self.s_hi[par]), ALU.subtract).then_inc(self.lo_ready, 1)
        for h in range(HP):
            eng.wait_ge(self.hi_ready, SPLITS * s + 2 + h)
            eng.tensor_tensor(self.w_lo[par][:, h, :], self.w_raw[par][:, h, :], f32(self.w_hi[par][:, h, :]),
                              ALU.subtract).then_inc(self.lo_ready, 1)


def project_out(nc, name, proj, x_sb, h, hT_hi, hT_lo, ident, stores, prefetch, prefetches,
                norm=None, meanwhile=None):
    with ExitStack() as ctx:
        a = Alloc(nc, ctx, name)
        y_ps = a.ps("y_ps", [P, QT, 2, BANK])
        turned = a.ps("turned", [P, KT, TOK])
        ln = LayerNorm(a, x_sb, h, turned, hT_hi, hT_lo, ident)
        row_scale = a.sb("row_scale", [P, QT])
        ve = a.sb("ve", [P, QT])
        root = a.sb("root", [P, QT])
        t0 = a.sb("t0", [P, QT])
        r0 = a.sb("r0", [P, QT])
        summed = a.sem("summed")
        small = a.sem("small")
        root_ready = a.sem("root_ready")
        mm_done = a.sem("mm_done")
        y_ready = a.sem("y_ready")
        x_ready = a.sem("x_ready")
        block = ctx.enter_context(nc.Block())

        def load(sp, s, par):
            sp.wait_ge(proj.lo_ready, SPLITS * (s - 1))
            proj.load(sp, s, par)

        @block.sync
        def _(sp):
            for i in range(prefetches):
                for par in range(2):
                    load(sp, 2 * (i + 1) + par, par)
                prefetch(sp, i)
            with sp.Fori(1 + prefetches, STEPS // 2 - 1) as i:
                for par in range(2):
                    load(sp, 2 * i + par, par)
            for sem, count in zip(proj.stored, stores):
                if count:
                    sp.wait_ge(sem, 16 * (count + 1))
            for par in range(2):
                load(sp, STEPS - 2 + par, par)

        if meanwhile is not None:
            @block.gpsimd
            def _(pool):
                meanwhile(pool)

        @block.scalar
        def _(act):
            proj.high(act, 1, 1)
            if norm is not None:
                act.wait_ge(small, 1)
                act.activation(root[:, :], ve[:, :], ACT.Sqrt).then_inc(root_ready, 1)
            with act.Fori(1, STEPS // 2) as i:
                for par in range(2):
                    act.wait_ge(mm_done, 2 * i + par - 1)
                    proj.high(act, 2 * i + par, par)
            for t in range(QT):
                ln.act_root(act, t)
            ln.act_hi(act)

        @block.vector
        def _(dve):
            proj.low(dve, 1, 1)
            if norm is not None:
                dve.wait_ge(summed, 1)
                dve.tensor_scalar(ve[:, :], turned[:, 0, 0:QT], 1.0 / (HEADS * D), EPS, ALU.mult, ALU.add).then_inc(small, 1)
                dve.wait_ge(root_ready, 1)
                dve.reciprocal(r0[:, :], root[:, :]).then_inc(small, 1)
                dve.wait_ge(small, 2)
                dve.tensor_tensor(t0[:, :], r0[:, :], r0[:, :], ALU.mult).then_inc(small, 1)
                dve.wait_ge(small, 3)
                dve.tensor_tensor(t0[:, :], t0[:, :], ve[:, :], ALU.mult).then_inc(small, 1)
                dve.wait_ge(small, 4)
                dve.tensor_scalar(t0[:, :], t0[:, :], -0.5, 1.5, ALU.mult, ALU.add).then_inc(small, 1)
                dve.wait_ge(small, 5)
                dve.tensor_tensor(row_scale[:, :], r0[:, :], t0[:, :], ALU.mult).then_inc(small, 1)
            with dve.Fori(1, STEPS // 2) as i:
                for par in range(2):
                    proj.low(dve, 2 * i + par, par)
            if norm is not None:
                dve.wait_ge(small, 6)
            for t in range(QT):
                for half in range(2):
                    n = 2 * t + half
                    dve.wait_ge(y_ready, n + 1)
                    x = x_sb[:, t, half * BANK:(half + 1) * BANK]
                    if norm is None:
                        dve.tensor_tensor(x, y_ps[:, t, half, :], x, ALU.add).then_inc(x_ready, 1)
                    else:
                        dve.scalar_tensor_tensor(out=x, in0=y_ps[:, t, half, :], scalar=row_scale[:, t:t + 1],
                                                 in1=x, op0=ALU.mult, op1=ALU.add).then_inc(x_ready, 1)
                    dve.wait_ge(x_ready, n + 1)
                    ln.dve_stats(dve, t, half)
                    if t > 0 and half == 0:
                        ln.dve_rows(dve, t - 1)
                ln.dve_variance(dve, t)
            ln.dve_rows(dve, QT - 1)
            ln.dve_lo(dve)

        def part(pe, par, h, t, b, first, last):
            tok, col = slice(t * P, (t + 1) * P), slice(b * BANK, (b + 1) * BANK)
            return three_pass(pe, y_ps[:, t, b, :], proj.s_hi[par][:, h, tok], proj.s_lo[par][:, h, tok],
                              proj.w_hi[par][:, h, col], proj.w_lo[par][:, h, col], first, last)

        def step(pe, s, par, first=False):
            pe.wait_ge(proj.lo_ready, SPLITS * (s + 1))
            for h in range(HP):
                for t in range(QT):
                    for b in range(2):
                        last = part(pe, par, h, t, b, first and h == 0, False)
            last.then_inc(mm_done, 1)

        @block.tensor
        def _(pe):
            if norm is not None:
                square_sum, ones = norm
                for t in range(QT):
                    for h in range(2):
                        last = pe.matmul(turned[:, 0, t:t + 1], square_sum[:, h, t * P:(t + 1) * P], ones[:, 0:1],
                                         start=h == 0, stop=h == 1)
                last.then_inc(summed, 1)
            step(pe, 0, 0, True)
            step(pe, 1, 1)
            with pe.Fori(1, STEPS // 2 - 1) as i:
                step(pe, 2 * i, 0)
                step(pe, 2 * i + 1, 1)
            step(pe, STEPS - 2, 0)
            pe.wait_ge(proj.lo_ready, SPLITS * STEPS)
            for t in range(QT):
                for b in range(2):
                    for h in range(HP):
                        last = part(pe, 1, h, t, b, False, h == HP - 1)
                    last.then_inc(y_ready, 1)
            pe.wait_ge(x_ready, 1)
            for t, count in zip(range(QT), (8, 10)):
                keep_clock(pe, y_ps[:, 0, 0, :], proj.s_hi[1][:, 0, 0:P], proj.w_hi[1][:, 0, 0:BANK], count)
                ln.pe_turn(pe, t)


HPAIRS = HEADS // 2


class PairWeights:

    def __init__(self, a, w_qk, w_gv):
        self.w = (w_qk, w_gv)
        self.raw = [a.sb(f"raw{i}", [P, KT, 4 * D]) for i in range(2)]
        self.hi = [a.sb(f"hi{i}", [P, KT, 4 * D], F32R) for i in range(2)]
        self.lo = [a.sb(f"lo{i}", [P, KT, 4 * D], F32R) for i in range(2)]
        self.arrived = [a.sem(f"arrived{i}") for i in range(2)]
        self.hi_ready = [a.sem(f"hi_ready{i}") for i in range(2)]
        self.lo_ready = [a.sem(f"lo_ready{i}") for i in range(2)]

    def load(self, sp, part, p):
        sp.dma_start(self.raw[part][:, :, :], self.w[part][bass.ds(p, 1)].rearrange("h p k n -> p (h k) n")).then_inc(self.arrived[part], 16)

    def load_half(self, sp, part, half):
        at = slice(half * KT // 2, (half + 1) * KT // 2)
        sp.dma_start(self.raw[part][:, at, :], self.w[part][0, :, at, :]).then_inc(self.arrived[part], 16)

    def first_pair(self, pool):
        for part in range(2):
            pool.wait_ge(self.arrived[part], 32)
            pool.tensor_copy(self.hi[part][:, :, :], self.raw[part][:, :, :]).then_inc(self.hi_ready[part], 1)
            pool.wait_ge(self.hi_ready[part], 1)
            pool.tensor_tensor(self.lo[part][:, :, :], self.raw[part][:, :, :], f32(self.hi[part][:, :, :]),
                               ALU.subtract).then_inc(self.lo_ready[part], 1)


def linear_attention(nc, weights, decay, norm_w, hT_hi, hT_lo, zT_dram, square_sum, proj, shared):
    with ExitStack() as ctx:
        a = Alloc(nc, ctx, "la_")
        w_hi, w_lo, raw = weights.hi, weights.lo, weights.raw
        norm = a.sb("norm", [P, HEADS])
        dec = a.sb("dec", [P, 2, TOK])
        gate = a.sb("gate", [P, 2, TOK])
        sig_qk = carve(shared.f, 0, 2, 2, TOK)
        qk = carve(shared.f, 4 * TOK, 2, 2, TOK)
        m = carve(shared.f, 8 * TOK, 2, QT, TOK)
        sig_v = carve(shared.f, 12 * TOK, QT, 2 * D)
        v = carve(shared.f, 12 * TOK + 4 * D, QT, 2 * D)
        qk_hi = carve(shared.r[0], 0, 2, 2, TOK)
        qk_lo = carve(shared.r[0], 4 * TOK, 2, 2, TOK)
        m_hi = carve(shared.r[0], 8 * TOK, 2, QT, TOK)
        m_lo = carve(shared.r[0], 12 * TOK, 2, QT, TOK)
        v_hi = carve(shared.r[1], 0, QT, 2 * D)
        v_lo = carve(shared.r[1], 4 * D, QT, 2 * D)
        squares = a.sb("squares", [P, 2, TOK])
        z = shared.out
        qk_ps = a.ps("qk_ps", [P, 2, 2, TOK])
        g_ps = a.ps("g_ps", [P, 2, TOK])
        v_ps = a.ps("v_ps", [P, QT, 2 * D])
        a_ps = a.ps("a_ps", [P, 2, QT, TOK])
        o_ps = a.ps("o_ps", [P, 2, TOK])

        norm_in = a.sem("norm_in")
        w_in, w_hi_ready, w_lo_ready = weights.arrived, weights.hi_ready, weights.lo_ready
        dec_in = a.sem("dec_in")
        qk_ready = a.sem("qk_ready")
        qk_sig = a.sem("qk_sig")
        qk_done = a.sem("qk_done")
        qk_hi_ready = a.sem("qk_hi_ready")
        qk_lo_ready = a.sem("qk_lo_ready")
        g_ready = a.sem("g_ready")
        gate_ready = a.sem("gate_ready")
        v_ready = a.sem("v_ready")
        v_sig = a.sem("v_sig")
        v_done = a.sem("v_done")
        v_hi_ready = a.sem("v_hi_ready")
        v_lo_ready = a.sem("v_lo_ready")
        a_ready = a.sem("a_ready")
        m_ready = a.sem("m_ready")
        m_hi_ready = a.sem("m_hi_ready")
        m_lo_ready = a.sem("m_lo_ready")
        o_ready = a.sem("o_ready")
        sq_ready = a.sem("sq_ready")
        sq_added = a.sem("sq_added")
        z_ready = a.sem("z_ready")
        z_stored = proj.stored[0]
        zeroed = a.sem("zeroed")
        block = ctx.enter_context(nc.Block())
        parts = ((0, slice(0, TOK)), (1, slice(P, TOK)))

        def load_decay(sp, p):
            sp.dma_start(dec[:, :, :], decay[bass.ds(p, 1)].rearrange("g p h n -> p (g h) n")).then_inc(dec_in, 16)

        def store_z(sp, p):
            sp.wait_ge(z_ready, 2 * p + 4)
            sp.dma_start(zT_dram[bass.ds(2 * p, 2)].rearrange("h p n -> p h n"), z[:, :, :]).then_inc(z_stored, 16)

        @block.sync
        def _(sp):
            sp.sem_inc(z_stored, 16)
            sp.dma_start(norm[:, :], norm_w).then_inc(norm_in, 16)
            load_decay(sp, 0)
            for part in range(2):
                sp.wait_ge(w_lo_ready[part], 1)
                weights.load(sp, part, 1)
            with sp.Fori(1, HPAIRS - 1) as p:
                sp.wait_ge(w_lo_ready[0], p + 1)
                weights.load(sp, 0, p + 1)
                sp.wait_ge(m_ready, 4 * p)
                load_decay(sp, p)
                sp.wait_ge(w_lo_ready[1], p + 1)
                weights.load(sp, 1, p + 1)
                store_z(sp, p - 1)
            sp.wait_ge(m_ready, 4 * (HPAIRS - 1))
            load_decay(sp, HPAIRS - 1)
            sp.wait_ge(qk_ready, HEADS)
            sp.wait_ge(z_stored, 16 * (HPAIRS - 1))
            for step in range(2):
                proj.load(sp, step, step)
            store_z(sp, HPAIRS - 2)
            store_z(sp, HPAIRS - 1)

        @block.gpsimd
        def _(pool):
            pool.memset(square_sum[:, :, :], 0.0).then_inc(sq_added, 1)
            for h in range(2):
                pool.memset(f32(m_hi[:, h, 1, 0:P]), 0.0).then_inc(zeroed, 1)
                pool.memset(f32(m_lo[:, h, 1, 0:P]), 0.0).then_inc(zeroed, 1)

            def add_squares(p):
                pool.wait_ge(sq_ready, p + 2)
                pool.wait_ge(sq_added, p + 1)
                pool.tensor_tensor(square_sum[:, :, :], square_sum[:, :, :], squares[:, :, :], ALU.add).then_inc(sq_added, 1)

            with pool.Fori(0, HPAIRS - 1) as p:
                add_squares(p)
            proj.low(pool, 0, 0)
            add_squares(HPAIRS - 1)

        def act_split(act, part, p):
            act.wait_ge(w_in[part], 16 * (p + 2))
            act.activation(w_hi[part][:, :, :], raw[part][:, :, :], ACT.Copy).then_inc(w_hi_ready[part], 1)

        def act_qk(act, p):
            for h in range(2):
                act.wait_ge(qk_ready, 2 * p + h + 1)
                act.activation(sig_qk[:, h, :, :], qk_ps[:, h, :, :], ACT.Sigmoid).then_inc(qk_sig, 1)
            for h in range(2):
                act.wait_ge(qk_done, 2 * p + h + 1)
                act.activation(qk_hi[:, h, :, :], qk[:, h, :, :], ACT.Copy).then_inc(qk_hi_ready, 1)

        def act_v(act, p):
            act.wait_ge(v_ready, p + 1)
            act.activation(sig_v[:, :, :], v_ps[:, :, :], ACT.Sigmoid).then_inc(v_sig, 1)
            act.wait_ge(v_done, p + 1)
            act.activation(v_hi[:, :, :], v[:, :, :], ACT.Copy).then_inc(v_hi_ready, 1)

        def act_gate(act, p):
            act.wait_ge(z_ready, 2 * p + 2)
            act.wait_ge(g_ready, p + 1)
            act.activation(gate[:, :, :], g_ps[:, :, :], ACT.Sigmoid).then_inc(gate_ready, 1)

        def act_decayed(act, p):
            for h in range(2):
                act.wait_ge(m_ready, 4 * p + 2 * h + 2)
                for jt, at in parts:
                    act.activation(m_hi[:, h, jt, at], m[:, h, jt, at], ACT.Copy).then_inc(m_hi_ready, 1)

        def act_squares(act, p):
            act.wait_ge(o_ready, p + 1)
            act.wait_ge(sq_added, p + 1)
            act.activation(squares[:, :, :], o_ps[:, :, :], ACT.Square).then_inc(sq_ready, 1)

        def act_pair(act, p, prefetch):
            act_decayed(act, p - 1)
            act.wait_ge(g_ready, p)
            act_split(act, 1, p)
            act_qk(act, p)
            act_squares(act, p - 1)
            if prefetch:
                act.wait_ge(qk_ready, 2 * p + 2)
                act_split(act, 0, p + 1)
            else:
                proj.high(act, 0, 0)
            act_v(act, p)

        @block.scalar
        def _(act):
            act_qk(act, 0)
            act.wait_ge(qk_ready, 2)
            act_split(act, 0, 1)
            act_v(act, 0)
            act_gate(act, 0)
            with act.Fori(1, HPAIRS - 1) as p:
                act_pair(act, p, True)
                act_gate(act, p)
            act_pair(act, HPAIRS - 1, False)
            act_decayed(act, HPAIRS - 1)
            act_gate(act, HPAIRS - 1)
            act_squares(act, HPAIRS - 1)

        def dve_split(dve, part, p):
            dve.wait_ge(w_hi_ready[part], p + 1)
            dve.tensor_tensor(w_lo[part][:, :, :], raw[part][:, :, :], f32(w_hi[part][:, :, :]),
                              ALU.subtract).then_inc(w_lo_ready[part], 1)

        def dve_qk(dve, p):
            for h in range(2):
                dve.wait_ge(qk_sig, 2 * p + h + 1)
                dve.tensor_tensor(qk[:, h, :, :], qk_ps[:, h, :, :], sig_qk[:, h, :, :], ALU.mult).then_inc(qk_done, 1)
            for h in range(2):
                dve.wait_ge(qk_hi_ready, 2 * p + h + 1)
                dve.tensor_tensor(qk_lo[:, h, :, :], qk[:, h, :, :], f32(qk_hi[:, h, :, :]), ALU.subtract).then_inc(qk_lo_ready, 1)

        def dve_v(dve, p):
            dve.wait_ge(v_sig, p + 1)
            dve.tensor_tensor(v[:, :, :], v_ps[:, :, :], sig_v[:, :, :], ALU.mult).then_inc(v_done, 1)
            dve.wait_ge(v_hi_ready, p + 1)
            dve.tensor_tensor(v_lo[:, :, :], v[:, :, :], f32(v_hi[:, :, :]), ALU.subtract).then_inc(v_lo_ready, 1)

        def dve_decayed(dve, p):
            dve.wait_ge(dec_in, 16 * (p + 1))
            for h in range(2):
                dve.wait_ge(a_ready, 2 * p + h + 1)
                for jt, at in parts:
                    dve.tensor_tensor(m[:, h, jt, at], a_ps[:, h, jt, at], dec[:, h, 0:TOK - jt * P], ALU.mult).then_inc(m_ready, 1)
            for h in range(2):
                dve.wait_ge(m_hi_ready, 4 * p + 2 * h + 2)
                for jt, at in parts:
                    dve.tensor_tensor(m_lo[:, h, jt, at], m[:, h, jt, at], f32(m_hi[:, h, jt, at]), ALU.subtract).then_inc(m_lo_ready, 1)

        def dve_z(dve, p):
            dve.wait_ge(sq_ready, p + 2)
            dve.wait_ge(gate_ready, p + 1)
            dve.wait_ge(z_stored, 16 * (p + 1))
            for h in range(2):
                dve.scalar_tensor_tensor(out=z[:, h, :], in0=gate[:, h, :], scalar=norm[:, bass.ds(2 * p + h, 1)],
                                         in1=o_ps[:, h, :], op0=ALU.mult, op1=ALU.mult).then_inc(z_ready, 1)

        def dve_pair(dve, p, prefetch):
            dve_decayed(dve, p - 1)
            dve_split(dve, 1, p)
            dve_qk(dve, p)
            dve_z(dve, p - 1)
            if prefetch:
                dve_split(dve, 0, p + 1)
            dve_v(dve, p)

        @block.vector
        def _(dve):
            dve.sem_inc(z_ready, 2)
            dve.sem_inc(sq_ready, 1)
            dve.wait_ge(norm_in, 16)
            dve_qk(dve, 0)
            dve_split(dve, 0, 1)
            dve_v(dve, 0)
            with dve.Fori(1, HPAIRS - 1) as p:
                dve_pair(dve, p, True)
            dve_pair(dve, HPAIRS - 1, False)
            dve_decayed(dve, HPAIRS - 1)
            dve_z(dve, HPAIRS - 1)

        def pe_features(pe, out, part, col):
            for k in range(KT):
                c = slice(col * D, (col + 1) * D)
                last = three_pass(pe, out, w_hi[part][:, k, c], w_lo[part][:, k, c], hT_hi[:, k, :], hT_lo[:, k, :],
                                  k == 0, k == KT - 1)
            return last

        def pe_qk(pe, p, wait=True):
            pe.wait_ge(w_lo_ready[0], p + 1)
            for h in range(2):
                if wait:
                    pe.wait_ge(qk_done, 2 * p + h - 1)
                for part in range(2):
                    last = pe_features(pe, qk_ps[:, h, part, :], 0, 2 * h + part)
                last.then_inc(qk_ready, 1)

        def pe_v(pe, p, wait=True):
            pe.wait_ge(w_lo_ready[1], p + 1)
            if wait:
                pe.wait_ge(v_done, p)
            for t in range(QT):
                for k in range(KT):
                    tok = slice(t * P, (t + 1) * P)
                    last = three_pass(pe, v_ps[:, t, :], hT_hi[:, k, tok], hT_lo[:, k, tok], w_hi[1][:, k, 2 * D:4 * D],
                                      w_lo[1][:, k, 2 * D:4 * D], k == 0, k == KT - 1)
            last.then_inc(v_ready, 1)
        def pe_gate(pe, p, wait=True):
            if wait:
                pe.wait_ge(gate_ready, p)
            for h in range(2):
                last = pe_features(pe, g_ps[:, h, :], 1, h)
            last.then_inc(g_ready, 1)

        def pe_scores(pe, p):
            for h in range(2):
                pe.wait_ge(qk_lo_ready, 2 * p + h + 1)
                for jt in range(QT):
                    key = slice(jt * P, (jt + 1) * P)
                    last = three_pass(pe, a_ps[:, h, jt, :], qk_hi[:, h, 1, key], qk_lo[:, h, 1, key],
                                      qk_hi[:, h, 0, :], qk_lo[:, h, 0, :], True, True)
                last.then_inc(a_ready, 1)

        def pe_values(pe, p):
            pe.wait_ge(v_lo_ready, p + 1)
            pe.wait_ge(z_ready, 2 * p + 2)
            pe.wait_ge(sq_ready, p + 1)
            pe.wait_ge(zeroed, 4)
            for h in range(2):
                pe.wait_ge(m_lo_ready, 4 * p + 2 * h + 2)
                for jt in range(QT):
                    f = slice(h * D, (h + 1) * D)
                    last = three_pass(pe, o_ps[:, h, :], v_hi[:, jt, f], v_lo[:, jt, f], m_hi[:, h, jt, :],
                                      m_lo[:, h, jt, :], jt == 0, jt == QT - 1)
            last.then_inc(o_ready, 1)

        @block.tensor
        def _(pe):
            pe_qk(pe, 0, False)
            pe_v(pe, 0, False)
            pe_gate(pe, 0, False)
            with pe.Fori(1, HPAIRS - 1) as p:
                pe_scores(pe, p - 1)
                pe_qk(pe, p)
                pe_values(pe, p - 1)
                pe_v(pe, p)
                pe_gate(pe, p)
            last = HPAIRS - 1
            pe_scores(pe, last - 1)
            pe_qk(pe, last)
            pe_values(pe, last - 1)
            pe_v(pe, last)
            pe_scores(pe, last)
            pe_gate(pe, last)
            pe_values(pe, last)


def lora_mixture(nc, wra_hi, wra_lo, wb_hi, wb_lo, hT_hi, hT_lo, ident, ones, x_sb, out):
    LORA_SCALE = 16.0 / float(np.sqrt(16.0))
    with ExitStack() as ctx:
        a = Alloc(nc, ctx, "mix_")
        lm = a.sb("lm", [P, QT, EXPERTS])
        ahlT = a.sb("ahlT", [ER + EXPERTS, TOK])
        beaten = a.sb("beaten", [P, QT, EXPERTS, EXPERTS])
        rank = a.sb("rank", [P, QT, EXPERTS])
        chosen = a.sb("chosen", [P, QT, EXPERTS])
        neg_max = a.sb("neg_max", [P, QT])
        e = a.sb("e", [P, QT, EXPERTS])
        ec = a.sb("ec", [P, QT, EXPERTS])
        total = a.sb("total", [P, QT])
        inverse = a.sb("inverse", [P, QT])
        gates = a.sb("gates", [P, QT, EXPERTS])
        gr = a.sb("gr", [P, QT, ER])
        gmT = a.sb("gmT", [ER, TOK])
        gmT_hi = a.sb("gmT_hi", [ER, TOK], F32R)
        gmT_lo = a.sb("gmT_lo", [ER, TOK], F32R)
        lm_ps = a.ps("lm_ps", [P, QT, EXPERTS])
        ahlT_ps = a.ps("ahlT_ps", [ER + EXPERTS, BANK])
        grT_ps = a.ps("grT_ps", [ER, BANK])
        y_ps = a.ps("y_ps", [P, QT, 2, BANK])
        lm_ready = a.sem("lm_ready")
        lm_copied = a.sem("lm_copied")
        small = a.sem("small")
        exp_ready = a.sem("exp_ready")
        ah_ready = a.sem("ah_ready")
        ah_copied = a.sem("ah_copied")
        gr_ready = a.sem("gr_ready")
        turned = a.sem("turned")
        gmT_ready = a.sem("gmT_ready")
        y_ready = a.sem("y_ready")
        res_ready = a.sem("res_ready")
        stored = a.sem("stored")
        block = ctx.enter_context(nc.Block())

        @block.sync
        def _(sp):
            for t in range(QT):
                sp.wait_ge(res_ready, 2 * t + 2)
                sp.dma_start(out[t], x_sb[:, t, :]).then_inc(stored, 16)
            sp.wait_ge(stored, 16 * QT)

        @block.tensor
        def _(pe):
            for k in range(KT):
                last = three_pass(pe, ahlT_ps[:, 0:TOK], wra_hi[:, k, :], wra_lo[:, k, :], hT_hi[:, k, :],
                                  hT_lo[:, k, :], k == 0, k == KT - 1)
            last.then_inc(ah_ready, 1)
            pe.wait_ge(ah_copied, 1)
            logits = slice(ER, ER + EXPERTS)
            for t in range(QT):
                last = pe.transpose(lm_ps[:, t, :], ahlT[logits, t * P:(t + 1) * P], ident[logits, logits])
            last.then_inc(lm_ready, 1)
            keep_clock(pe, ahlT_ps[:, :], wra_hi[:, 0, :], hT_hi[:, 0:2, :], 18)
            pe.wait_ge(gr_ready, QT * EXPERTS)
            for t in range(QT):
                last = pe.transpose(grT_ps[:, t * P:(t + 1) * P], gr[:, t, :], ident[:, :])
            last.then_inc(turned, 1)
            pe.wait_ge(gmT_ready, 3)
            for t in range(QT):
                for b in range(2):
                    tok, col = slice(t * P, (t + 1) * P), slice(b * BANK, (b + 1) * BANK)
                    three_pass(pe, y_ps[:, t, b, :], gmT_hi[:, tok], gmT_lo[:, tok], wb_hi[:, col], wb_lo[:, col],
                               True, True).then_inc(y_ready, 1)

        @block.scalar
        def _(act):
            act.wait_ge(ah_ready, 1)
            act.activation(ahlT[:, :], ahlT_ps[:, 0:TOK], ACT.Copy).then_inc(ah_copied, 1)
            act.wait_ge(small, 1)
            for t in range(QT):
                act.activation(e[:, t, :], lm[:, t, 0:EXPERTS], ACT.Exp, bias=neg_max[:, t:t + 1]).then_inc(exp_ready, 1)
        @block.vector
        def _(dve):
            dve.memset(beaten[:, :, :, :], 0.0).then_inc(lm_copied, 1)
            dve.wait_ge(lm_ready, 1)
            dve.tensor_copy(lm[:, :, :], lm_ps[:, :, :]).then_inc(lm_copied, 1)
            dve.wait_ge(lm_copied, 2)
            dve.tensor_reduce(neg_max[:, :], lm[:, :, 0:EXPERTS], AX.X, ALU.max, negate=True).then_inc(small, 1)
            count = 1
            for t in range(QT):
                for j in range(EXPERTS):
                    for rows, op in ((slice(j + 1, EXPERTS), ALU.is_le), (slice(0, j), ALU.is_lt)):
                        if rows.start < rows.stop:
                            dve.tensor_scalar(beaten[:, t, rows, j], lm[:, t, rows], lm[:, t, j:j + 1], None, op).then_inc(small, 1)
                            count += 1
            dve.wait_ge(small, count)
            dve.tensor_reduce(rank[:, :, :], beaten[:, :, :, :], AX.X, ALU.add).then_inc(small, 1)
            dve.wait_ge(small, count + 1)
            dve.tensor_scalar(chosen[:, :, :], rank[:, :, :], 2.0, None, ALU.is_lt).then_inc(small, 1)
            dve.wait_ge(small, count + 2)
            dve.wait_ge(exp_ready, QT)
            dve.tensor_tensor(ec[:, :, :], e[:, :, :], chosen[:, :, :], ALU.mult).then_inc(small, 1)
            dve.wait_ge(small, count + 3)
            dve.tensor_reduce(total[:, :], ec[:, :, :], AX.X, ALU.add).then_inc(small, 1)
            dve.wait_ge(small, count + 4)
            dve.reciprocal(inverse[:, :], total[:, :]).then_inc(small, 1)
            dve.wait_ge(small, count + 5)
            for t in range(QT):
                dve.tensor_scalar(gates[:, t, :], ec[:, t, :], inverse[:, t:t + 1], LORA_SCALE,
                                  ALU.mult, ALU.mult).then_inc(small, 1)
            dve.wait_ge(small, count + 5 + QT)
            for t in range(QT):
                for x in range(EXPERTS):
                    r = slice(x * LORA, (x + 1) * LORA)
                    dve.tensor_scalar(gr[:, t, r], ones[:, 0:LORA], gates[:, t, x:x + 1], None, ALU.mult).then_inc(gr_ready, 1)
            dve.wait_ge(ah_copied, 1)
            dve.wait_ge(turned, 1)
            dve.tensor_tensor(gmT[:, :], grT_ps[:, 0:TOK], ahlT[0:ER, :], ALU.mult).then_inc(gmT_ready, 1)
            dve.wait_ge(gmT_ready, 1)
            dve.tensor_copy(gmT_hi[:, :], gmT[:, :]).then_inc(gmT_ready, 1)
            dve.wait_ge(gmT_ready, 2)
            dve.tensor_tensor(gmT_lo[:, :], gmT[:, :], f32(gmT_hi[:, :]), ALU.subtract).then_inc(gmT_ready, 1)
            for t in range(QT):
                for b in range(2):
                    dve.wait_ge(y_ready, 2 * t + b + 1)
                    x = x_sb[:, t, b * BANK:(b + 1) * BANK]
                    dve.tensor_tensor(x, y_ps[:, t, b, :], x, ALU.add).then_inc(res_ready, 1)


def perceiver_layer(nc, x, ctxT, wk, wv, wq, wo, w_qk, w_gv, decay, norm_w, w_out, w_ra, w_b, out):
    kT_dram = nc.dram_tensor("kT_scratch", (KVH, D, KV), F32, kind="Internal").ap()
    v_dram = nc.dram_tensor("v_scratch", (KVH, P, KVT, D), F32, kind="Internal").ap()
    oT_dram = nc.dram_tensor("oT_scratch", (HEADS, D, TOK), F32, kind="Internal").ap()
    zT_dram = nc.dram_tensor("zT_scratch", (HEADS, D, TOK), F32, kind="Internal").ap()
    with ExitStack() as ctx:
        a = Alloc(nc, ctx, "")
        ident = a.sb("ident", [P, P])
        ones = a.sb("ones", [P, P])
        x_sb = a.sb("x_sb", [P, QT, HIDDEN])
        shared = Shared(a)
        s_raw = carve(shared.stage, 0, 2, HP, TOK)
        zero_done = a.sem("zero_done")
        with nc.Block() as block:
            @block.gpsimd
            def _(pool):
                pool.memset(ones[:, :], 1.0)
                pool.memset(ident[:, :], 0.0).then_inc(zero_done, 1)
                pool.wait_ge(zero_done, 1)
                pool.affine_select(out=ident[:, :], in_=ident[:, :], compare_op=ALU.not_equal, fill=1.0, base=0,
                                   pattern=[[-1, P]], channel_multiplier=1)
        r0, r1 = shared.r
        wo_proj = Projection(Alloc(nc, ctx, "wo_p_"), oT_dram, wo, carve(shared.f, 0, 2, HP, HIDDEN), s_raw,
                             (carve(r1, 0, HP, HIDDEN), carve(r1, HP * HIDDEN, HP, HIDDEN),
                              carve(r0, 0, HP, TOK), carve(r0, HP * TOK, HP, TOK)))
        with ExitStack() as inner:
            b = Alloc(nc, inner, "x_")
            hT_hi = b.sb("hT_hi", [P, KT, TOK], F32R)
            hT_lo = b.sb("hT_lo", [P, KT, TOK], F32R)
            project_keys_values(nc, x, ctxT, wk, wv, wq, x_sb, hT_hi, hT_lo, ident, kT_dram, v_dram, shared)
            cross_attention(nc, wq, kT_dram, v_dram, hT_hi, hT_lo, ident, oT_dram, shared, wo_proj)
        square_sum = a.sb("square_sum", [P, 2, TOK])
        weights = PairWeights(Alloc(nc, ctx, "pair_"), w_qk, w_gv)
        hT_hi = a.sb("hT_hi", [P, KT, TOK], F32R)
        hT_lo = a.sb("hT_lo", [P, KT, TOK], F32R)

        def load_first_pair(sp, i):
            weights.load_half(sp, i // 2, i % 2)

        with ExitStack() as inner:
            b = Alloc(nc, inner, "wo_")
            wo_proj.set_odd([b.sb(f"odd{i}", [P, HP, n], F32R)[:, :, :] for i, n in enumerate((HIDDEN, HIDDEN, TOK, TOK))])
            project_out(nc, "wo_", wo_proj, x_sb, carve(shared.f, 0, QT, HIDDEN), hT_hi, hT_lo, ident,
                        (HEADS // 2, HEADS // 2), load_first_pair, 4, meanwhile=weights.first_pair)
        raw, hi = [tile[0][:, :, :].rearrange("p k n -> p (k n)") for tile in (weights.raw, weights.hi)]
        out_proj = Projection(Alloc(nc, ctx, "lo_p_"), zT_dram, w_out, carve(raw, 0, 2, HP, HIDDEN), s_raw,
                              (carve(hi, 0, HP, HIDDEN), carve(hi, HP * HIDDEN, HP, HIDDEN),
                               carve(r1, 8 * D, HP, TOK), carve(r1, 8 * D + HP * TOK, HP, TOK)))
        linear_attention(nc, weights, decay, norm_w, hT_hi, hT_lo, zT_dram, square_sum, out_proj, shared)
        out_proj.set_odd((carve(r0, 0, HP, HIDDEN), carve(r0, HP * HIDDEN, HP, HIDDEN),
                          carve(r1, 8 * D + 2 * HP * TOK, HP, TOK), carve(r1, 8 * D + 3 * HP * TOK, HP, TOK)))
        wra = a.sb("wra", [P, KT, ER + EXPERTS])
        wra_hi = a.sb("wra_hi", [P, KT, ER + EXPERTS], F32R)
        wra_lo = a.sb("wra_lo", [P, KT, ER + EXPERTS], F32R)
        wb = a.sb("wb", [ER, HIDDEN])
        wb_hi = a.sb("wb_hi", [ER, HIDDEN], F32R)
        wb_lo = a.sb("wb_lo", [ER, HIDDEN], F32R)
        mix_in = a.sem("mix_in")
        mix_hi_ready = a.sem("mix_hi_ready")

        def load_mixture(sp, i):
            sp.dma_start(wra[:, :, :], w_ra).then_inc(mix_in, 16)
            sp.dma_start(wb[:, :], w_b).then_inc(mix_in, 16)

        def split_mixture(pool):
            pool.wait_ge(mix_in, 32)
            pool.tensor_copy(wra_hi[:, :, :], wra[:, :, :]).then_inc(mix_hi_ready, 1)
            pool.tensor_copy(wb_hi[:, :], wb[:, :]).then_inc(mix_hi_ready, 1)
            pool.wait_ge(mix_hi_ready, 2)
            pool.tensor_tensor(wb_lo[:, :], wb[:, :], f32(wb_hi[:, :]), ALU.subtract)
            pool.tensor_tensor(wra_lo[:, :, :], wra[:, :, :], f32(wra_hi[:, :, :]), ALU.subtract)

        project_out(nc, "lo_", out_proj, x_sb, carve(shared.f, 0, QT, HIDDEN), hT_hi, hT_lo, ident,
                    (HPAIRS, 0), load_mixture, 1, norm=(square_sum, ones), meanwhile=split_mixture)
        lora_mixture(nc, wra_hi, wra_lo, wb_hi, wb_lo, hT_hi, hT_lo, ident, ones, x_sb, out)


def decay_table():
    layer, layers = 1, 32
    factor = 1.0 - layer / (layers - 1 + 1e-05) + 1e-05
    slope = (2.0 ** (-8.0 / HEADS)) ** (np.arange(HEADS) + 1.0) * factor
    dist = np.arange(TOK)[None, :] - np.arange(P)[:, None]
    table = np.where(dist >= 0, np.exp(-slope[:, None, None] * np.maximum(dist, 0)), 0.0)
    return np.ascontiguousarray(table.reshape(HPAIRS, 2, P, TOK).transpose(0, 2, 1, 3)).astype(np.float32)


def kernel(x, ctx_4096, L0_xattn_Wq, L0_xattn_Wk, L0_xattn_Wv, L0_xattn_Wo, L0_attn_qkv_w, L0_attn_out_w,
           L0_attn_gate_w, L0_attn_norm_w, L0_ffn_A, L0_ffn_B, L0_ffn_Wr):
    import concourse.bacc as bacc
    from concourse.bass_utils import run_bass_kernel_spmd

    def turned(w):
        return np.asarray(w).T.reshape(KT, P, -1).transpose(1, 0, 2)

    qkv = turned(L0_attn_qkv_w).reshape(P, KT, HPAIRS, 2, 3, D)
    gate = turned(L0_attn_gate_w).reshape(P, KT, HPAIRS, 2, D)
    w_gv = np.stack([gate, qkv[:, :, :, :, 2]], axis=3)
    data = {
        "x": np.asarray(x).reshape(QT, P, HIDDEN).transpose(1, 0, 2),
        "ctxT": np.asarray(ctx_4096).reshape(NCHUNK, CCHUNK, KT, P).transpose(0, 3, 2, 1),
        "wk": np.asarray(L0_xattn_Wk).reshape(KT, P, KVH * D).transpose(1, 0, 2),
        "wv": np.asarray(L0_xattn_Wv).reshape(KT, P, KVH * D).transpose(1, 0, 2),
        "wq": np.asarray(L0_xattn_Wq).reshape(KT, P, HEADS, D).transpose(2, 1, 0, 3),
        "wo": np.asarray(L0_xattn_Wo).reshape(HEADS, D, HIDDEN),
        "w_qk": qkv[:, :, :, :, 0:2].transpose(2, 0, 1, 3, 4, 5).reshape(HPAIRS, P, KT, 4 * D),
        "w_gv": w_gv.transpose(2, 0, 1, 3, 4, 5).reshape(HPAIRS, P, KT, 4 * D),
        "decay": decay_table(),
        "norm_w": np.asarray(L0_attn_norm_w).reshape(HEADS, D).T,
        "w_out": np.asarray(L0_attn_out_w).T.reshape(HEADS, D, HIDDEN),
        "w_ra": np.concatenate([turned(np.asarray(L0_ffn_A).reshape(ER, HIDDEN)), turned(L0_ffn_Wr)], axis=2),
        "w_b": np.asarray(L0_ffn_B).transpose(0, 2, 1).reshape(ER, HIDDEN),
    }
    nc = bacc.Bacc("TRN2", target_bir_lowering=False, num_devices=1)
    arrays, args = {}, []
    for name, value in data.items():
        value = np.ascontiguousarray(value)
        arrays[f"in_{name}"] = value
        args.append(nc.dram_tensor(f"in_{name}", value.shape, mybir.dt.from_np(value.dtype), kind="ExternalInput").ap())
    out = nc.dram_tensor("out", (QT, P, HIDDEN), F32, kind="ExternalOutput").ap()
    perceiver_layer(nc, *args, out)
    result = run_bass_kernel_spmd(nc, [arrays], core_ids=[0])
    return result.results[0]["out"].reshape(1, TOK, HIDDEN)
```
